# Optimizing a Trainium2 kernel written in Bass

```python
import numpy as np
import jax
import jax.numpy as jnp

def _softmax(x, axis=-1):
    return jax.nn.softmax(x, axis=axis)

def _gelu(x):
    return jax.nn.gelu(x, approximate=True)

def _silu(x):
    return jax.nn.silu(x)

def _sigmoid(x):
    return jax.nn.sigmoid(x)

def _layernorm(x, axis=-1, eps=1e-05):
    m = jnp.mean(x, axis=axis, keepdims=True)
    v = jnp.var(x, axis=axis, keepdims=True)
    return (x - m) / jnp.sqrt(v + eps)

def _scatter_add(tgt, idx, src, axis=0):
    return tgt.at[idx].add(src)

def _segment_sum(src, seg, n):
    return jax.ops.segment_sum(src, seg, n)
kernel_name = 'mk_gps_d1_gnn_r8_ceea18'

def setup_inputs(seed: int=0):
    np.random.seed(seed)
    _w = jnp.asarray

    def _rec_inputs():
        import jax
        import jax.numpy as jnp
        _gk = jax.random.key(seed)
        x = -0.0002117 + 1 * jax.random.normal(jax.random.fold_in(_gk, 1), (1250, 512), jnp.float32)
        src = jax.random.randint(jax.random.fold_in(_gk, 2), (40000,), 0, 1250, jnp.int32)
        dst = jax.random.randint(jax.random.fold_in(_gk, 3), (40000,), 0, 1250, jnp.int32)
        _o = jnp.argsort(dst, stable=True)
        src = src[_o]
        dst = dst[_o]
        return (x, src, dst)
    x, src, dst = _rec_inputs()

    def _L0_gnn_setup():
        import jax, jax.numpy as jnp
        import numpy as np
        from math import sqrt
        N_NODES = 6250
        N_EDGES = 50000
        D_EMB = 512
        HEADS = 8
        DK = 32
        DV = 32
        key = jax.random.key(seed)
        ks = jax.random.split(key, 8)
        x = jax.random.normal(ks[0], (N_NODES, D_EMB), dtype=jnp.float32)
        edge_index = jax.random.randint(ks[1], (2, N_EDGES), 0, N_NODES, dtype=jnp.int64)

        def lin(k, fan_in, fan_out):
            bound = 1.0 / sqrt(fan_in)
            kw, kb = jax.random.split(k)
            W = jax.random.uniform(kw, (fan_in, fan_out), minval=-bound, maxval=bound, dtype=jnp.float32)
            b = jax.random.uniform(kb, (fan_out,), minval=-bound, maxval=bound, dtype=jnp.float32)
            return (W, b)
        Wk, bk = lin(ks[2], D_EMB, HEADS * DK)
        Wq, bq = lin(ks[3], D_EMB, HEADS * DK)
        Wv, bv = lin(ks[4], D_EMB, HEADS * DV)
        Wa, ba = lin(ks[5], HEADS * DV, D_EMB)
        Wf, bf = lin(ks[6], D_EMB, D_EMB)
        return {'x': x, 'edge_index': edge_index, 'Wk': Wk, 'bk': bk, 'Wq': Wq, 'bq': bq, 'Wv': Wv, 'bv': bv, 'Wa': Wa, 'ba': ba, 'Wf': Wf, 'bf': bf}
    _L0_gnn_all = _L0_gnn_setup()
    _L0_gnn_in = {k: v for k, v in _L0_gnn_all.items() if k in ('Wk', 'bk', 'Wq', 'bq', 'Wv', 'bv', 'Wa', 'ba', 'Wf', 'bf')}
    del _L0_gnn_all

    def _L0_mix_setup():
        import jax, jax.numpy as jnp
        import numpy as np
        D_MODEL = 512
        NUM_HEADS = 8
        HEAD_DIM = D_MODEL // NUM_HEADS
        EPS = 1e-06

        def _feature_map(t):
            return jax.nn.elu(t) + 1.0
        key = jax.random.key(seed)
        ks = jax.random.split(key, 9)
        s = 1.0 / np.sqrt(D_MODEL)
        x = jax.random.normal(ks[0], (4, 1024, D_MODEL), dtype=jnp.float32)
        Wq = jax.random.uniform(ks[1], (D_MODEL, D_MODEL), jnp.float32, -s, s)
        bq = jax.random.uniform(ks[2], (D_MODEL,), jnp.float32, -s, s)
        Wk = jax.random.uniform(ks[3], (D_MODEL, D_MODEL), jnp.float32, -s, s)
        bk = jax.random.uniform(ks[4], (D_MODEL,), jnp.float32, -s, s)
        Wv = jax.random.uniform(ks[5], (D_MODEL, D_MODEL), jnp.float32, -s, s)
        bv = jax.random.uniform(ks[6], (D_MODEL,), jnp.float32, -s, s)
        Wo = jax.random.uniform(ks[7], (D_MODEL, D_MODEL), jnp.float32, -s, s)
        bo = jax.random.uniform(ks[8], (D_MODEL,), jnp.float32, -s, s)
        return {'x': x, 'Wq': Wq, 'bq': bq, 'Wk': Wk, 'bk': bk, 'Wv': Wv, 'bv': bv, 'Wo': Wo, 'bo': bo}
    _L0_mix_all = _L0_mix_setup()
    _L0_mix_in = {k: v for k, v in _L0_mix_all.items() if k in ('Wq', 'bq', 'Wk', 'bk', 'Wv', 'bv', 'Wo', 'bo')}
    del _L0_mix_all

    def _L0_ffn_setup():
        import jax, jax.numpy as jnp
        import numpy as np
        D, E, DR, K, DFF, DSH = (512, 64, 64, 2, 256, 1024)
        TEMP = 0.7
        SHARED_SCALE = 0.25
        EPS = 1e-05

        def _ln(x, g, b):
            m = jnp.mean(x, axis=-1, keepdims=True)
            v = jnp.mean(jnp.square(x - m), axis=-1, keepdims=True)
            return (x - m) * jax.lax.rsqrt(v + EPS) * g + b
        key = jax.random.key(seed)
        ks = jax.random.split(key, 16)
        s = 0.02
        return {'x': jax.random.normal(ks[0], (1, 512, D), dtype=jnp.float32), 'ln1_g': jnp.ones((D,), jnp.float32), 'ln1_b': jnp.zeros((D,), jnp.float32), 'Wr': jax.random.normal(ks[1], (D, DR), jnp.float32) * s, 'codebook': jax.random.normal(ks[2], (E, DR), jnp.float32), 'W1': jax.random.normal(ks[3], (E, D, DFF), jnp.float32) * s, 'b1': jnp.zeros((E, DFF), jnp.float32), 'W2': jax.random.normal(ks[4], (E, DFF, D), jnp.float32) * s, 'b2': jnp.zeros((E, D), jnp.float32), 'Ws1': jax.random.normal(ks[5], (D, DSH), jnp.float32) * s, 'bs1': jnp.zeros((DSH,), jnp.float32), 'Ws2': jax.random.normal(ks[6], (DSH, D), jnp.float32) * s, 'bs2': jnp.zeros((D,), jnp.float32), 'ffln_g': jnp.ones((D,), jnp.float32), 'ffln_b': jnp.zeros((D,), jnp.float32), 'Wf1': jax.random.normal(ks[7], (D, DFF), jnp.float32) * s, 'bf1': jnp.zeros((DFF,), jnp.float32), 'Wf2': jax.random.normal(ks[8], (DFF, D), jnp.float32) * s, 'bf2': jnp.zeros((D,), jnp.float32)}
    _L0_ffn_all = _L0_ffn_setup()
    _L0_ffn_in = {k: v for k, v in _L0_ffn_all.items() if k in ('ln1_g', 'ln1_b', 'Wr', 'codebook', 'W1', 'b1', 'W2', 'b2', 'Ws1', 'bs1', 'Ws2', 'bs2', 'ffln_g', 'ffln_b', 'Wf1', 'bf1', 'Wf2', 'bf2')}
    del _L0_ffn_all
    return {'x': x, 'src': src, 'dst': dst, 'L0_gnn_Wk': _L0_gnn_in['Wk'], 'L0_gnn_bk': _L0_gnn_in['bk'], 'L0_gnn_Wq': _L0_gnn_in['Wq'], 'L0_gnn_bq': _L0_gnn_in['bq'], 'L0_gnn_Wv': _L0_gnn_in['Wv'], 'L0_gnn_bv': _L0_gnn_in['bv'], 'L0_gnn_Wa': _L0_gnn_in['Wa'], 'L0_gnn_ba': _L0_gnn_in['ba'], 'L0_gnn_Wf': _L0_gnn_in['Wf'], 'L0_gnn_bf': _L0_gnn_in['bf'], 'L0_mix_Wq': _L0_mix_in['Wq'], 'L0_mix_bq': _L0_mix_in['bq'], 'L0_mix_Wk': _L0_mix_in['Wk'], 'L0_mix_bk': _L0_mix_in['bk'], 'L0_mix_Wv': _L0_mix_in['Wv'], 'L0_mix_bv': _L0_mix_in['bv'], 'L0_mix_Wo': _L0_mix_in['Wo'], 'L0_mix_bo': _L0_mix_in['bo'], 'L0_ffn_ln1_g': _L0_ffn_in['ln1_g'], 'L0_ffn_ln1_b': _L0_ffn_in['ln1_b'], 'L0_ffn_Wr': _L0_ffn_in['Wr'], 'L0_ffn_codebook': _L0_ffn_in['codebook'], 'L0_ffn_W1': _L0_ffn_in['W1'], 'L0_ffn_b1': _L0_ffn_in['b1'], 'L0_ffn_W2': _L0_ffn_in['W2'], 'L0_ffn_b2': _L0_ffn_in['b2'], 'L0_ffn_Ws1': _L0_ffn_in['Ws1'], 'L0_ffn_bs1': _L0_ffn_in['bs1'], 'L0_ffn_Ws2': _L0_ffn_in['Ws2'], 'L0_ffn_bs2': _L0_ffn_in['bs2'], 'L0_ffn_ffln_g': _L0_ffn_in['ffln_g'], 'L0_ffn_ffln_b': _L0_ffn_in['ffln_b'], 'L0_ffn_Wf1': _L0_ffn_in['Wf1'], 'L0_ffn_bf1': _L0_ffn_in['bf1'], 'L0_ffn_Wf2': _L0_ffn_in['Wf2'], 'L0_ffn_bf2': _L0_ffn_in['bf2']}

def reference(x, src, dst, L0_gnn_Wk, L0_gnn_bk, L0_gnn_Wq, L0_gnn_bq, L0_gnn_Wv, L0_gnn_bv, L0_gnn_Wa, L0_gnn_ba, L0_gnn_Wf, L0_gnn_bf, L0_mix_Wq, L0_mix_bq, L0_mix_Wk, L0_mix_bk, L0_mix_Wv, L0_mix_bv, L0_mix_Wo, L0_mix_bo, L0_ffn_ln1_g, L0_ffn_ln1_b, L0_ffn_Wr, L0_ffn_codebook, L0_ffn_W1, L0_ffn_b1, L0_ffn_W2, L0_ffn_b2, L0_ffn_Ws1, L0_ffn_bs1, L0_ffn_Ws2, L0_ffn_bs2, L0_ffn_ffln_g, L0_ffn_ffln_b, L0_ffn_Wf1, L0_ffn_bf1, L0_ffn_Wf2, L0_ffn_bf2):
    import jax
    import jax.numpy as jnp

    def _L0_gnn_ref(x, edge_index, Wk, bk, Wq, bq, Wv, bv, Wa, ba, Wf, bf):
        import jax, jax.numpy as jnp
        import numpy as np
        from math import sqrt
        N_NODES = 6250
        N_EDGES = 50000
        D_EMB = 512
        HEADS = 8
        DK = 32
        DV = 32
        N = x.shape[0]
        receivers, senders = (edge_index[0], edge_index[1])
        K = (x @ Wk + bk).reshape(N, HEADS, DK)
        Q = (x @ Wq + bq).reshape(N, HEADS, DK)
        V = (x @ Wv + bv).reshape(N, HEADS, DV)
        att = jnp.exp(jnp.einsum('ehd,ehd->eh', Q[receivers], K[senders]) / sqrt(DK))
        denom = jax.ops.segment_sum(att, receivers, num_segments=N)
        att = att / denom[receivers]
        msg = att[:, :, None] * V[senders]
        agg = jnp.zeros((N, HEADS, DV), dtype=V.dtype).at[receivers].add(msg)
        out = jax.nn.relu(agg).reshape(N, HEADS * DV)
        out = jax.nn.relu(out @ Wa + ba)
        out = jax.nn.relu(out @ Wf + bf)
        return x + out

    def _L0_mix_ref(x, Wq, bq, Wk, bk, Wv, bv, Wo, bo):
        import jax, jax.numpy as jnp
        import numpy as np
        D_MODEL = 512
        NUM_HEADS = 8
        HEAD_DIM = D_MODEL // NUM_HEADS
        EPS = 1e-06

        def _feature_map(t):
            return jax.nn.elu(t) + 1.0
        B, N, C = x.shape
        H, D = (NUM_HEADS, HEAD_DIM)
        q = (x @ Wq.T + bq).reshape(B, N, H, D).transpose(0, 2, 1, 3)
        k = (x @ Wk.T + bk).reshape(B, N, H, D).transpose(0, 2, 1, 3)
        v = (x @ Wv.T + bv).reshape(B, N, H, D).transpose(0, 2, 1, 3)
        q = _feature_map(q)
        k = _feature_map(k)
        kv = jnp.einsum('bhnd,bhne->bhde', k, v)
        k_sum = k.sum(axis=2)
        z = jnp.einsum('bhnd,bhd->bhn', q, k_sum)[..., None] + EPS
        out = jnp.einsum('bhnd,bhde->bhne', q, kv) / z
        out = out.transpose(0, 2, 1, 3).reshape(B, N, C)
        return out @ Wo.T + bo

    def _L0_ffn_ref(x, ln1_g, ln1_b, Wr, codebook, W1, b1, W2, b2, Ws1, bs1, Ws2, bs2, ffln_g, ffln_b, Wf1, bf1, Wf2, bf2):
        import jax, jax.numpy as jnp
        import numpy as np
        D, E, DR, K, DFF, DSH = (512, 64, 64, 2, 256, 1024)
        TEMP = 0.7
        SHARED_SCALE = 0.25
        EPS = 1e-05

        def _ln(x, g, b):
            m = jnp.mean(x, axis=-1, keepdims=True)
            v = jnp.mean(jnp.square(x - m), axis=-1, keepdims=True)
            return (x - m) * jax.lax.rsqrt(v + EPS) * g + b
        B, S, _ = x.shape
        T = B * S
        h = _ln(x, ln1_g, ln1_b).reshape(T, D)
        r = h @ Wr
        logits = r @ codebook.T / TEMP
        probs = jax.nn.softmax(logits, axis=-1)
        vals, idx = jax.lax.top_k(probs, K)
        w = vals / jnp.sum(vals, axis=-1, keepdims=True)
        combine = jnp.zeros((T, E), x.dtype).at[jnp.arange(T)[:, None], idx].set(w)
        eh = jax.nn.silu(jnp.einsum('td,edf->tef', h, W1) + b1)
        eo = jnp.einsum('tef,efd->ted', eh, W2) + b2
        moe = jnp.einsum('te,ted->td', combine, eo)
        shared = (jax.nn.silu(h @ Ws1 + bs1) @ Ws2 + bs2) * SHARED_SCALE
        hmoe = (moe + shared).reshape(B, S, D)
        f = _ln(hmoe, ffln_g, ffln_b)
        f = jax.nn.silu(f @ Wf1 + bf1) @ Wf2 + bf2
        return x + hmoe + f
    edge_index = jnp.stack([src, dst])
    xn = _layernorm(x, axis=-1)
    x = x + _L0_gnn_ref(xn, edge_index, L0_gnn_Wk, L0_gnn_bk, L0_gnn_Wq, L0_gnn_bq, L0_gnn_Wv, L0_gnn_bv, L0_gnn_Wa, L0_gnn_ba, L0_gnn_Wf, L0_gnn_bf) + _L0_mix_ref(xn[None], L0_mix_Wq, L0_mix_bq, L0_mix_Wk, L0_mix_bk, L0_mix_Wv, L0_mix_bv, L0_mix_Wo, L0_mix_bo)[0]
    x = x + _L0_ffn_ref(_layernorm(x, axis=-1)[None], L0_ffn_ln1_g, L0_ffn_ln1_b, L0_ffn_Wr, L0_ffn_codebook, L0_ffn_W1, L0_ffn_b1, L0_ffn_W2, L0_ffn_b2, L0_ffn_Ws1, L0_ffn_bs1, L0_ffn_Ws2, L0_ffn_bs2, L0_ffn_ffln_g, L0_ffn_ffln_b, L0_ffn_Wf1, L0_ffn_bf1, L0_ffn_Wf2, L0_ffn_bf2)[0]
    return x

_drawn_inputs = setup_inputs


def setup_inputs(seed=0):
    import zlib

    import numpy as np

    out = dict(_drawn_inputs(seed))
    spreads = {'L0_ffn_ln1_g': (1.0, 0.2),
     'L0_ffn_ln1_b': (0.0, 0.1),
     'L0_ffn_b1': (0.0, 0.1),
     'L0_ffn_b2': (0.0, 0.1),
     'L0_ffn_bs1': (0.0, 0.1),
     'L0_ffn_bs2': (0.0, 0.1),
     'L0_ffn_ffln_g': (1.0, 0.2),
     'L0_ffn_ffln_b': (0.0, 0.1),
     'L0_ffn_bf1': (0.0, 0.1),
     'L0_ffn_bf2': (0.0, 0.1)}
    factors = {}
    for name, (base, spread) in spreads.items():
        noise = np.random.default_rng([zlib.crc32(name.encode()), seed]).standard_normal(out[name].shape)
        drawn = base * np.exp(spread * noise) if base else spread * noise
        out[name] = jnp.asarray(drawn.astype(out[name].dtype))
    for name, factor in factors.items():
        out[name] = (out[name] * factor).astype(out[name].dtype)
    return out
```

```python
from contextlib import ExitStack

import numpy as np
import concourse.bass as bass
from concourse import mybir

F32 = mybir.dt.float32
F32R = mybir.dt.float32r
BF16 = mybir.dt.bfloat16
F16 = mybir.dt.float16
I32 = mybir.dt.int32
U32 = mybir.dt.uint32
ALU = mybir.AluOpType
ACT = mybir.ActivationFunctionType
AX = mybir.AxisListType

N, D, P = 1250, 512, 125
T = N // P
KD = D // 128
EDGES = 40000
EC = EDGES // P
EG = 4
HEADS, DK = 8, 32
E, TOPK, DFF, DSH = 64, 2, 256, 1024
B = 128
RANKS = -(-N // B) * B
U = 4
GROUPS = E // U
NOBODY = 1 << 20
RING = 6
CHUNKS = [(0, 500), (500, 500), (1000, 250)]
BANKED = [(0, 512), (512, 512), (1024, 226)]
TINY = 1.2e-38

COLS = {}
for _name, _n in (("mbq", 4), ("gbq", 2), ("gbk", 2), ("ba", 4), ("bs1", 8), ("bf1", 2), ("g1", 4),
                  ("b1ln", 4), ("gf", 4), ("bfln", 4), ("eb1", 2 * E)):
    COLS[_name] = (sum(n for _, n in COLS.values()), _n)
NCOLS = sum(n for _, n in COLS.values())
ROWS = {"mbk": 0, "mbv": 1, "mbo": 2, "gbf": 3, "bs2": 4, "bf2": 5, "gbv": 6}


class Turns:

    def __init__(self, plan):
        self.first, self.who = {}, []
        for name, consumers in plan:
            self.first[name] = len(self.who)
            self.who += consumers

    def bank(self, name, i):
        return (self.first[name] + i) % RING

    def filled(self, name, i):
        return self.first[name] + i + 1

    def read(self, g):
        return self.who[g], self.who[:g + 1].count(self.who[g])

    def group_read(self, name, i):
        return self.read(self.first[name] + i)


TURNS = Turns([
    ("xnT", ["act", "dve"] * 5),
    ("mix_q", ["act"] * 12),
    ("mix_kv", ["dve"] * 20),
    ("mix_o", ["dve"] * 24),
    ("mix_wo", ["dve"] * 10),
    ("gnn_qk", ["act"] * 12),
    ("gnn_v", ["dve"] * 10),
    ("aggT", ["act"] * 10),
    ("gnn_a", ["act"] * 12),
    ("gnn_f", ["dve"] * 10),
    ("hT", ["act"] * 10),
    ("rT", ["act"] * 3),
    ("logit", ["dve"] * 2),
    ("rank", ["dve"] * 3),
    ("combT", ["act"] * 3),
    ("shared", (["act"] * 4) + (["act"] * 4 + ["dve"] * 2) * 4 + ["dve"] * 2),
    ("fT", ["act"] * 10),
    ("f1", ["act"] * 6),
    ("f2", ["dve"] * 10),
])


def at_least(eng, sem, value):
    if not isinstance(value, int) or value > 0:
        eng.wait_ge(sem, value)


def block_kernel(nc, A, out):
    ctx = ExitStack()
    with ctx:
        KB = 1024
        base = nc.sbuf_base + (-nc.sbuf_base) % 64

        def at(name, shape, dt, offset):
            return nc.alloc_sbuf_tensor_at(name, shape, dt, offset=base + int(offset))

        def sem(name):
            return ctx.enter_context(nc.semaphore(name))

        fixed = [0]

        def keep(name, shape, dt):
            size = int(np.prod(shape[1:])) * mybir.dt.size(dt)
            off = fixed[0]
            fixed[0] += size + (-size) % 64
            return at(name, shape, dt, off)

        ident = keep("ident", [128, 128], F32)
        cols = keep("cols", [128, NCOLS], F32)
        rows = keep("rows", [128, len(ROWS), D], F32)
        XR = keep("XR", [P, T, D], F32)
        st = keep("st", [P, T, 6], F32)
        mv = keep("mv", [P, T, 2], F32)
        mv2 = keep("mv2", [P, T, 2], F32)
        rs = keep("rs", [P, T], F32)
        eps = keep("eps", [P, 1], F32)
        Wr_s = keep("Wr_s", [128, KD, E], F32)
        cbT_s = keep("cbT_s", [E, E], F32)
        b2_s = keep("b2_s", [E, D], F32)
        den = keep("den", [P, T, 1], F32)
        wtop = keep("wtop", [P, T, TOPK], F32)
        idxg = keep("idxg", [128, U, 1], U32)
        idxs = keep("idxs", [128, U, 1], U32)
        lst = keep("lst", [128, E + U], U32)
        gat = keep("gat", [128, E + U], U32)
        carry = keep("carry", [1, 2, 1], F32)
        rounds = keep("rounds", [1, 1], I32)
        ranges = keep("ranges", [T, 2], I32)
        zeros = keep("zeros", [1, 640], BF16)
        fixed[0] += (-fixed[0]) % 64
        W1 = [keep(f"W1_{u}", [128, KD, DFF], F32) for u in range(U)]
        W2 = [keep(f"W2_{u}", [128, 2, D], F32) for u in range(U)]
        G = fixed[0]

        def ph(name, shape, dt, kb):
            return at(name, shape, dt, G + kb * KB)

        xs = ph("xs", [P, T, D], F32, 0)
        xn = ph("xn", [P, T, D], F32, 20)
        xnT = ph("xnT", [128, KD, N], F32, 40)
        mW = ph("mW", [128, 3, KD, D], F32, 60)
        mWo = ph("mWo", [128, KD, D], F32, 84)
        gW = ph("gW", [128, 3, KD, HEADS * DK], F32, 92)
        qT = ph("qT", [128, KD, N], F32, 104)
        eq = ph("eq", [128, 2, 500], F32, 124)
        rq = ph("rq", [128, 2, 500], F32, 128)
        tk = ph("tk", [P, 2, D], F32, 124)
        ek = ph("ek", [P, 2, D], F32, 128)
        kf = ph("kf", [P, 2, D], F32, 34)
        vt = ph("vt", [P, 2, KD, 129], F32, 20)
        kvb = ph("kvb", [128, KD, 128], F32, 26)
        ksb = ph("ksb", [128, KD, 128], F32, 28)
        zt = ph("zt", [128, 2, 500], F32, 30)
        moT = ph("moT", [128, KD, N], F32, 0)
        fqk = ph("fqk", [128, 2, N], F32, 60)
        qk_hi = ph("qk_hi", [128, 2, N], F32R, 20)
        qk_lo = ph("qk_lo", [128, 2, N], F32R, 30)
        V = ph("V", [P, T, HEADS, DK + 1], F32, 120.5)

        C = ph("C", [P, T, N], F32, 40)
        Wa_s = ph("Wa_s", [128, 2, D], F32, 90)
        Wf_s = ph("Wf_s", [128, KD, D], F32, 94)
        ohB = ph("ohB", [P, EG, N], BF16, 102)
        ohA = ph("ohA", [P, EG, P], BF16, 112)
        iota = ph("iota", [P, N], F16, 113)
        e_i = ph("e_i", [P, 2, EC], I32, 115.5)
        e_f = ph("e_f", [P, 2, EC], F32, 118)
        neg = ph("neg", [P, EC], F32, 86.5)
        cmx = ph("cmx", [P, 2, EC], F32, 84)
        ov = ph("ov", [T, 3, EC], F32, 102)
        gi = ph("gi", [T, 2, EC], F32, 106)
        lim = ph("lim", [T, 8], F32, 131)
        att = ph("att", [P, 3, N], F32, 102)
        Kst = ph("Kst", [128, 2, N], F32R, 0)
        Qst = ph("Qst", [128, 2, N], F32R, 10)
        agg = ph("agg", [P, T, HEADS * DK], F32, 20)
        aggT = ph("aggT", [128, 2, N], F32, 0)
        h1T = ph("h1T", [128, KD, N], F32, 40)
        tf = ph("tf", [P, 2, D], F32, 30)

        yz = ph("yz", [P, T, D], F32, 102)
        HM = ph("HM", [P, T, D], F32, 20)
        hT = ph("hT", [128, KD, N], F32, 60)
        Ws1_s = ph("Ws1_s", [128, KD, DSH], F32, 80)
        Ws2_s = ph("Ws2_s", [128, DSH // 128, D], F32, 0)
        hsT = ph("hsT", [128, 2, DSH // 128, 250], F32, 96)
        Wf1_s = ph("Wf1_s", [128, KD, DFF], F32, 16)
        Wf2_s = ph("Wf2_s", [128, 2, D], F32, 112)
        rTs = ph("rTs", [E, N], F32, 96)
        prob = ph("prob", [P, T, E], F32, 40)
        M1 = ph("M1", [P, T, E], F32, 42.5)
        M2 = ph("M2", [P, T, E], F32, 45)
        Mb = ph("Mb", [P, T, E], BF16, 47.5)
        tmpr = ph("tmpr", [P, T, E], F32, 49)
        rankS = ph("rankS", [P, T, E], F32, 51.5)
        combT = ph("combT", [E, N], F32, 54)
        iotaE = ph("iotaE", [P, E], F32, 130)
        iotaE_i = ph("iotaE_i", [P, E], I32, 130.5)
        sm = ph("sm", [P, 16, T], F32, 124)
        top8 = ph("top8", [P, T, 8], F32, 124.75)
        idx8 = ph("idx8", [P, T, 8], U32, 125.25)
        posf = ph("posf", [P, TOPK, T], F32, 125.75)
        posi = ph("posi", [P, TOPK, T], U32, 126)
        toki = ph("toki", [P, TOPK, T], U32, 126.25)
        ltri = ph("ltri", [P, P], BF16, 126.5)
        ones = ph("ones", [P, P], BF16, 126.75)
        nobody = ph("nobody", [128, RANKS * E // 128], U32, 127)
        Zg = ph("Zg", [128, U, D], F32, 116)
        hgT = ph("hgT", [128, 2, KD, B], F32, 124)
        ehT = ph("ehT", [128, 2, 2, B], F32, 128)
        eo = ph("eo", [128, U, D], F32, 40)
        Yt = ph("Yt", [P, 2, TOPK, D], F32, 80)
        fz = ph("fz", [P, 2, D], F32, 88)
        fT = ph("fT", [128, KD, N], F32, 60)
        f1T = ph("f1T", [128, 2, N], F32, 96)
        outS = ph("outS", [P, 2, D], F32, 92)

        ps = ctx.enter_context(nc.psum_tensor("ps", [128, 8 * 512], F32))

        def bank(b, n, p=128, off=0):
            return ps[0:p, b * 512 + off:b * 512 + off + n]

        qk_d = nc.dram_tensor("qk_d", [2, 2, 2 * 128, N], F32, kind="Internal").ap()
        z_d = nc.dram_tensor("z_d", [N, D], F32, kind="Internal").ap()
        y_d = nc.dram_tensor("y_d", [N * TOPK, D], F32, kind="Internal").ap()
        list_d = nc.dram_tensor("list_d", [RANKS * E, 1], U32, kind="Internal").ap()

        x_in = [sem(f"x_in{i}") for i in range(2)]
        edges_in, cols_in, rows_in = sem("edges_in"), sem("cols_in"), sem("rows_in")
        mw_in, mwo_in, gw_in = sem("mw_in"), sem("mwo_in"), sem("gw_in")
        waf_in, small_in = sem("waf_in"), sem("small_in")
        ws1_in, ws2_in, wf1_in, wf2_in = sem("ws1_in"), sem("ws2_in"), sem("wf1_in"), sem("wf2_in")
        st_in = [sem(f"st_in{i}") for i in range(2)]
        w_in = [sem(f"w_in{u}") for u in range(U)]
        consts = sem("consts")
        filled = sem("filled")
        act_read, dve_read = sem("act_read"), sem("dve_read")
        ln_var, ln_std = sem("ln_var"), sem("ln_std")
        xn_made, xr_made = sem("xn_made"), sem("xr_made")
        feat_q = sem("feat_q")
        qT_made = sem("qT_made")
        tk_made, ek_made, kf_made = sem("tk_made"), sem("ek_made"), sem("kf_made")
        kv_summed, kvb_made = sem("kv_summed"), sem("kvb_made")
        kv_used = sem("kv_used")
        split_made = sem("split_made")
        qk_out = [sem(f"qk_out{i}") for i in range(4)]
        cmax_made, range_made = sem("cmax_made"), sem("range_made")
        edges_f = sem("edges_f")
        oh_made = [sem(f"oh_made{b}") for b in range(T)]
        oh_used = [sem(f"oh_used{b}") for b in range(T)]
        c_sum, c_kept = sem("c_sum"), sem("c_kept")
        s_made, s_exp, att_made, att_used = sem("s_made"), sem("s_exp"), sem("att_made"), sem("att_used")
        head_sum, head_kept = sem("head_sum"), sem("head_kept")
        st_used = sem("st_used")
        y_made, z_made, z_out = sem("y_made"), sem("z_made"), sem("z_out")
        lmax_made, prob_exp, m_made = sem("lmax_made"), sem("prob_exp"), sem("m_made")
        comb_made, pos_made, list_clear, list_made = (sem("comb_made"), sem("pos_made"),
                                                      sem("list_clear"), sem("list_made"))
        round_made, lst_in, gat_made = sem("round_made"), sem("lst_in"), sem("gat_made")
        zg_in = [sem(f"zg_in{u}") for u in range(U)]
        tr_done, tr_read, h_done, h_read = sem("tr_done"), sem("tr_read"), sem("h_done"), sem("h_read")
        e_done, e_read = sem("e_done"), sem("e_read")
        y_out = [sem(f"y_out{u}") for u in range(U)]
        yt_in = [sem(f"yt_in{i}") for i in range(2)]
        yt_used, fz_made = sem("yt_used"), sem("fz_made")
        out_made = sem("out_made")
        out_sent = [sem(f"out_sent{i}") for i in range(2)]
        blk = ctx.enter_context(nc.Block())

        def col(name, i, n=1, p=128):
            o = COLS[name][0] + i
            return cols[0:p, o:o + n]

        def row(name, n=D):
            return rows[0:P, ROWS[name], 0:n]

        @blk.sync
        def _(sp):
            x_v = A["x"].rearrange("(t p) d -> p t d", p=P)
            for i in range(2):
                sp.dma_start(xs[:, 5 * i:5 * i + 5, :], x_v[:, 5 * i:5 * i + 5, :]).then_inc(x_in[i], 16)
            sp.dma_start(cols[:, :], A["cols"]).then_inc(cols_in, 16)
            for j, w in enumerate(("mWqT", "mWkT", "mWvT")):
                sp.dma_start(mW[:, j], A[w].rearrange("(p k) n -> p k n", k=KD)).then_inc(mw_in, 16)
            for name, j in ROWS.items():
                sp.dma_start(rows[:, j, :], A["rows"][j:j + 1, :].partition_broadcast(128)).then_inc(rows_in, 16)
            sp.dma_start(mWo[:, :, :], A["mWoT"].rearrange("(k p) n -> p k n", p=128)).then_inc(mwo_in, 16)
            for j, w in enumerate(("gWq", "gWk", "gWv")):
                sp.dma_start(gW[:, j], A[w].rearrange("(p k) n -> p k n", k=KD)).then_inc(gw_in, 16)
            sp.dma_start(Wr_s[:, :, :], A["Wr"].rearrange("(p k) n -> p k n", k=KD)).then_inc(small_in, 16)
            sp.dma_start(cbT_s[:, :], A["cbT"]).then_inc(small_in, 16)
            sp.dma_start(b2_s[:, :], A["b2"]).then_inc(small_in, 16)

            def weights(e, u, static=False):
                w1 = A["W1"] if static else A["W1"]
                sp.dma_start(W1[u][:, :, :], w1[bass.ds(e, 1)].rearrange("e (p k) f -> p (e k) f", k=KD)).then_inc(w_in[u], 16)
                sp.dma_start(W2[u][:, :, :], A["W2"][bass.ds(e, 1)].rearrange("e (p m) n -> p (e m) n", m=2)).then_inc(w_in[u], 16)

            for u in range(U):
                weights(u, u)
            sp.wait_ge(filled, TURNS.filled("mix_o", 23))
            for j, w in enumerate(("src", "dst")):
                sp.dma_start(e_i[:, j, :], A[w]).then_inc(edges_in, 16)
            sp.wait_ge(filled, TURNS.filled("gnn_v", 9))
            sp.dma_start(Wa_s[:, :, :], A["Wa"].rearrange("(p k) n -> p k n", k=2)).then_inc(waf_in, 16)
            sp.dma_start(Wf_s[:, :, :], A["Wf"].rearrange("(p k) n -> p k n", k=KD)).then_inc(waf_in, 16)
            for i in range(4):
                sp.wait_ge(qk_out[i], 32)
            for h in range(HEADS):
                if h >= 2:
                    sp.wait_ge(st_used, h - 1)
                for j in range(4):
                    d = h * DK
                    sp.dma_start(Kst[32 * j:32 * j + 32, h % 2, :].bitcast(F32), qk_d[1, j // 2, d:d + DK, :]).then_inc(st_in[h % 2], 16)
                    sp.dma_start(Qst[32 * j:32 * j + 32, h % 2, :].bitcast(F32), qk_d[0, j % 2, d:d + DK, :]).then_inc(st_in[h % 2], 16)
            sp.wait_ge(filled, TURNS.filled("gnn_a", 11))
            sp.dma_start(Ws2_s[:, :, :], A["Ws2"].rearrange("(k p) n -> p k n", p=128)).then_inc(ws2_in, 16)
            sp.dma_start(Wf1_s[:, :, :], A["Wf1"].rearrange("(p k) n -> p k n", k=KD)).then_inc(wf1_in, 16)
            sp.wait_ge(filled, TURNS.filled("gnn_f", 9))
            sp.dma_start(Ws1_s[:, :, :], A["Ws1"].rearrange("(p k) n -> p k n", k=KD)).then_inc(ws1_in, 16)
            with sp.Fori(1, GROUPS) as g:
                for u in range(U):
                    sp.wait_ge(e_done, U * g + u - U + 1)
                    weights(U * g + u, u)
            sp.wait_ge(round_made, 1)
            R = sp.value_load(rounds[0:1, 0:1], min_val=1, max_val=RANKS // B)
            with sp.If(R > 1):
                with sp.Fori(1, R) as r:
                    with sp.Fori(0, GROUPS) as g:
                        for u in range(U):
                            sp.wait_ge(e_done, E * r + U * g + u - U + 1)
                            weights(U * g + u, u)
            sp.dma_start(Wf2_s[:, :, :], A["Wf2"].rearrange("(p k) n -> p k n", k=2)).then_inc(wf2_in, 16)
            for u in range(U):
                sp.wait_ge(y_out[u], R * (16 * GROUPS))
            y_v = y_d.rearrange("(t p k) d -> t p k d", p=P, k=TOPK)
            for t in range(T):
                if t >= 2:
                    sp.wait_ge(yt_used, t - 1)
                sp.dma_start(Yt[:, t % 2], y_v[t]).then_inc(yt_in[t % 2], 16)
            o_v = out.rearrange("(t p) d -> t p d", p=P)
            for t in range(T):
                sp.wait_ge(out_made, t + 1)
                sp.dma_start(o_v[t], outS[:, t % 2, :]).then_inc(out_sent[t % 2], 16)
            for i in range(2):
                sp.wait_ge(out_sent[i], 16 * (T // 2))

        @blk.gpsimd
        def _(gp):
            nc.gpsimd.memset(ident[:, :], 0.0)
            nc.gpsimd.memset(eps[:, :], 1e-5)
            nc.gpsimd.memset(zeros[:, :], 0.0)
            gp.drain()
            nc.gpsimd.affine_select(out=ident[:, :], in_=ident[:, :], compare_op=ALU.not_equal, fill=1.0,
                                    base=0, pattern=[[-1, 128]], channel_multiplier=1)
            gp.drain().then_inc(consts, 1)
            gp.wait_ge(rows_in, 16 * len(ROWS))
            for t in range(T):
                gp.wait_ge(xn_made, t + 1)
                nc.gpsimd.tensor_tensor(XR[:, t, :], xs[:, t, :], xn[:, t, :], ALU.add)
            gp.drain()
            for t in range(T):
                nc.gpsimd.tensor_tensor(XR[:, t, :], XR[:, t, :], row("mbo"), ALU.add)
            gp.drain().then_inc(xr_made, 1)
            gp.wait_ge(act_read, TURNS.group_read("xnT", 8)[1])
            gp.wait_ge(dve_read, TURNS.group_read("xnT", 9)[1])
            nc.gpsimd.memset(vt[:, :, :, 128:129], 1.0)
            gp.drain().then_inc(consts, 1)
            gp.wait_ge(filled, TURNS.filled("mix_o", 23))
            nc.gpsimd.iota(gi[:, 0, :], pattern=[[1, EC // EG], [0, EG]], base=1, channel_multiplier=0,
                           allow_small_or_imprecise_dtypes=True)
            nc.gpsimd.iota(gi[:, 1, :], pattern=[[-1, EC // EG], [0, EG]], base=EC // EG, channel_multiplier=0,
                           allow_small_or_imprecise_dtypes=True)
            nc.gpsimd.iota(lim[:, 0:1], pattern=[[0, 1]], base=0, channel_multiplier=P,
                           allow_small_or_imprecise_dtypes=True)
            nc.gpsimd.iota(lim[:, 1:2], pattern=[[0, 1]], base=-P, channel_multiplier=-P,
                           allow_small_or_imprecise_dtypes=True)
            nc.gpsimd.iota(iota[:, :], pattern=[[1, N]], base=0, channel_multiplier=0,
                           allow_small_or_imprecise_dtypes=True)
            gp.wait_ge(edges_f, 1)
            nc.gpsimd.partition_all_reduce(cmx[:, 0, :], e_f[:, 1, :], P, bass.bass_isa.ReduceOp.max)
            nc.gpsimd.partition_all_reduce(cmx[:, 1, :], neg[:, :], P, bass.bass_isa.ReduceOp.max)
            gp.drain().then_inc(cmax_made, 1)
            gp.drain().then_inc(consts, 1)
            for i in range(4):
                gp.wait_ge(split_made, i + 1)
                w, m = i // 2, i % 2
                gp.dma_start(qk_d[w, 0, 128 * m:128 * m + 128, :], qk_hi[:, i % 2, :].bitcast(F32)).then_inc(qk_out[i], 16)
                gp.dma_start(qk_d[w, 1, 128 * m:128 * m + 128, :], qk_lo[:, i % 2, :].bitcast(F32)).then_inc(qk_out[i], 16)
            z_v = z_d.rearrange("(t p) d -> t p d", p=P)
            gp.wait_ge(head_sum, HEADS)
            gp.wait_ge(filled, TURNS.filled("gnn_f", 9))
            for t in range(T):
                gp.wait_ge(y_made, t + 1)
                nc.gpsimd.tensor_tensor(XR[:, t, :], XR[:, t, :], yz[:, t, :], ALU.add)
            gp.drain().then_inc(xr_made, 1)
            for t in range(T):
                gp.wait_ge(z_made, t + 1)
                gp.dma_start(z_v[t], yz[:, t, :]).then_inc(z_out, 16)
            nc.gpsimd.iota(iotaE_i[:, :], pattern=[[1, E]], base=0, channel_multiplier=0)
            gp.wait_ge(z_out, 16 * T)
            gp.wait_ge(act_read, TURNS.group_read("hT", 9)[1])
            nc.gpsimd.iota(toki[:, :, :], pattern=[[1, TOPK], [TOPK * P, T]], base=0, channel_multiplier=TOPK)
            nc.gpsimd.memset(nobody[:, :], NOBODY)
            nc.gpsimd.memset(lst[:, :], NOBODY)
            nc.gpsimd.memset(ones[:, :], 1.0)
            gp.drain()
            nc.gpsimd.tensor_copy(iotaE[:, :], iotaE_i[:, :])
            nc.gpsimd.affine_select(out=ltri[:, :], in_=ones[:, :], compare_op=ALU.is_gt, fill=0.0,
                                    base=0, pattern=[[1, P]], channel_multiplier=-1)
            gp.drain().then_inc(consts, 1)
            gp.dma_start(list_d.rearrange("(p n) o -> p (n o)", p=128), nobody[:, :]).then_inc(list_clear, 16)
            gp.wait_ge(list_clear, 16)
            gp.wait_ge(pos_made, 1)
            for k in range(TOPK):
                for t in range(T):
                    gp.indirect_dma_start(
                        out=list_d, out_offset=bass.IndirectOffsetOnAxis(ap=posi[:, k, t:t + 1], axis=0),
                        in_=toki[:, k, t:t + 1], in_offset=None).then_inc(list_made, 16)
            gp.wait_ge(list_made, 16 * TOPK * T)
            gp.wait_ge(dve_read, TURNS.group_read("rank", 2)[1])
            nc.gpsimd.memset(Zg[:, :, :], 0.0)
            gp.drain()
            gp.wait_ge(round_made, 1)
            R = gp.value_load(rounds[0:1, 0:1], min_val=1, max_val=RANKS // B)

            def wait_alone(s, value, j=0):
                gp.wait_ge(s, value)
                nc.gpsimd.tensor_tensor(carry[:, j, :], eps[0:1, :], eps[0:1, :], ALU.add)

            def gather(n, c, u):
                nc.gpsimd.tensor_copy(idxg[:, u, :], gat[:, bass.ds(c, 1)])
                gp.drain()
                gp.indirect_dma_start(out=Zg[:, u, :], out_offset=None, in_=z_d,
                                      in_offset=bass.IndirectOffsetOnAxis(ap=idxg[:, u, :], axis=0),
                                      bounds_check=N - 1, oob_is_err=False).then_inc(zg_in[u], 16)

            def one_round(r):
                gp.dma_start(lst[:, 0:E], list_d.rearrange("(r p e) o -> r p (e o)", p=B, e=E)[bass.ds(r, 1)]
                             .rearrange("r p e -> (r p) e")).then_inc(lst_in, 16)
                wait_alone(gat_made, r + 1)
                for u in range(U):
                    gather(E * r + u, u, u)

                def group(g):
                    for u in range(U):
                        n = E * r + U * g + u
                        if not (isinstance(g, int) and isinstance(r, int)):
                            wait_alone(y_out[u], (GROUPS * r + g) * 16)
                        nc.gpsimd.tensor_copy(idxs[:, u, :], lst[:, bass.ds(U * g + u, 1)])
                        gp.drain()
                        wait_alone(e_read, n + 1, 1)
                        gp.indirect_dma_start(out=y_d, out_offset=bass.IndirectOffsetOnAxis(ap=idxs[:, u, :], axis=0),
                                              in_=eo[:, u, :], in_offset=None,
                                              bounds_check=N * TOPK - 1, oob_is_err=False).then_inc(y_out[u], 16)
                        gather(n + U, U * g + u + U, u)
                group(0)
                with gp.Fori(1, GROUPS) as g:
                    group(g)

            one_round(0)
            with gp.If(R > 1):
                with gp.Fori(1, R) as r:
                    one_round(r)
            for u in range(U):
                wait_alone(zg_in[u], R * (16 * (GROUPS + 1)))
                gp.drain()

        @blk.vector
        def _(v):
            V_ = nc.vector

            def reads(name, i):
                v.wait_ge(filled, TURNS.filled(name, i))

            def stats(src, mvt, tiles):
                for t in tiles:
                    V_.bn_stats(st[:, t, :], src[:, t, :])
                v.drain()
                for t in tiles:
                    V_.bn_aggr(mvt[:, t, :], st[:, t, :])
                v.drain().then_inc(ln_var, 1)

            def inverse_std(count):
                v.wait_ge(ln_std, count)
                V_.reciprocal(rs[:, :], rs[:, :])
                v.drain()

            def normalise(dst, src, mvt, t):
                return V_.tensor_scalar(dst, src, mvt[:, t, 0:1], rs[:, t:t + 1], ALU.subtract, ALU.mult)

            v.wait_ge(x_in[0], 16)
            v.wait_ge(x_in[1], 16)
            v.wait_ge(consts, 1)
            stats(xs, mv, range(T))
            inverse_std(1)
            for t in range(T):
                normalise(xn[:, t, :], xs[:, t, :], mv, t).then_inc(xn_made, 1)
            for t in range(1, T, 2):
                reads("xnT", t)
                V_.tensor_copy(xnT[:, :, t * P:t * P + P],
                               bank(TURNS.bank("xnT", t), 4 * P).rearrange("p (k n) -> p k n", k=4)).then_inc(dve_read, 1)
            for m in range(KD):
                for c, (o, n) in enumerate(CHUNKS):
                    i = 3 * m + c
                    v.wait_ge(feat_q, i + 1)
                    V_.scalar_tensor_tensor(qT[:, m, o:o + n], eq[:, i % 2, 0:n], 1.0, rq[:, i % 2, 0:n],
                                            ALU.min, ALU.add).then_inc(qT_made, 1)
            v.wait_ge(rows_in, 16 * len(ROWS))
            v.wait_ge(consts, 2)
            v.drain()
            for t in range(T):
                reads("mix_kv", 2 * t)
                V_.tensor_tensor(tk[:, t % 2, :], bank(TURNS.bank("mix_kv", 2 * t), D, P), row("mbk"), ALU.add).then_inc(dve_read, 1)
                v.drain().then_inc(tk_made, 1)
                if t >= 2:
                    v.wait_ge(kv_used, t - 1)
                V_.tensor_scalar(kf[:, t % 2, :], tk[:, t % 2, :], 0.0, None, ALU.max)
                reads("mix_kv", 2 * t + 1)
                V_.tensor_tensor(vt[:, t % 2, :, 0:128], bank(TURNS.bank("mix_kv", 2 * t + 1), D, P).rearrange("p (k n) -> p k n", k=KD),
                                 row("mbv").rearrange("p (k n) -> p k n", k=KD), ALU.add).then_inc(dve_read, 1)
                v.wait_ge(ek_made, t + 1)
                v.drain()
                V_.scalar_tensor_tensor(kf[:, t % 2, :], ek[:, t % 2, :], 1.0, kf[:, t % 2, :], ALU.min, ALU.add)
                v.drain().then_inc(kf_made, 1)
            V_.memset(kvb[:, :, :], 0.0)
            V_.memset(ksb[:, :, :], 0.0)
            v.drain()
            v.wait_ge(kv_summed, 1)
            for p in range(KD):
                src = ps[:, (6 + p // 2) * 512 + (p % 2) * 129:(6 + p // 2) * 512 + (p % 2) * 129 + 129]
                for a in (0, 64):
                    V_.tensor_copy(kvb[a:a + 64, p, a:a + 64], src[a:a + 64, a:a + 64])
                    V_.tensor_copy(ksb[a:a + 64, p, a:a + 64], src[a:a + 64, 128:129].to_broadcast([64, 64]))
            v.drain().then_inc(kvb_made, 1)
            v.wait_ge(xr_made, 1)
            for i in range(12):
                p, (o, n) = i // 3, CHUNKS[i % 3]
                reads("mix_o", 2 * i)
                V_.tensor_scalar(zt[:, i % 2, 0:n], bank(TURNS.bank("mix_o", 2 * i), n), 1e-6, None, ALU.add).then_inc(dve_read, 1)
                v.drain()
                V_.reciprocal(zt[:, i % 2, 0:n], zt[:, i % 2, 0:n])
                v.drain()
                reads("mix_o", 2 * i + 1)
                V_.tensor_tensor(moT[:, p, o:o + n], bank(TURNS.bank("mix_o", 2 * i + 1), n), zt[:, i % 2, 0:n], ALU.mult).then_inc(dve_read, 1)
            for t in range(T):
                reads("mix_wo", t)
                V_.tensor_tensor(XR[:, t, :], bank(TURNS.bank("mix_wo", t), D, P), XR[:, t, :], ALU.add).then_inc(dve_read, 1)
            v.wait_ge(edges_in, 32)
            V_.tensor_copy(e_f[:, :, :], e_i[:, :, :])
            v.drain()
            V_.tensor_scalar(neg[:, :], e_f[:, 1, :], -1.0, None, ALU.mult)
            v.drain().then_inc(edges_f, 1)
            for i in range(4):
                v.wait_ge(act_read, TURNS.group_read("gnn_qk", 3 * i + 2)[1])
                if i >= 2:
                    v.wait_ge(qk_out[i - 2], 32)
                V_.tensor_copy(qk_hi[:, i % 2, :], fqk[:, i % 2, :])
                v.drain()
                V_.tensor_tensor(qk_lo[:, i % 2, :], fqk[:, i % 2, :], qk_hi[:, i % 2, :].bitcast(F32), ALU.subtract)
                v.drain().then_inc(split_made, 1)
            V_.memset(V[:, :, :, DK:DK + 1], 1.0)
            for t in range(T):
                reads("gnn_v", t)
                V_.tensor_tensor(V[:, t, :, 0:DK], bank(TURNS.bank("gnn_v", t), HEADS * DK, P).rearrange("p (h d) -> p h d", h=HEADS),
                                 row("gbv", HEADS * DK).rearrange("p (h d) -> p h d", h=HEADS), ALU.add).then_inc(dve_read, 1)
            v.wait_ge(cmax_made, 1)
            v.wait_ge(consts, 3)
            lo, hi = lim[:, 2:3], lim[:, 3:4]
            V_.tensor_scalar(ov[:, 0, :], cmx[0:T, 0, :], lim[:, 0:1], None, ALU.is_ge)
            V_.tensor_scalar(ov[:, 1, :], cmx[0:T, 1, :], lim[:, 1:2], None, ALU.is_gt)
            v.drain()
            V_.tensor_tensor(ov[:, 2, :], ov[:, 0, :], ov[:, 1, :], ALU.mult)
            v.drain()
            V_.tensor_tensor(ov[:, 0, :], ov[:, 2, :], gi[:, 0, :], ALU.mult)
            V_.tensor_tensor(ov[:, 1, :], ov[:, 2, :], gi[:, 1, :], ALU.mult)
            v.drain()
            V_.tensor_reduce(hi, ov[:, 0, :], axis=AX.X, op=ALU.max)
            V_.tensor_reduce(lo, ov[:, 1, :], axis=AX.X, op=ALU.max)
            v.drain()
            V_.tensor_scalar(hi, hi, 1.0, None, ALU.max)
            V_.tensor_scalar(lo, lo, -1.0, float(EC // EG), ALU.mult, ALU.add)
            v.drain()
            V_.tensor_scalar(lim[:, 4:5], hi, -1.0, None, ALU.add)
            v.drain()
            V_.tensor_tensor(lo, lo, lim[:, 4:5], ALU.min)
            v.drain()
            V_.tensor_tensor(hi, hi, lo, ALU.subtract)
            v.drain()
            V_.tensor_copy(ranges[:, :], lim[:, 2:4])
            v.drain().then_inc(range_made, 1)
            for b in range(T):
                lo_b = v.value_load(ranges[b:b + 1, 0:1], min_val=0, max_val=EC // EG - 1)
                n_b = v.value_load(ranges[b:b + 1, 1:2], min_val=1, max_val=EC // EG)
                with v.Fori(0, n_b) as g:
                    grp = nc.s_assert_within(lo_b + g, 0, EC // EG - 1, skip_runtime_bounds_check_because=
                                             "first group + count is at most the number of groups, as made above")
                    for j in range(EG):
                        v.wait_ge(oh_used[b], g * EG + j + 1)
                        V_.tensor_scalar(ohA[:, j, :], iota[:, b * P:b * P + P], e_f[:, 1, bass.ds(grp * EG + j, 1)], None, ALU.is_equal)
                        V_.tensor_scalar(ohB[:, j, :], iota[:, :], e_f[:, 0, bass.ds(grp * EG + j, 1)], None, ALU.is_equal)\
                          .then_inc(oh_made[b], 1)
            v.wait_ge(c_kept, T)

            def keep_head(h):
                v.wait_ge(head_sum, h + 1)
                s = bank(6 + h % 2, T * (DK + 1), P).rearrange("p (t d) -> p t d", t=T)
                V_.tensor_scalar(den[:, :, :], s[:, :, DK:DK + 1], TINY, None, ALU.max)
                v.drain()
                V_.reciprocal(den[:, :, :], den[:, :, :])
                v.drain()
                V_.tensor_tensor(agg[:, :, h * DK:h * DK + DK], s[:, :, 0:DK], den[:, :, :].to_broadcast([P, T, DK]), ALU.mult).then_inc(head_kept, 1)
                v.drain()

            for n in range(HEADS * T):
                h, s = divmod(n, T)
                v.wait_ge(s_exp, n + 1)
                if n >= 3:
                    v.wait_ge(att_used, n - 2)
                V_.tensor_tensor(att[:, n % 3, :], ps[0:P, (n % 2) * 1536:(n % 2) * 1536 + N], C[:, s, :], ALU.mult).then_inc(att_made, 1)
                if s == 1 and h >= 1:
                    keep_head(h - 1)
            keep_head(HEADS - 1)
            for t in range(T):
                reads("gnn_f", t)
                V_.tensor_tensor(tf[:, t % 2, :], bank(TURNS.bank("gnn_f", t), D, P), row("gbf"), ALU.add).then_inc(dve_read, 1)
                v.drain()
                V_.scalar_tensor_tensor(XR[:, t, :], tf[:, t % 2, :], 0.0, XR[:, t, :], ALU.max, ALU.add)
            v.drain()
            stats(XR, mv, range(T))
            inverse_std(2)
            for t in range(T):
                normalise(yz[:, t, :], XR[:, t, :], mv, t).then_inc(y_made, 1)
            v.drain()
            stats(yz, mv2, range(T))
            inverse_std(3)
            v.wait_ge(xr_made, 2)
            for t in range(T):
                normalise(yz[:, t, :], yz[:, t, :], mv2, t).then_inc(z_made, 1)
            V_.tensor_scalar(row("bs2"), row("bs2"), 0.25, None, ALU.mult)
            for i in range(2):
                reads("logit", i)
                V_.tensor_scalar(prob[:, 5 * i:5 * i + 5, :], bank(TURNS.bank("logit", i), 5 * E, P).rearrange("p (t e) -> p t e", t=5),
                                 1 / 0.7, None, ALU.mult).then_inc(dve_read, 1)
            v.drain()
            V_.tensor_reduce(sm[:, 0, :], prob[:, :, :], axis=AX.X, op=ALU.max)
            v.drain()
            V_.tensor_scalar(sm[:, 0, :], sm[:, 0, :], -1.0, None, ALU.mult)
            v.drain().then_inc(lmax_made, 1)
            v.wait_ge(prob_exp, T)
            V_.reciprocal(sm[:, 1, :], sm[:, 1, :])
            v.drain()
            V_.tensor_tensor(prob[:, :, :], prob[:, :, :], sm[:, 1, :].unsqueeze(2).to_broadcast([P, T, E]), ALU.mult)
            v.drain()
            for t in range(T):
                V_.max(top8[:, t, :], prob[:, t, :])
            v.drain()
            for t in range(T):
                V_.max_index(idx8[:, t, :], top8[:, t, :], prob[:, t, :])
            V_.tensor_tensor(sm[:, 2, :].unsqueeze(2), top8[:, :, 0:1], top8[:, :, 1:2], ALU.add)
            v.drain()
            V_.reciprocal(sm[:, 2, :], sm[:, 2, :])
            V_.tensor_copy(sm[:, 3:5, :].rearrange("p k t -> p t k"), idx8[:, :, 0:TOPK])
            v.drain()
            v.wait_ge(consts, 4)
            V_.tensor_tensor(wtop[:, :, :], top8[:, :, 0:TOPK], sm[:, 2, :].unsqueeze(2).to_broadcast([P, T, TOPK]), ALU.mult)
            for k, M in ((0, M1), (1, M2)):
                V_.tensor_tensor(M[:, :, :], iotaE[:, :].unsqueeze(1).to_broadcast([P, T, E]),
                                 sm[:, 3 + k, :].unsqueeze(2).to_broadcast([P, T, E]), ALU.is_equal)
            v.drain()
            V_.tensor_tensor(Mb[:, :, :], M1[:, :, :], M2[:, :, :], ALU.add)
            v.drain().then_inc(m_made, 1)
            V_.tensor_tensor(prob[:, :, :], M1[:, :, :], wtop[:, :, 0:1].to_broadcast([P, T, E]), ALU.mult)
            V_.tensor_tensor(tmpr[:, :, :], M2[:, :, :], wtop[:, :, 1:2].to_broadcast([P, T, E]), ALU.mult)
            v.drain()
            V_.tensor_tensor(prob[:, :, :], prob[:, :, :], tmpr[:, :, :], ALU.add)
            v.drain()
            V_.tensor_scalar(prob[:, :, :], prob[:, :, :], 4.0, None, ALU.mult)
            v.drain().then_inc(comb_made, 1)
            for i in range(2):
                reads("rank", i)
                V_.tensor_copy(rankS[:, 5 * i:5 * i + 5, :], bank(TURNS.bank("rank", i), 5 * E, P).rearrange("p (t e) -> p t e", t=5)).then_inc(dve_read, 1)
            reads("rank", 2)
            V_.tensor_reduce(sm[0:1, 5, 0:1], bank(TURNS.bank("rank", 2), E, 1), axis=AX.X, op=ALU.max).then_inc(dve_read, 1)
            v.drain()
            for k, M in ((0, M1), (1, M2)):
                V_.tensor_tensor(tmpr[:, :, :], M[:, :, :], rankS[:, :, :], ALU.mult)
                v.drain()
                V_.tensor_reduce(sm[:, 6 + k, :], tmpr[:, :, :], axis=AX.X, op=ALU.add)
                v.drain()
                V_.scalar_tensor_tensor(posf[:, k, :], sm[:, 6 + k, :], float(E), sm[:, 3 + k, :], ALU.mult, ALU.add)
            v.drain()
            V_.tensor_copy(posi[:, :, :], posf[:, :, :])
            v.drain().then_inc(pos_made, 1)
            V_.tensor_scalar(sm[0:1, 5, 1:2], sm[0:1, 5, 0:1], float(B - 1), None, ALU.add)
            v.drain()
            V_.tensor_copy(rounds[:, :], sm[0:1, 5, 1:2])
            v.drain()
            V_.tensor_single_scalar(rounds[:, :], rounds[:, :], B.bit_length() - 1, ALU.logical_shift_right)
            v.drain().then_inc(round_made, 1)
            for c in range(5):
                for k in range(2):
                    t = 2 * c + k
                    g = shared_out(c, k)
                    reads("shared", g)
                    V_.scalar_tensor_tensor(HM[:, t, :], bank(TURNS.bank("shared", g), D, P), 0.25, row("bs2"), ALU.mult, ALU.add).then_inc(dve_read, 1)
            R = v.value_load(rounds[0:1, 0:1], min_val=1, max_val=RANKS // B)

            def one_round(r):
                v.wait_ge(lst_in, 16 * (r + 1))
                if not isinstance(r, int):
                    v.wait_ge(zg_in[U - 1], 16 * (GROUPS + 1) * r)
                V_.tensor_single_scalar(gat[:, :], lst[:, :], 1, ALU.logical_shift_right)
                v.drain().then_inc(gat_made, 1)

                def group(g, first):
                    for u in range(U):
                        n = E * r + U * g + u
                        v.wait_ge(tr_done, n + 1)
                        at_least(v, h_done, n - 1)
                        for k in range(KD):
                            i = V_.tensor_scalar(hgT[:, u % 2, k, :], bank(u % 2, B, 128, k * B), col("g1", k), col("b1ln", k), ALU.mult, ALU.add)
                        i.then_inc(tr_read, 1)
                group(0, True)
                with v.Fori(1, GROUPS) as g:
                    group(g, False)

            v.wait_ge(cols_in, 16)
            one_round(0)
            with v.If(R > 1):
                with v.Fori(1, R) as r:
                    one_round(r)
            for t in range(T):
                v.wait_ge(yt_in[t % 2], 16 * (t // 2 + 1))
                V_.scalar_tensor_tensor(HM[:, t, :], Yt[:, t % 2, 0, :], wtop[:, t, 0:1], HM[:, t, :], ALU.mult, ALU.add)
                v.drain()
                V_.scalar_tensor_tensor(HM[:, t, :], Yt[:, t % 2, 1, :], wtop[:, t, 1:2], HM[:, t, :], ALU.mult, ALU.add)
                v.drain().then_inc(yt_used, 1)
            stats(HM, mv, range(T))
            inverse_std(4)
            for t in range(T):
                if t >= 2:
                    v.wait_ge(filled, TURNS.filled("fT", t - 2))
                normalise(fz[:, t % 2, :], HM[:, t, :], mv, t).then_inc(fz_made, 1)
                V_.tensor_tensor(XR[:, t, :], XR[:, t, :], row("bf2"), ALU.add)
                v.drain()
                V_.tensor_tensor(XR[:, t, :], XR[:, t, :], HM[:, t, :], ALU.add)
            v.drain()
            for t in range(T):
                reads("f2", t)
                if t >= 2:
                    v.wait_ge(out_sent[t % 2], 16 * (t // 2))
                V_.tensor_tensor(outS[:, t % 2, :], bank(TURNS.bank("f2", t), D, P), XR[:, t, :], ALU.add).then_inc(dve_read, 1)
                v.drain().then_inc(out_made, 1)

        @blk.scalar
        def _(a):
            S_ = nc.scalar

            def reads(name, i):
                a.wait_ge(filled, TURNS.filled(name, i))

            def std(mvt, count):
                a.wait_ge(ln_var, count)
                S_.activation(rs[:, :].unsqueeze(2), mvt[:, :, 1:2], ACT.Sqrt, bias=eps[:, :]).then_inc(ln_std, 1)

            std(mv, 1)
            for t in range(0, T, 2):
                reads("xnT", t)
                S_.copy(xnT[:, :, t * P:t * P + P], bank(TURNS.bank("xnT", t), 4 * P).rearrange("p (k n) -> p k n", k=4)).then_inc(act_read, 1)
            a.wait_ge(cols_in, 16)
            for m in range(KD):
                for c, (o, n) in enumerate(CHUNKS):
                    i = 3 * m + c
                    reads("mix_q", i)
                    if i >= 2:
                        a.wait_ge(qT_made, i - 1)
                    b = bank(TURNS.bank("mix_q", i), n)
                    S_.activation(eq[:, i % 2, 0:n], b, ACT.Exp, bias=col("mbq", m))
                    S_.activation(rq[:, i % 2, 0:n], b, ACT.Relu, bias=col("mbq", m)).then_inc(act_read, 1)
                    a.drain().then_inc(feat_q, 1)
            a.wait_ge(qT_made, 12)
            for t in range(T):
                a.wait_ge(tk_made, t + 1)
                if t >= 2:
                    a.wait_ge(kf_made, t - 1)
                S_.activation(ek[:, t % 2, :], tk[:, t % 2, :], ACT.Exp).then_inc(ek_made, 1)
            for i in range(4):
                for c, (o, n) in enumerate(CHUNKS):
                    reads("gnn_qk", 3 * i + c)
                    if i >= 2 and c == 0:
                        a.wait_ge(split_made, i - 1)
                    S_.activation(fqk[:, i % 2, o:o + n], bank(TURNS.bank("gnn_qk", 3 * i + c), n), ACT.Identity,
                                  bias=col("gbq" if i < 2 else "gbk", i % 2)).then_inc(act_read, 1)
            a.wait_ge(filled, TURNS.filled("gnn_v", 9))
            for b in range(T):
                a.wait_ge(c_sum, b + 1)
                S_.copy(C[:, b, :], ps[0:P, (b % 2) * 1536:(b % 2) * 1536 + N]).then_inc(c_kept, 1)
            for n in range(HEADS * T):
                a.wait_ge(s_made, n + 1)
                b = ps[0:P, (n % 2) * 1536:(n % 2) * 1536 + N]
                S_.activation(b, b, ACT.Exp, scale=float(DK) ** -0.5).then_inc(s_exp, 1)
            for t in range(T):
                reads("aggT", t)
                S_.activation(aggT[:, :, t * P:t * P + P], bank(TURNS.bank("aggT", t), 2 * P).rearrange("p (k n) -> p k n", k=2),
                              ACT.Relu).then_inc(act_read, 1)
            for m in range(KD):
                for c, (o, n) in enumerate(CHUNKS):
                    i = 3 * m + c
                    reads("gnn_a", i)
                    S_.activation(h1T[:, m, o:o + n], bank(TURNS.bank("gnn_a", i), n), ACT.Relu, bias=col("ba", m)).then_inc(act_read, 1)
            std(mv, 2)
            std(mv2, 3)
            for t in range(T):
                reads("hT", t)
                for k in range(KD):
                    i = S_.activation(hT[:, k, t * P:t * P + P], bank(TURNS.bank("hT", t), P, 128, k * P), ACT.Identity,
                                      bias=col("b1ln", k), scale=col("g1", k))
                i.then_inc(act_read, 1)
            for c, (o, n) in enumerate(CHUNKS):
                reads("rT", c)
                S_.copy(rTs[:, o:o + n], bank(TURNS.bank("rT", c), n, E)).then_inc(act_read, 1)
            a.wait_ge(lmax_made, 1)
            for t in range(T):
                S_.activation(prob[:, t, :], prob[:, t, :], ACT.Exp, bias=sm[:, 0, t:t + 1], accum_out=sm[:, 1, t:t + 1]).then_inc(prob_exp, 1)
            for c, tiles in enumerate(((0, 4), (4, 4), (8, 2))):
                reads("combT", c)
                S_.copy(combT[:, tiles[0] * P:(tiles[0] + tiles[1]) * P], bank(TURNS.bank("combT", c), tiles[1] * P, E)).then_inc(act_read, 1)
            for c in range(5):
                if c >= 2:
                    a.wait_ge(filled, TURNS.filled("shared", shared_out(c - 2, 1)))
                for i in range(4):
                    g = shared_hid(c, i)
                    reads("shared", g)
                    for k in range(2):
                        j = S_.activation(hsT[:, c % 2, 2 * i + k, :], bank(TURNS.bank("shared", g), 250, 128, 250 * k), ACT.Silu, bias=col("bs1", 2 * i + k))
                    j.then_inc(act_read, 1)
            a.wait_ge(round_made, 1)
            R = a.value_load(rounds[0:1, 0:1], min_val=1, max_val=RANKS // B)

            def hidden(r, g, u):
                n = E * r + U * g + u
                a.wait_ge(h_done, n + 1)
                at_least(a, e_done, n - 1)
                for m in range(2):
                    i = S_.activation(ehT[:, u % 2, m, :], bank(2 + u % 2, B, 128, m * B), ACT.Silu,
                                      bias=cols[:, bass.ds(COLS["eb1"][0] + m + 2 * (U * g + u), 1)])
                i.then_inc(h_read, 1)

            def result(r, g, u):
                n = E * r + U * g + u
                a.wait_ge(e_done, n + 1)
                at_least(a, y_out[u], 16 * (GROUPS * r + g))
                S_.copy(eo[:, u, :], bank(4 + u % 2, D)).then_inc(e_read, 1)

            def one_round(r):
                def group(g, first):
                    for u in range(U):
                        hidden(r, g, u)
                        if u:
                            result(r, g, u - 1)
                        elif not first:
                            result(r, g - 1, U - 1)
                group(0, True)
                with a.Fori(1, GROUPS) as g:
                    group(g, False)
                result(r, GROUPS - 1, U - 1)

            one_round(0)
            with a.If(R > 1):
                with a.Fori(1, R) as r:
                    one_round(r)
            std(mv, 4)
            for t in range(T):
                reads("fT", t)
                for k in range(KD):
                    i = S_.activation(fT[:, k, t * P:t * P + P], bank(TURNS.bank("fT", t), P, 128, k * P), ACT.Identity,
                                      bias=col("bfln", k), scale=col("gf", k))
                i.then_inc(act_read, 1)
            for c, (o, n) in enumerate(CHUNKS):
                for m in range(2):
                    i = 2 * c + m
                    reads("f1", i)
                    S_.activation(f1T[:, m, o:o + n], bank(TURNS.bank("f1", i), n), ACT.Silu, bias=col("bf1", m)).then_inc(act_read, 1)

        @blk.tensor
        def _(pe):
            MM = nc.tensor.matmul

            def turn(name, i):
                g = TURNS.first[name] + i
                if g >= RING:
                    who, count = TURNS.read(g - RING)
                    pe.wait_ge(act_read if who == "act" else dve_read, count)
                return TURNS.bank(name, i)

            def read_by_now(name, i):
                who, count = TURNS.group_read(name, i)
                pe.wait_ge(act_read if who == "act" else dve_read, count)

            pe.wait_ge(consts, 1)
            for t in range(T):
                pe.wait_ge(xn_made, t + 1)
                b = turn("xnT", t)
                for k in range(KD):
                    i = nc.tensor.transpose(bank(b, P, 128, k * P), xn[:, t, k:D:KD], ident[0:P, 0:P])
                i.then_inc(filled, 1)
            read_by_now("xnT", 8)
            read_by_now("xnT", 9)
            pe.wait_ge(mw_in, 48)
            for m in range(KD):
                for c, (o, n) in enumerate(CHUNKS):
                    b = turn("mix_q", 3 * m + c)
                    for k in range(KD):
                        i = MM(bank(b, n), mW[:, 0, k, m * 128:m * 128 + 128], xnT[:, k, o:o + n], start=k == 0, stop=k == KD - 1)
                    i.then_inc(filled, 1)

            def sum_kv(t):
                pe.wait_ge(kf_made, t + 1)
                read_by_now("mix_kv", 2 * t + 1)
                for p in range(KD):
                    i = MM(bank(6 + p // 2, 129, 128, (p % 2) * 129), kf[:, t % 2, p * 128:p * 128 + 128], vt[:, t % 2, p, :],
                           start=t == 0 and p % 2 == 0, stop=t == T - 1 and p % 2 == 1, skip_group_check=True)
                i.then_inc(kv_used, 1)

            for t in range(T):
                for w in range(2):
                    b = turn("mix_kv", 2 * t + w)
                    for k in range(KD):
                        i = MM(bank(b, D, P), xnT[:, k, t * P:t * P + P], mW[:, 1 + w, k, :], start=k == 0, stop=k == KD - 1)
                    i.then_inc(filled, 1)
                if t:
                    sum_kv(t - 1)
            sum_kv(T - 1)
            pe.drain().then_inc(kv_summed, 1)
            pe.wait_ge(kvb_made, 1)
            pe.wait_ge(qT_made, 12)
            for i in range(12):
                p, (o, n) = i // 3, CHUNKS[i % 3]
                for j, w in enumerate((ksb, kvb)):
                    b = turn("mix_o", 2 * i + j)
                    MM(bank(b, n), w[:, p, :], qT[:, p, o:o + n], start=True, stop=True).then_inc(filled, 1)
            read_by_now("mix_o", 23)
            pe.wait_ge(mwo_in, 16)
            for t in range(T):
                b = turn("mix_wo", t)
                for k in range(KD):
                    i = MM(bank(b, D, P), moT[:, k, t * P:t * P + P], mWo[:, k, :], start=k == 0, stop=k == KD - 1)
                i.then_inc(filled, 1)
            pe.wait_ge(gw_in, 48)
            for i in range(4):
                for c, (o, n) in enumerate(CHUNKS):
                    b = turn("gnn_qk", 3 * i + c)
                    for k in range(KD):
                        j = MM(bank(b, n), gW[:, i // 2, k, (i % 2) * 128:(i % 2) * 128 + 128], xnT[:, k, o:o + n], start=k == 0, stop=k == KD - 1)
                    j.then_inc(filled, 1)
            for t in range(T):
                b = turn("gnn_v", t)
                for k in range(KD):
                    i = MM(bank(b, HEADS * DK, P), xnT[:, k, t * P:t * P + P], gW[:, 2, k, :], start=k == 0, stop=k == KD - 1)
                i.then_inc(filled, 1)
            for i in range(RING):
                read_by_now("gnn_v", 9 - i)
            pe.wait_ge(range_made, 1)
            for b in range(T):
                if b >= 2:
                    pe.wait_ge(c_kept, b - 1)
                for o, n in BANKED:
                    i = MM(ps[0:P, (b % 2) * 1536 + o:(b % 2) * 1536 + o + n], zeros[0:1, 0:P], zeros[0:1, 0:n],
                           start=True, stop=False, skip_group_check=True)
                i.then_inc(oh_used[b], EG)
                n_b = pe.value_load(ranges[b:b + 1, 1:2], min_val=1, max_val=EC // EG)
                with pe.Fori(0, n_b) as g:
                    for j in range(EG):
                        pe.wait_ge(oh_made[b], g * EG + j + 1)
                        for o, n in BANKED:
                            i = MM(ps[0:P, (b % 2) * 1536 + o:(b % 2) * 1536 + o + n], ohA[:, j, :], ohB[:, j, o:o + n],
                                   start=False, stop=False, skip_group_check=True)
                        i.then_inc(oh_used[b], 1)
                pe.drain().then_inc(c_sum, 1)
            def scores(n):
                h, s = divmod(n, T)
                if s == 0:
                    pe.wait_ge(st_in[h % 2], 128 * (h // 2 + 1))
                if n >= 2:
                    pe.wait_ge(att_made, n - 1)
                for o, c in BANKED:
                    i = MM(ps[0:P, (n % 2) * 1536 + o:(n % 2) * 1536 + o + c], Kst[:, h % 2, s * P:s * P + P], Qst[:, h % 2, o:o + c],
                           start=True, stop=True)
                i.then_inc(s_made, 1)
                if s == T - 1:
                    pe.drain().then_inc(st_used, 1)

            def sums(n):
                h, s = divmod(n, T)
                pe.wait_ge(att_made, n + 1)
                if s == 0 and h >= 2:
                    pe.wait_ge(head_kept, h - 1)
                for t in range(T):
                    i = MM(bank(6 + h % 2, DK + 1, P, t * (DK + 1)), att[:, n % 3, t * P:t * P + P], V[:, s, h, :],
                           start=s == 0 and t == 0, stop=s == T - 1 and t == T - 1, skip_group_check=True)
                i.then_inc(att_used, 1)
                if s == T - 1:
                    pe.drain().then_inc(head_sum, 1)

            pe.wait_ge(c_kept, T)
            scores(0)
            for n in range(HEADS * T):
                if n + 1 < HEADS * T:
                    scores(n + 1)
                sums(n)
            pe.wait_ge(head_kept, HEADS)
            for t in range(T):
                b = turn("aggT", t)
                for k in range(2):
                    i = nc.tensor.transpose(bank(b, P, 128, k * P), agg[:, t, k:HEADS * DK:2], ident[0:P, 0:P])
                i.then_inc(filled, 1)
            for i in range(2):
                read_by_now("aggT", 9 - i)
            pe.wait_ge(waf_in, 32)
            for m in range(KD):
                for c, (o, n) in enumerate(CHUNKS):
                    b = turn("gnn_a", 3 * m + c)
                    for k in range(2):
                        i = MM(bank(b, n), Wa_s[:, k, m:D:KD], aggT[:, k, o:o + n], start=k == 0, stop=k == 1)
                    i.then_inc(filled, 1)
            read_by_now("gnn_a", 11)
            for t in range(T):
                b = turn("gnn_f", t)
                for k in range(KD):
                    i = MM(bank(b, D, P), h1T[:, k, t * P:t * P + P], Wf_s[:, k, :], start=k == 0, stop=k == KD - 1)
                i.then_inc(filled, 1)
            for t in range(T):
                pe.wait_ge(z_made, t + 1)
                b = turn("hT", t)
                for k in range(KD):
                    i = nc.tensor.transpose(bank(b, P, 128, k * P), yz[:, t, k:D:KD], ident[0:P, 0:P])
                i.then_inc(filled, 1)
            read_by_now("hT", 9)
            pe.wait_ge(small_in, 48)
            for c, (o, n) in enumerate(CHUNKS):
                b = turn("rT", c)
                for k in range(KD):
                    i = MM(bank(b, n, E), Wr_s[:, k, :], hT[:, k, o:o + n], start=k == 0, stop=k == KD - 1)
                i.then_inc(filled, 1)
            read_by_now("rT", 2)
            for c in range(2):
                b = turn("logit", c)
                for t in range(5):
                    i = MM(bank(b, E, P, t * E), rTs[:, (5 * c + t) * P:(5 * c + t + 1) * P], cbT_s[:, :], start=True, stop=True)
                i.then_inc(filled, 1)
            pe.wait_ge(m_made, 1)
            for c in range(3):
                b = turn("rank", c)
                for t in (range(5 * c, 5 * c + 5) if c < 2 else (T,)):
                    o = (t - 5 * c) * E
                    for q in range(min(t + 1, T)):
                        i = MM(bank(b, E, P, o), (ltri if q == t else ones)[:, :], Mb[:, q, :], start=q == 0, stop=q == min(t, T - 1))
                i.then_inc(filled, 1)
            pe.wait_ge(comb_made, 1)
            for c, (t0, n) in enumerate(((0, 4), (4, 4), (8, 2))):
                b = turn("combT", c)
                for t in range(n):
                    i = nc.tensor.transpose(bank(b, P, E, t * P), prob[:, t0 + t, :], ident[0:P, 0:P])
                i.then_inc(filled, 1)
            pe.wait_ge(ws1_in, 16)
            pe.wait_ge(ws2_in, 16)

            def shared_rows(c):
                read_by_now("shared", shared_hid(c, 3))
                if c == 0:
                    read_by_now("combT", 2)
                for k2 in range(2):
                    t = 2 * c + k2
                    b = turn("shared", shared_out(c, k2))
                    MM(bank(b, D, P), combT[:, t * P:t * P + P], b2_s[:, :], start=True, stop=False)
                    for k in range(DSH // 128):
                        i = MM(bank(b, D, P), hsT[:, c % 2, k, k2 * P:k2 * P + P], Ws2_s[:, k, :], start=False, stop=k == DSH // 128 - 1)
                    i.then_inc(filled, 1)

            for c in range(5):
                for g in range(4):
                    b = turn("shared", shared_hid(c, g))
                    for k2 in range(2):
                        for k in range(KD):
                            i = MM(bank(b, 250, 128, 250 * k2), Ws1_s[:, k, (2 * g + k2) * 128:(2 * g + k2 + 1) * 128],
                                   hT[:, k, c * 250:c * 250 + 250], start=k == 0, stop=k == KD - 1)
                    i.then_inc(filled, 1)
                if c:
                    shared_rows(c - 1)
            shared_rows(4)
            for i in range(RING):
                read_by_now("shared", len(TURNS.who[TURNS.first["shared"]:TURNS.first["fT"]]) - 1 - i)
            R = pe.value_load(rounds[0:1, 0:1], min_val=1, max_val=RANKS // B)

            def transposes(r, g, u):
                n = E * r + U * g + u
                pe.wait_ge(zg_in[u], 16 * ((GROUPS + 1) * r + g + 1))
                at_least(pe, tr_read, n - 1)
                for k in range(KD):
                    i = nc.tensor.transpose(bank(u % 2, B, 128, k * B), Zg[:, u, k:D:KD], ident[:, :])
                i.then_inc(tr_done, 1)

            def hidden(r, g, u):
                n = E * r + U * g + u
                pe.wait_ge(tr_read, n + 1)
                pe.wait_ge(w_in[u], 32 * (GROUPS * r + g + 1))
                at_least(pe, h_read, n - 1)
                for m in range(2):
                    for k in range(KD):
                        i = MM(bank(2 + u % 2, B, 128, m * B), W1[u][:, k, m:DFF:2], hgT[:, u % 2, k, :], start=k == 0, stop=k == KD - 1)
                i.then_inc(h_done, 1)

            def result(r, g, u):
                n = E * r + U * g + u
                pe.wait_ge(h_read, n + 1)
                at_least(pe, e_read, n - 1)
                for m in range(2):
                    i = MM(bank(4 + u % 2, D), ehT[:, u % 2, m, :], W2[u][:, m, :], start=m == 0, stop=m == 1)
                i.then_inc(e_done, 1)

            def one_round(r):
                def group(g, first):
                    for u in range(U):
                        transposes(r, g, u)
                        if u:
                            hidden(r, g, u - 1)
                            if u > 1:
                                result(r, g, u - 2)
                            elif not first:
                                result(r, g - 1, U - 1)
                        elif not first:
                            hidden(r, g - 1, U - 1)
                            result(r, g - 1, U - 2)
                group(0, True)
                with pe.Fori(1, GROUPS) as g:
                    group(g, False)
                hidden(r, GROUPS - 1, U - 1)
                result(r, GROUPS - 1, U - 2)
                result(r, GROUPS - 1, U - 1)

            one_round(0)
            with pe.If(R > 1):
                with pe.Fori(1, R) as r:
                    one_round(r)
            pe.wait_ge(tr_read, R * E)
            pe.wait_ge(h_read, R * E)
            pe.wait_ge(e_read, R * E)
            for t in range(T):
                pe.wait_ge(fz_made, t + 1)
                b = turn("fT", t)
                for k in range(KD):
                    i = nc.tensor.transpose(bank(b, P, 128, k * P), fz[:, t % 2, k:D:KD], ident[0:P, 0:P])
                i.then_inc(filled, 1)
            pe.wait_ge(wf1_in, 16)
            pe.wait_ge(wf2_in, 16)
            for c, (o, n) in enumerate(CHUNKS):
                read_by_now("fT", min(T - 1, (o + n) // P - 1))
                for m in range(2):
                    b = turn("f1", 2 * c + m)
                    for k in range(KD):
                        i = MM(bank(b, n), Wf1_s[:, k, m:DFF:2], fT[:, k, o:o + n], start=k == 0, stop=k == KD - 1)
                    i.then_inc(filled, 1)
            for t in range(T):
                read_by_now("f1", 2 * min(2, t // 4) + 1)
                b = turn("f2", t)
                for k in range(2):
                    i = MM(bank(b, D, P), f1T[:, k, t * P:t * P + P], Wf2_s[:, k, :], start=k == 0, stop=k == 1)
                i.then_inc(filled, 1)


def shared_hid(c, i):
    return i if c == 0 else 4 + 6 * (c - 1) + i


def shared_out(c, k):
    return 4 + 6 * c + 4 + k if c < 4 else 4 + 6 * 4 + k


def kernel(**inputs):
    import concourse.bacc as bacc
    from concourse.bass_utils import run_bass_kernel_spmd

    g = {k: np.asarray(a) for k, a in inputs.items()}

    def pk(a, k):
        return a.reshape(128, k)

    def kp(a):
        return a.reshape(-1, 128).T

    cols = np.concatenate([
        kp(g["L0_mix_bq"]), kp(g["L0_gnn_bq"]), kp(g["L0_gnn_bk"]), pk(g["L0_gnn_ba"], 4), kp(g["L0_ffn_bs1"]),
        pk(g["L0_ffn_bf1"], 2), pk(g["L0_ffn_ln1_g"], 4), pk(g["L0_ffn_ln1_b"], 4), pk(g["L0_ffn_ffln_g"], 4),
        pk(g["L0_ffn_ffln_b"], 4), g["L0_ffn_b1"].reshape(E, 128, 2).transpose(1, 0, 2).reshape(128, 2 * E)], axis=1)
    gbv = np.zeros(D, np.float32)
    gbv[:HEADS * DK] = g["L0_gnn_bv"]
    rows = np.stack([g["L0_mix_bk"], g["L0_mix_bv"], g["L0_mix_bo"], g["L0_gnn_bf"], g["L0_ffn_bs2"], g["L0_ffn_bf2"], gbv])
    arrays = {
        "x": g["x"], "cols": cols, "rows": rows,
        "src": g["src"].reshape(EC, P).T, "dst": g["dst"].reshape(EC, P).T,
        "mWqT": g["L0_mix_Wq"].T, "mWkT": g["L0_mix_Wk"].T, "mWvT": g["L0_mix_Wv"].T, "mWoT": g["L0_mix_Wo"].T,
        "gWq": g["L0_gnn_Wq"], "gWk": g["L0_gnn_Wk"], "gWv": g["L0_gnn_Wv"], "Wa": g["L0_gnn_Wa"], "Wf": g["L0_gnn_Wf"],
        "Wr": g["L0_ffn_Wr"], "cbT": g["L0_ffn_codebook"].T, "W1": g["L0_ffn_W1"], "W2": g["L0_ffn_W2"],
        "b2": g["L0_ffn_b2"], "Ws1": g["L0_ffn_Ws1"], "Ws2": g["L0_ffn_Ws2"], "Wf1": g["L0_ffn_Wf1"], "Wf2": g["L0_ffn_Wf2"],
    }
    arrays = {f"in_{k}": np.ascontiguousarray(a) for k, a in arrays.items()}
    nc = bacc.Bacc("TRN2", target_bir_lowering=False, num_devices=1)
    A = {k[3:]: nc.dram_tensor(k, a.shape, mybir.dt.from_np(a.dtype), kind="ExternalInput").ap() for k, a in arrays.items()}
    out = nc.dram_tensor("out_dram", (N, D), F32, kind="ExternalOutput").ap()
    block_kernel(nc, A, out)
    r = run_bass_kernel_spmd(nc, [arrays], core_ids=[0])
    return r.results[0]["out_dram"]
```

```python
from contextlib import ExitStack

import numpy as np
import concourse.bass as bass
from concourse import mybir

F32 = mybir.dt.float32
F32R = mybir.dt.float32r
BF16 = mybir.dt.bfloat16
F16 = mybir.dt.float16
I32 = mybir.dt.int32
U32 = mybir.dt.uint32
ALU = mybir.AluOpType
ACT = mybir.ActivationFunctionType
AX = mybir.AxisListType

N, D, P = 1250, 512, 125
T = N // P
KD = D // 128
EDGES = 40000
EC = EDGES // P
EG = 4
HEADS, DK = 8, 32
E, TOPK, DFF, DSH = 64, 2, 256, 1024
B = 128
RANKS = -(-N // B) * B
U = 4
GROUPS = E // U
NOBODY = 1 << 20
RING = 6
CHUNKS = [(0, 500), (500, 500), (1000, 250)]
BANKED = [(0, 512), (512, 512), (1024, 226)]
NQ = 1280
HALF, PIECE = NQ // 2, NQ // 4
TINY = 1.2e-38

COLS = {}
for _name, _n in (("mbq", 4), ("gbq", 2), ("gbk", 2), ("ba", 4), ("bs1", 8), ("bf1", 2), ("g1", 4),
                  ("b1ln", 4), ("gf", 4), ("bfln", 4), ("eb1", 2 * E)):
    COLS[_name] = (sum(n for _, n in COLS.values()), _n)
NCOLS = sum(n for _, n in COLS.values())
ROWS = {"mbk": 0, "mbv": 1, "mbo": 2, "gbf": 3, "bs2": 4, "bf2": 5, "gbv": 6}


class Turns:

    def __init__(self, plan):
        self.first, self.who = {}, []
        for name, consumers in plan:
            self.first[name] = len(self.who)
            self.who += consumers

    def bank(self, name, i):
        return (self.first[name] + i) % RING

    def filled(self, name, i):
        return self.first[name] + i + 1

    def read(self, g):
        return self.who[g], self.who[:g + 1].count(self.who[g])

    def group_read(self, name, i):
        return self.read(self.first[name] + i)


TURNS = Turns([
    ("xnT", ["act", "dve"] * 5),
    ("mix_q", ["act"] * 12),
    ("mix_kv", ["dve"] * 20),
    ("mix_o", ["dve"] * 24),
    ("mix_wo", ["dve"] * 10),
    ("gnn_qk", ["act"] * 12),
    ("gnn_v", ["dve"] * 10),
    ("gnn_a", ["act"] * 12),
    ("gnn_f", ["dve"] * 10),
    ("hT", ["act"] * 10),
    ("rT", ["act"] * 3),
    ("logit", ["dve"] * 2),
    ("rank", ["dve"] * 3),
    ("combT", ["act"] * 3),
    ("shared", (["act"] * 4) + (["act"] * 4 + ["dve"] * 2) * 4 + ["dve"] * 2),
    ("fT", ["act"] * 10),
    ("f1", ["act"] * 6),
    ("f2", ["dve"] * 10),
])


def at_least(eng, sem, value):
    if not isinstance(value, int) or value > 0:
        eng.wait_ge(sem, value)


def block_kernel(nc, A, out):
    ctx = ExitStack()
    with ctx:
        KB = 1024
        base = nc.sbuf_base + (-nc.sbuf_base) % 64

        def at(name, shape, dt, offset):
            return nc.alloc_sbuf_tensor_at(name, shape, dt, offset=base + int(offset))

        def sem(name):
            return ctx.enter_context(nc.semaphore(name))

        fixed = [0]

        def keep(name, shape, dt):
            size = int(np.prod(shape[1:])) * mybir.dt.size(dt)
            off = fixed[0]
            fixed[0] += size + (-size) % 64
            return at(name, shape, dt, off)

        ident = keep("ident", [128, 128], F32)
        cols = keep("cols", [128, NCOLS], F32)
        rows = keep("rows", [128, len(ROWS), D], F32)
        XR = keep("XR", [P, T, D], F32)
        st = keep("st", [P, T, 6], F32)
        mv = keep("mv", [P, T, 2], F32)
        mv2 = keep("mv2", [P, T, 2], F32)
        rs = keep("rs", [P, T], F32)
        eps = keep("eps", [P, 1], F32)
        Wr_s = keep("Wr_s", [128, KD, E], F32)
        cbT_s = keep("cbT_s", [E, E], F32)
        b2_s = keep("b2_s", [E, D], F32)
        spare = keep("spare", [1, 1], F32)
        tiny = keep("tiny", [128, 1], F32)
        counted = keep("counted", [1, 2], F32)
        wtop = keep("wtop", [P, T, TOPK], F32)
        idxg = keep("idxg", [128, U, 1], U32)
        idxs = keep("idxs", [128, U, 1], U32)
        lst = keep("lst", [128, E + U], U32)
        gat = keep("gat", [128, E + U], U32)
        carry = keep("carry", [1, 3, 1], F32)
        rounds = keep("rounds", [1, 1], I32)
        ranges = keep("ranges", [T, 2], I32)
        zeros = keep("zeros", [1, 640], BF16)
        fixed[0] += (-fixed[0]) % 64
        W1 = [keep(f"W1_{u}", [128, KD, DFF], F32) for u in range(U)]
        W2 = [keep(f"W2_{u}", [128, 2, D], F32) for u in range(U)]
        G = fixed[0]

        def ph(name, shape, dt, kb):
            return at(name, shape, dt, G + kb * KB)

        xs = ph("xs", [P, T, D], F32, 0)
        xn = ph("xn", [P, T, D], F32, 20)
        xnT = ph("xnT", [128, KD, N], F32, 40)
        mW = ph("mW", [128, 3, KD, D], F32, 60)
        mWo = ph("mWo", [128, KD, D], F32, 84)
        gW = ph("gW", [128, 3, KD, HEADS * DK], F32, 92)
        qT = ph("qT", [128, KD, N], F32, 104)
        eq = ph("eq", [128, 2, 500], F32, 124)
        rq = ph("rq", [128, 2, 500], F32, 128)
        tk = ph("tk", [P, 2, D], F32, 124)
        ek = ph("ek", [P, 2, D], F32, 128)
        kf = ph("kf", [P, 2, D], F32, 34)
        vt = ph("vt", [P, 2, KD, 129], F32, 20)
        kvb = ph("kvb", [128, KD, 128], F32, 26)
        ksb = ph("ksb", [128, KD, 128], F32, 28)
        zt = ph("zt", [128, 2, 500], F32, 30)
        moT = ph("moT", [128, KD, N], F32, 0)
        fqk = ph("fqk", [128, 2, N], F32, 60)
        qk_hi = ph("qk_hi", [128, 2, N], F32R, 20)
        qk_lo = ph("qk_lo", [128, 2, N], F32R, 30)
        V = ph("V", [P, T, HEADS // 2, 3, DK], F32, 119.25)

        C = ph("C", [P, T, NQ], F32, 40)
        Wa_s = ph("Wa_s", [128, 2, D], F32, 20)
        Wf_s = ph("Wf_s", [128, KD, D], F32, 0)
        ohB = ph("ohB", [P, EG, N], BF16, 104)
        ohA = ph("ohA", [P, EG, P], BF16, 103)
        iota = ph("iota", [P, N], F16, 114.25)
        e_i = ph("e_i", [P, 2, EC], I32, 104)
        e_f = ph("e_f", [P, 2, EC], F32, 116.75)
        neg = ph("neg", [P, EC], F32, 86.5)
        cmx = ph("cmx", [P, 2, EC], F32, 84)
        ov = ph("ov", [T, 3, EC], F32, 104)
        gi = ph("gi", [T, 2, EC], F32, 108)
        lim = ph("lim", [T, 8], F32, 111)
        dA = ph("dA", [P, EG, P], F16, 92)
        sqA = ph("sqA", [P, EG, P], F32, 93)
        att = ph("att", [P, 4, 2, PIECE], F32, 104)
        rden = ph("rden", [128, 2, PIECE], F32, 114)
        Kst = ph("Kst", [128, 4, N], F32R, 0)
        Qst = ph("Qst", [128, 4, NQ], F32R, 20)
        aggT = ph("aggT", [128, 2, NQ], F32, 92)
        h1T = ph("h1T", [128, KD, N], F32, 40)
        tf = ph("tf", [P, 2, D], F32, 30)

        yz = ph("yz", [P, T, D], F32, 102)
        HM = ph("HM", [P, T, D], F32, 20)
        hT = ph("hT", [128, KD, N], F32, 60)
        Ws1_s = ph("Ws1_s", [128, KD, DSH], F32, 80)
        Ws2_s = ph("Ws2_s", [128, DSH // 128, D], F32, 0)
        hsT = ph("hsT", [128, 2, DSH // 128, 250], F32, 96)
        Wf1_s = ph("Wf1_s", [128, KD, DFF], F32, 16)
        Wf2_s = ph("Wf2_s", [128, 2, D], F32, 112)
        rTs = ph("rTs", [E, N], F32, 96)
        prob = ph("prob", [P, T, E], F32, 40)
        M1 = ph("M1", [P, T, E], F32, 42.5)
        M2 = ph("M2", [P, T, E], F32, 45)
        Mb = ph("Mb", [P, T, E], BF16, 47.5)
        tmpr = ph("tmpr", [P, T, E], F32, 49)
        rankS = ph("rankS", [P, T, E], F32, 51.5)
        combT = ph("combT", [E, N], F32, 54)
        iotaE = ph("iotaE", [P, E], F32, 130)
        iotaE_i = ph("iotaE_i", [P, E], I32, 130.5)
        sm = ph("sm", [P, 16, T], F32, 124)
        top8 = ph("top8", [P, T, 8], F32, 124.75)
        idx8 = ph("idx8", [P, T, 8], U32, 125.25)
        posf = ph("posf", [P, TOPK, T], F32, 125.75)
        posi = ph("posi", [P, TOPK, T], U32, 126)
        toki = ph("toki", [P, TOPK, T], U32, 126.25)
        ltri = ph("ltri", [P, P], BF16, 126.5)
        ones = ph("ones", [P, P], BF16, 126.75)
        nobody = ph("nobody", [128, RANKS * E // 128], U32, 127)
        Zg = ph("Zg", [128, U, D], F32, 116)
        hgT = ph("hgT", [128, 2, KD, B], F32, 124)
        ehT = ph("ehT", [128, 2, 2, B], F32, 128)
        eo = ph("eo", [128, U, D], F32, 40)
        Yt = ph("Yt", [P, 2, TOPK, D], F32, 80)
        fz = ph("fz", [P, 2, D], F32, 88)
        fT = ph("fT", [128, KD, N], F32, 60)
        f1T = ph("f1T", [128, 2, N], F32, 96)
        outS = ph("outS", [P, 2, D], F32, 92)

        ps = ctx.enter_context(nc.psum_tensor("ps", [128, 8 * 512], F32))

        def bank(b, n, p=128, off=0):
            return ps[0:p, b * 512 + off:b * 512 + off + n]

        def scores_of(n):
            return ps[0:P, (n % 2) * 1024:(n % 2) * 1024 + 1024].rearrange("p (a n) -> p a n", a=2)[:, :, 0:PIECE]

        def sums_of(i, p0, n):
            o = 2048 + (i % 2) * 1024
            return ps[p0:p0 + n, o:o + 1024].rearrange("p (a n) -> p a n", a=2)[:, :, 0:PIECE]

        qk_d = nc.dram_tensor("qk_d", [2, 2, 2 * 128, N], F32, kind="Internal").ap()
        z_d = nc.dram_tensor("z_d", [N, D], F32, kind="Internal").ap()
        y_d = nc.dram_tensor("y_d", [N * TOPK, D], F32, kind="Internal").ap()
        list_d = nc.dram_tensor("list_d", [RANKS * E, 1], U32, kind="Internal").ap()

        x_in = [sem(f"x_in{i}") for i in range(2)]
        edges_in, cols_in, rows_in = sem("edges_in"), sem("cols_in"), sem("rows_in")
        mw_in, mwo_in, gw_in = sem("mw_in"), sem("mwo_in"), sem("gw_in")
        waf_in, small_in = sem("waf_in"), sem("small_in")
        ws1_in, ws2_in, wf1_in, wf2_in = sem("ws1_in"), sem("ws2_in"), sem("wf1_in"), sem("wf2_in")
        st_in = [sem(f"st_in{i}") for i in range(4)]
        w_in = [sem(f"w_in{u}") for u in range(U)]
        consts = sem("consts")
        filled = sem("filled")
        act_read, dve_read = sem("act_read"), sem("dve_read")
        ln_var, ln_std = sem("ln_var"), sem("ln_std")
        xn_made, xr_made = sem("xn_made"), sem("xr_made")
        feat_q = sem("feat_q")
        qT_made = sem("qT_made")
        tk_made, ek_made, kf_made = sem("tk_made"), sem("ek_made"), sem("kf_made")
        kv_summed, kvb_made = sem("kv_summed"), sem("kvb_made")
        kv_used = sem("kv_used")
        split_made = sem("split_made")
        qk_out = [sem(f"qk_out{i}") for i in range(4)]
        cmax_made, range_made = sem("cmax_made"), sem("range_made")
        edges_f = sem("edges_f")
        oh_made = [sem(f"oh_made{b}") for b in range(T)]
        oh_used = [sem(f"oh_used{b}") for b in range(T)]
        dA_made = [sem(f"dA_made{b}") for b in range(T)]
        dA_used = [sem(f"dA_used{b}") for b in range(T)]
        ohA_made = [sem(f"ohA_made{b}") for b in range(T)]
        c_sum, c_kept, pads_made = sem("c_sum"), sem("c_kept"), sem("pads_made")
        s_made, s_exp, att_made, att_used = sem("s_made"), sem("s_exp"), sem("att_made"), sem("att_used")
        head_sum, head_kept, den_kept, rden_used = sem("head_sum"), sem("head_kept"), sem("den_kept"), sem("rden_used")
        idx_made = sem("idx_made")
        st_used = sem("st_used")
        y_made, z_made, z_out = sem("y_made"), sem("z_made"), sem("z_out")
        lmax_made, prob_exp, m_made = sem("lmax_made"), sem("prob_exp"), sem("m_made")
        comb_made, pos_made, list_clear, list_made = (sem("comb_made"), sem("pos_made"),
                                                      sem("list_clear"), sem("list_made"))
        round_made, lst_in, gat_made = sem("round_made"), sem("lst_in"), sem("gat_made")
        zg_in = [sem(f"zg_in{u}") for u in range(U)]
        tr_done, tr_read, h_done, h_read = sem("tr_done"), sem("tr_read"), sem("h_done"), sem("h_read")
        e_done, e_read = sem("e_done"), sem("e_read")
        y_out = [sem(f"y_out{u}") for u in range(U)]
        yt_in = [sem(f"yt_in{i}") for i in range(2)]
        yt_used, fz_made = sem("yt_used"), sem("fz_made")
        out_made = sem("out_made")
        out_sent = [sem(f"out_sent{i}") for i in range(2)]
        blk = ctx.enter_context(nc.Block())

        def col(name, i, n=1, p=128):
            o = COLS[name][0] + i
            return cols[0:p, o:o + n]

        def row(name, n=D):
            return rows[0:P, ROWS[name], 0:n]

        def in_range(group):
            return nc.s_assert_within(group, 0, EC // EG - 1, skip_runtime_bounds_check_because=
                                      "first group + count is at most the number of groups, as made on VectorE")

        @blk.sync
        def _(sp):
            x_v = A["x"].rearrange("(t p) d -> p t d", p=P)
            for i in range(2):
                sp.dma_start(xs[:, 5 * i:5 * i + 5, :], x_v[:, 5 * i:5 * i + 5, :]).then_inc(x_in[i], 16)
            sp.dma_start(cols[:, :], A["cols"]).then_inc(cols_in, 16)
            for j, w in enumerate(("mWqT", "mWkT", "mWvT")):
                sp.dma_start(mW[:, j], A[w].rearrange("(p k) n -> p k n", k=KD)).then_inc(mw_in, 16)
            for name, j in ROWS.items():
                sp.dma_start(rows[:, j, :], A["rows"][j:j + 1, :].partition_broadcast(128)).then_inc(rows_in, 16)
            sp.dma_start(mWo[:, :, :], A["mWoT"].rearrange("(k p) n -> p k n", p=128)).then_inc(mwo_in, 16)
            for j, w in enumerate(("gWq", "gWk", "gWv")):
                sp.dma_start(gW[:, j], A[w].rearrange("(p k) n -> p k n", k=KD)).then_inc(gw_in, 16)
            sp.dma_start(Wr_s[:, :, :], A["Wr"].rearrange("(p k) n -> p k n", k=KD)).then_inc(small_in, 16)
            sp.dma_start(cbT_s[:, :], A["cbT"]).then_inc(small_in, 16)
            sp.dma_start(b2_s[:, :], A["b2"]).then_inc(small_in, 16)

            def weights(e, u, static=False):
                w1 = A["W1"] if static else A["W1"]
                sp.dma_start(W1[u][:, :, :], w1[bass.ds(e, 1)].rearrange("e (p k) f -> p (e k) f", k=KD)).then_inc(w_in[u], 16)
                sp.dma_start(W2[u][:, :, :], A["W2"][bass.ds(e, 1)].rearrange("e (p m) n -> p (e m) n", m=2)).then_inc(w_in[u], 16)

            for u in range(U):
                weights(u, u)
            sp.wait_ge(filled, TURNS.filled("mix_o", 23))
            for j, w in enumerate(("src", "dst")):
                sp.dma_start(e_i[:, j, :], A[w]).then_inc(edges_in, 16)
            for i in range(4):
                sp.wait_ge(qk_out[i], 32)
            for h in range(HEADS):
                if h >= 4:
                    sp.wait_ge(st_used, h // 2 - 1)
                for j in range(4):
                    d = h * DK
                    sp.dma_start(Kst[32 * j:32 * j + 32, h % 4, :].bitcast(F32), qk_d[1, j // 2, d:d + DK, :]).then_inc(st_in[h % 4], 16)
                    sp.dma_start(Qst[32 * j:32 * j + 32, h % 4, 0:N].bitcast(F32), qk_d[0, j % 2, d:d + DK, :]).then_inc(st_in[h % 4], 16)
            sp.wait_ge(st_used, 3)
            sp.dma_start(Wa_s[:, :, :], A["Wa"].rearrange("(k p) n -> p k n", p=128)).then_inc(waf_in, 16)
            sp.dma_start(Wf_s[:, :, :], A["Wf"].rearrange("(p k) n -> p k n", k=KD)).then_inc(waf_in, 16)
            sp.wait_ge(filled, TURNS.filled("gnn_f", 9))
            sp.dma_start(Ws2_s[:, :, :], A["Ws2"].rearrange("(k p) n -> p k n", p=128)).then_inc(ws2_in, 16)
            sp.dma_start(Wf1_s[:, :, :], A["Wf1"].rearrange("(p k) n -> p k n", k=KD)).then_inc(wf1_in, 16)
            sp.dma_start(Ws1_s[:, :, :], A["Ws1"].rearrange("(p k) n -> p k n", k=KD)).then_inc(ws1_in, 16)
            with sp.Fori(1, GROUPS) as g:
                for u in range(U):
                    sp.wait_ge(e_done, U * g + u - U + 1)
                    weights(U * g + u, u)
            sp.wait_ge(round_made, 1)
            R = sp.value_load(rounds[0:1, 0:1], min_val=1, max_val=RANKS // B)
            with sp.If(R > 1):
                with sp.Fori(1, R) as r:
                    with sp.Fori(0, GROUPS) as g:
                        for u in range(U):
                            sp.wait_ge(e_done, E * r + U * g + u - U + 1)
                            weights(U * g + u, u)
            sp.dma_start(Wf2_s[:, :, :], A["Wf2"].rearrange("(p k) n -> p k n", k=2)).then_inc(wf2_in, 16)
            for u in range(U):
                sp.wait_ge(y_out[u], R * (16 * GROUPS))
            y_v = y_d.rearrange("(t p k) d -> t p k d", p=P, k=TOPK)
            for t in range(T):
                if t >= 2:
                    sp.wait_ge(yt_used, t - 1)
                sp.dma_start(Yt[:, t % 2], y_v[t]).then_inc(yt_in[t % 2], 16)
            o_v = out.rearrange("(t p) d -> t p d", p=P)
            for t in range(T):
                sp.wait_ge(out_made, t + 1)
                sp.dma_start(o_v[t], outS[:, t % 2, :]).then_inc(out_sent[t % 2], 16)
            for i in range(2):
                sp.wait_ge(out_sent[i], 16 * (T // 2))

        @blk.gpsimd
        def _(gp):
            nc.gpsimd.memset(ident[:, :], 0.0)
            nc.gpsimd.memset(eps[:, :], 1e-5)
            nc.gpsimd.memset(tiny[:, :], TINY)
            nc.gpsimd.memset(zeros[:, :], 0.0)
            gp.drain()
            nc.gpsimd.affine_select(out=ident[:, :], in_=ident[:, :], compare_op=ALU.not_equal, fill=1.0,
                                    base=0, pattern=[[-1, 128]], channel_multiplier=1)
            gp.drain().then_inc(consts, 1)
            gp.wait_ge(rows_in, 16 * len(ROWS))
            for t in range(T):
                gp.wait_ge(xn_made, t + 1)
                nc.gpsimd.tensor_tensor(XR[:, t, :], xs[:, t, :], xn[:, t, :], ALU.add)
            gp.drain()
            for t in range(T):
                nc.gpsimd.tensor_tensor(XR[:, t, :], XR[:, t, :], row("mbo"), ALU.add)
            gp.drain().then_inc(xr_made, 1)
            gp.wait_ge(act_read, TURNS.group_read("xnT", 8)[1])
            gp.wait_ge(dve_read, TURNS.group_read("xnT", 9)[1])
            nc.gpsimd.memset(vt[:, :, :, 128:129], 1.0)
            gp.drain().then_inc(consts, 1)
            gp.wait_ge(filled, TURNS.filled("mix_o", 23))
            nc.gpsimd.iota(gi[:, 0, :], pattern=[[1, EC // EG], [0, EG]], base=1, channel_multiplier=0,
                           allow_small_or_imprecise_dtypes=True)
            nc.gpsimd.iota(gi[:, 1, :], pattern=[[-1, EC // EG], [0, EG]], base=EC // EG, channel_multiplier=0,
                           allow_small_or_imprecise_dtypes=True)
            nc.gpsimd.iota(lim[:, 0:1], pattern=[[0, 1]], base=0, channel_multiplier=P,
                           allow_small_or_imprecise_dtypes=True)
            nc.gpsimd.iota(lim[:, 1:2], pattern=[[0, 1]], base=-P, channel_multiplier=-P,
                           allow_small_or_imprecise_dtypes=True)
            nc.gpsimd.iota(iota[:, :], pattern=[[1, N]], base=0, channel_multiplier=0,
                           allow_small_or_imprecise_dtypes=True)
            gp.wait_ge(edges_f, 1)
            nc.gpsimd.partition_all_reduce(cmx[:, 0, :], e_f[:, 1, :], P, bass.bass_isa.ReduceOp.max)
            nc.gpsimd.partition_all_reduce(cmx[:, 1, :], neg[:, :], P, bass.bass_isa.ReduceOp.max)
            gp.drain().then_inc(cmax_made, 1)
            gp.drain().then_inc(consts, 1)
            for i in range(4):
                gp.wait_ge(split_made, i + 1)
                w, m = i // 2, i % 2
                gp.dma_start(qk_d[w, 0, 128 * m:128 * m + 128, :], qk_hi[:, i % 2, :].bitcast(F32)).then_inc(qk_out[i], 16)
                gp.dma_start(qk_d[w, 1, 128 * m:128 * m + 128, :], qk_lo[:, i % 2, :].bitcast(F32)).then_inc(qk_out[i], 16)
            gp.wait_ge(range_made, 1)
            at_range = [(gp.value_load(ranges[b:b + 1, 0:1], min_val=0, max_val=EC // EG - 1),
                         gp.value_load(ranges[b:b + 1, 1:2], min_val=1, max_val=EC // EG)) for b in range(T)]
            for b, (lo_b, n_b) in enumerate(at_range):
                with gp.Fori(0, n_b) as g:
                    grp = in_range(lo_b + g)
                    gp.wait_ge(dA_used[b], g + 1)
                    nc.gpsimd.tensor_tensor(dA[:, :, :], iota[:, b * P:b * P + P].unsqueeze(1).to_broadcast([P, EG, P]),
                                            e_f[:, 1, bass.ds(grp * EG, EG)].unsqueeze(2).to_broadcast([P, EG, P]),
                                            ALU.subtract).then_inc(dA_made[b], 1)
            for i in range(4):
                gp.wait_ge(qk_out[i], 32)
            nc.gpsimd.memset(C[:, :, N:NQ], 0.0)
            nc.gpsimd.memset(Qst[:, :, N:NQ].bitcast(F32), 0.0)
            gp.drain().then_inc(pads_made, 1)
            z_v = z_d.rearrange("(t p) d -> t p d", p=P)
            gp.wait_ge(filled, TURNS.filled("gnn_f", 9))
            for t in range(T):
                gp.wait_ge(y_made, t + 1)
                nc.gpsimd.tensor_tensor(XR[:, t, :], XR[:, t, :], yz[:, t, :], ALU.add)
            gp.drain().then_inc(xr_made, 1)
            for t in range(T):
                gp.wait_ge(z_made, t + 1)
                gp.dma_start(z_v[t], yz[:, t, :]).then_inc(z_out, 16)
            nc.gpsimd.iota(iotaE_i[:, :], pattern=[[1, E]], base=0, channel_multiplier=0)
            gp.wait_ge(z_out, 16 * T)
            gp.wait_ge(act_read, TURNS.group_read("hT", 9)[1])
            nc.gpsimd.iota(toki[:, :, :], pattern=[[1, TOPK], [TOPK * P, T]], base=0, channel_multiplier=TOPK)
            nc.gpsimd.memset(nobody[:, :], NOBODY)
            nc.gpsimd.memset(lst[:, :], NOBODY)
            nc.gpsimd.memset(ones[:, :], 1.0)
            gp.drain()
            nc.gpsimd.tensor_copy(iotaE[:, :], iotaE_i[:, :])
            nc.gpsimd.affine_select(out=ltri[:, :], in_=ones[:, :], compare_op=ALU.is_gt, fill=0.0,
                                    base=0, pattern=[[1, P]], channel_multiplier=-1)
            gp.drain().then_inc(consts, 1)
            gp.dma_start(list_d.rearrange("(p n) o -> p (n o)", p=128), nobody[:, :]).then_inc(list_clear, 16)
            gp.wait_ge(list_clear, 16)
            gp.wait_ge(pos_made, 1)
            for k in range(TOPK):
                for t in range(T):
                    gp.indirect_dma_start(
                        out=list_d, out_offset=bass.IndirectOffsetOnAxis(ap=posi[:, k, t:t + 1], axis=0),
                        in_=toki[:, k, t:t + 1], in_offset=None).then_inc(list_made, 16)
            gp.wait_ge(list_made, 16 * TOPK * T)
            gp.wait_ge(dve_read, TURNS.group_read("rank", 2)[1])
            nc.gpsimd.memset(Zg[:, :, :], 0.0)
            gp.drain()
            gp.wait_ge(round_made, 1)
            R = gp.value_load(rounds[0:1, 0:1], min_val=1, max_val=RANKS // B)

            def wait_alone(s, value, j=0):
                gp.wait_ge(s, value)
                nc.gpsimd.tensor_tensor(carry[:, j, :], eps[0:1, :], eps[0:1, :], ALU.add)

            def rows_of(u):
                gp.indirect_dma_start(out=Zg[:, u, :], out_offset=None, in_=z_d,
                                      in_offset=bass.IndirectOffsetOnAxis(ap=idxg[:, u, :], axis=0),
                                      bounds_check=N - 1, oob_is_err=False).then_inc(zg_in[u], 16)

            def one_round(r):
                gp.dma_start(lst[:, 0:E], list_d.rearrange("(r p e) o -> r p (e o)", p=B, e=E)[bass.ds(r, 1)]
                             .rearrange("r p e -> (r p) e")).then_inc(lst_in, 16)
                wait_alone(gat_made, r + 1)
                for u in range(U):
                    nc.gpsimd.tensor_copy(idxg[:, u, :], gat[:, u:u + 1])
                gp.drain()
                for u in range(U):
                    rows_of(u)

                def group(g):
                    for u in range(U):
                        n = E * r + U * g + u
                        wait_alone(e_read, n + 1)
                        if not (isinstance(g, int) and isinstance(r, int)):
                            wait_alone(y_out[u], (GROUPS * r + g) * 16, 1)
                        nc.gpsimd.tensor_copy(idxs[:, u, :], lst[:, bass.ds(U * g + u, 1)])
                        nc.gpsimd.tensor_copy(idxg[:, u, :], gat[:, bass.ds(U * g + u + U, 1)]).then_inc(idx_made, 1)
                        wait_alone(idx_made, n + 1, 2)
                        gp.indirect_dma_start(out=y_d, out_offset=bass.IndirectOffsetOnAxis(ap=idxs[:, u, :], axis=0),
                                              in_=eo[:, u, :], in_offset=None,
                                              bounds_check=N * TOPK - 1, oob_is_err=False).then_inc(y_out[u], 16)
                        rows_of(u)
                group(0)
                with gp.Fori(1, GROUPS) as g:
                    group(g)

            one_round(0)
            with gp.If(R > 1):
                with gp.Fori(1, R) as r:
                    one_round(r)
            for u in range(U):
                wait_alone(zg_in[u], R * (16 * (GROUPS + 1)))
                gp.drain()

        @blk.vector
        def _(v):
            V_ = nc.vector

            def reads(name, i):
                v.wait_ge(filled, TURNS.filled(name, i))

            def stats(src, mvt, tiles):
                for t in tiles:
                    V_.bn_stats(st[:, t, :], src[:, t, :])
                v.drain()
                for t in tiles:
                    V_.bn_aggr(mvt[:, t, :], st[:, t, :])
                v.drain().then_inc(ln_var, 1)

            def inverse_std(count):
                v.wait_ge(ln_std, count)
                V_.reciprocal(rs[:, :], rs[:, :])
                v.drain()

            def normalise(dst, src, mvt, t):
                return V_.tensor_scalar(dst, src, mvt[:, t, 0:1], rs[:, t:t + 1], ALU.subtract, ALU.mult)

            v.wait_ge(x_in[0], 16)
            v.wait_ge(x_in[1], 16)
            v.wait_ge(consts, 1)
            stats(xs, mv, range(T))
            inverse_std(1)
            for t in range(T):
                normalise(xn[:, t, :], xs[:, t, :], mv, t).then_inc(xn_made, 1)
            for t in range(1, T, 2):
                reads("xnT", t)
                V_.tensor_copy(xnT[:, :, t * P:t * P + P],
                               bank(TURNS.bank("xnT", t), 4 * P).rearrange("p (k n) -> p k n", k=4)).then_inc(dve_read, 1)
            for m in range(KD):
                for c, (o, n) in enumerate(CHUNKS):
                    i = 3 * m + c
                    v.wait_ge(feat_q, i + 1)
                    V_.scalar_tensor_tensor(qT[:, m, o:o + n], eq[:, i % 2, 0:n], 1.0, rq[:, i % 2, 0:n],
                                            ALU.min, ALU.add).then_inc(qT_made, 1)
            v.wait_ge(rows_in, 16 * len(ROWS))
            v.wait_ge(consts, 2)
            v.drain()
            for t in range(T):
                reads("mix_kv", 2 * t)
                V_.tensor_tensor(tk[:, t % 2, :], bank(TURNS.bank("mix_kv", 2 * t), D, P), row("mbk"), ALU.add).then_inc(dve_read, 1)
                v.drain().then_inc(tk_made, 1)
                if t >= 2:
                    v.wait_ge(kv_used, t - 1)
                V_.tensor_scalar(kf[:, t % 2, :], tk[:, t % 2, :], 0.0, None, ALU.max)
                reads("mix_kv", 2 * t + 1)
                V_.tensor_tensor(vt[:, t % 2, :, 0:128], bank(TURNS.bank("mix_kv", 2 * t + 1), D, P).rearrange("p (k n) -> p k n", k=KD),
                                 row("mbv").rearrange("p (k n) -> p k n", k=KD), ALU.add).then_inc(dve_read, 1)
                v.wait_ge(ek_made, t + 1)
                v.drain()
                V_.scalar_tensor_tensor(kf[:, t % 2, :], ek[:, t % 2, :], 1.0, kf[:, t % 2, :], ALU.min, ALU.add)
                v.drain().then_inc(kf_made, 1)
            V_.memset(kvb[:, :, :], 0.0)
            V_.memset(ksb[:, :, :], 0.0)
            v.drain()
            v.wait_ge(kv_summed, 1)
            for p in range(KD):
                src = ps[:, (6 + p // 2) * 512 + (p % 2) * 129:(6 + p // 2) * 512 + (p % 2) * 129 + 129]
                for a in (0, 64):
                    V_.tensor_copy(kvb[a:a + 64, p, a:a + 64], src[a:a + 64, a:a + 64])
                    V_.tensor_copy(ksb[a:a + 64, p, a:a + 64], src[a:a + 64, 128:129].to_broadcast([64, 64]))
            v.drain().then_inc(kvb_made, 1)
            v.wait_ge(xr_made, 1)
            for i in range(12):
                p, (o, n) = i // 3, CHUNKS[i % 3]
                reads("mix_o", 2 * i)
                V_.tensor_scalar(zt[:, i % 2, 0:n], bank(TURNS.bank("mix_o", 2 * i), n), 1e-6, None, ALU.add).then_inc(dve_read, 1)
                v.drain()
                V_.reciprocal(zt[:, i % 2, 0:n], zt[:, i % 2, 0:n])
                v.drain()
                reads("mix_o", 2 * i + 1)
                V_.tensor_tensor(moT[:, p, o:o + n], bank(TURNS.bank("mix_o", 2 * i + 1), n), zt[:, i % 2, 0:n], ALU.mult).then_inc(dve_read, 1)
            for t in range(T):
                reads("mix_wo", t)
                V_.tensor_tensor(XR[:, t, :], bank(TURNS.bank("mix_wo", t), D, P), XR[:, t, :], ALU.add).then_inc(dve_read, 1)
            v.wait_ge(edges_in, 32)
            V_.tensor_copy(e_f[:, :, :], e_i[:, :, :])
            v.drain()
            V_.tensor_scalar(neg[:, :], e_f[:, 1, :], -1.0, None, ALU.mult)
            v.drain().then_inc(edges_f, 1)
            for i in range(4):
                v.wait_ge(act_read, TURNS.group_read("gnn_qk", 3 * i + 2)[1])
                if i >= 2:
                    v.wait_ge(qk_out[i - 2], 32)
                V_.tensor_copy(qk_hi[:, i % 2, :], fqk[:, i % 2, :])
                v.drain()
                V_.tensor_tensor(qk_lo[:, i % 2, :], fqk[:, i % 2, :], qk_hi[:, i % 2, :].bitcast(F32), ALU.subtract)
                v.drain().then_inc(split_made, 1)
            V_.memset(V[:, :, :, 1, :], 1.0)
            for t in range(T):
                reads("gnn_v", t)
                V_.tensor_tensor(V[:, t, :, 0:3:2, :], bank(TURNS.bank("gnn_v", t), HEADS * DK, P).rearrange("p (h j d) -> p h j d", j=2, d=DK),
                                 row("gbv", HEADS * DK).rearrange("p (h j d) -> p h j d", j=2, d=DK), ALU.add).then_inc(dve_read, 1)
            v.wait_ge(cmax_made, 1)
            v.wait_ge(consts, 3)
            lo, hi = lim[:, 2:3], lim[:, 3:4]
            V_.tensor_scalar(ov[:, 0, :], cmx[0:T, 0, :], lim[:, 0:1], None, ALU.is_ge)
            V_.tensor_scalar(ov[:, 1, :], cmx[0:T, 1, :], lim[:, 1:2], None, ALU.is_gt)
            v.drain()
            V_.tensor_tensor(ov[:, 2, :], ov[:, 0, :], ov[:, 1, :], ALU.mult)
            v.drain()
            V_.tensor_tensor(ov[:, 0, :], ov[:, 2, :], gi[:, 0, :], ALU.mult)
            V_.tensor_tensor(ov[:, 1, :], ov[:, 2, :], gi[:, 1, :], ALU.mult)
            v.drain()
            V_.tensor_reduce(hi, ov[:, 0, :], axis=AX.X, op=ALU.max)
            V_.tensor_reduce(lo, ov[:, 1, :], axis=AX.X, op=ALU.max)
            v.drain()
            V_.tensor_scalar(hi, hi, 1.0, None, ALU.max)
            V_.tensor_scalar(lo, lo, -1.0, float(EC // EG), ALU.mult, ALU.add)
            v.drain()
            V_.tensor_scalar(lim[:, 4:5], hi, -1.0, None, ALU.add)
            v.drain()
            V_.tensor_tensor(lo, lo, lim[:, 4:5], ALU.min)
            v.drain()
            V_.tensor_tensor(hi, hi, lo, ALU.subtract)
            v.drain()
            V_.tensor_copy(ranges[:, :], lim[:, 2:4])
            v.drain().then_inc(range_made, 1)
            at_range = [(v.value_load(ranges[b:b + 1, 0:1], min_val=0, max_val=EC // EG - 1),
                         v.value_load(ranges[b:b + 1, 1:2], min_val=1, max_val=EC // EG)) for b in range(T)]
            for b, (lo_b, n_b) in enumerate(at_range):
                with v.Fori(0, n_b) as g:
                    grp = in_range(lo_b + g)
                    for j in range(EG):
                        v.wait_ge(oh_used[b], g * EG + j + 1)
                        V_.tensor_scalar(ohB[:, j, :], iota[:, :], e_f[:, 0, bass.ds(grp * EG + j, 1)], None, ALU.is_equal)\
                          .then_inc(oh_made[b], 1)
            v.wait_ge(c_kept, T)
            v.wait_ge(pads_made, 1)

            def keep_heads(i):
                v.wait_ge(den_kept, i + 1)
                V_.reciprocal(rden[:, :, :], rden[:, :, :])
                v.drain()
                for j in range(2):
                    h = 2 * (i // 2) + j
                    o = (i % 2) * HALF
                    V_.scalar_tensor_tensor(aggT[32 * (h % 4):32 * (h % 4) + 32, h // 4, o:o + HALF].rearrange("p (a n) -> p a n", a=2),
                                            sums_of(i, 96 * j, 32), 0.0, rden[32 * j + 32:32 * j + 64, :, :], ALU.max, ALU.mult)
                v.drain().then_inc(head_kept, 1)

            for n in range(HEADS * 2 * T):
                i, s = divmod(n // 2, T)
                v.wait_ge(s_exp, n + 1)
                if n >= 4:
                    v.wait_ge(att_used, n // 2 - 1)
                o = (i % 2) * HALF
                V_.tensor_tensor(att[:, n % 4, :, :], scores_of(n), C[:, s, o:o + HALF].rearrange("p (a n) -> p a n", a=2), ALU.mult).then_inc(att_made, 1)
                if s == 1 and n % 2 and i >= 1:
                    keep_heads(i - 1)
            keep_heads(HEADS - 1)
            for t in range(T):
                reads("gnn_f", t)
                V_.tensor_tensor(tf[:, t % 2, :], bank(TURNS.bank("gnn_f", t), D, P), row("gbf"), ALU.add).then_inc(dve_read, 1)
                v.drain()
                V_.scalar_tensor_tensor(XR[:, t, :], tf[:, t % 2, :], 0.0, XR[:, t, :], ALU.max, ALU.add)
            v.drain()
            stats(XR, mv, range(T))
            inverse_std(2)
            for t in range(T):
                normalise(yz[:, t, :], XR[:, t, :], mv, t).then_inc(y_made, 1)
            v.drain()
            stats(yz, mv2, range(T))
            inverse_std(3)
            v.wait_ge(xr_made, 2)
            for t in range(T):
                normalise(yz[:, t, :], yz[:, t, :], mv2, t).then_inc(z_made, 1)
            V_.tensor_scalar(row("bs2"), row("bs2"), 0.25, None, ALU.mult)
            for i in range(2):
                reads("logit", i)
                V_.tensor_scalar(prob[:, 5 * i:5 * i + 5, :], bank(TURNS.bank("logit", i), 5 * E, P).rearrange("p (t e) -> p t e", t=5),
                                 1 / 0.7, None, ALU.mult).then_inc(dve_read, 1)
            v.drain()
            V_.tensor_reduce(sm[:, 0, :], prob[:, :, :], axis=AX.X, op=ALU.max)
            v.drain()
            V_.tensor_scalar(sm[:, 0, :], sm[:, 0, :], -1.0, None, ALU.mult)
            v.drain().then_inc(lmax_made, 1)
            v.wait_ge(prob_exp, T)
            V_.reciprocal(sm[:, 1, :], sm[:, 1, :])
            v.drain()
            V_.tensor_tensor(prob[:, :, :], prob[:, :, :], sm[:, 1, :].unsqueeze(2).to_broadcast([P, T, E]), ALU.mult)
            v.drain()
            for t in range(T):
                V_.max(top8[:, t, :], prob[:, t, :])
            v.drain()
            for t in range(T):
                V_.max_index(idx8[:, t, :], top8[:, t, :], prob[:, t, :])
            V_.tensor_tensor(sm[:, 2, :].unsqueeze(2), top8[:, :, 0:1], top8[:, :, 1:2], ALU.add)
            v.drain()
            V_.reciprocal(sm[:, 2, :], sm[:, 2, :])
            V_.tensor_copy(sm[:, 3:5, :].rearrange("p k t -> p t k"), idx8[:, :, 0:TOPK])
            v.drain()
            v.wait_ge(consts, 4)
            V_.tensor_tensor(wtop[:, :, :], top8[:, :, 0:TOPK], sm[:, 2, :].unsqueeze(2).to_broadcast([P, T, TOPK]), ALU.mult)
            for k, M in ((0, M1), (1, M2)):
                V_.tensor_tensor(M[:, :, :], iotaE[:, :].unsqueeze(1).to_broadcast([P, T, E]),
                                 sm[:, 3 + k, :].unsqueeze(2).to_broadcast([P, T, E]), ALU.is_equal)
            v.drain()
            V_.tensor_tensor(Mb[:, :, :], M1[:, :, :], M2[:, :, :], ALU.add)
            v.drain().then_inc(m_made, 1)
            V_.tensor_tensor(prob[:, :, :], M1[:, :, :], wtop[:, :, 0:1].to_broadcast([P, T, E]), ALU.mult)
            V_.tensor_tensor(tmpr[:, :, :], M2[:, :, :], wtop[:, :, 1:2].to_broadcast([P, T, E]), ALU.mult)
            v.drain()
            V_.tensor_tensor(prob[:, :, :], prob[:, :, :], tmpr[:, :, :], ALU.add)
            v.drain()
            V_.tensor_scalar(prob[:, :, :], prob[:, :, :], 4.0, None, ALU.mult)
            v.drain().then_inc(comb_made, 1)
            for i in range(2):
                reads("rank", i)
                V_.tensor_copy(rankS[:, 5 * i:5 * i + 5, :], bank(TURNS.bank("rank", i), 5 * E, P).rearrange("p (t e) -> p t e", t=5)).then_inc(dve_read, 1)
            reads("rank", 2)
            V_.tensor_reduce(sm[0:1, 5, 0:1], bank(TURNS.bank("rank", 2), E, 1), axis=AX.X, op=ALU.max).then_inc(dve_read, 1)
            v.drain()
            for k, M in ((0, M1), (1, M2)):
                V_.tensor_tensor(tmpr[:, :, :], M[:, :, :], rankS[:, :, :], ALU.mult)
                v.drain()
                V_.tensor_reduce(sm[:, 6 + k, :], tmpr[:, :, :], axis=AX.X, op=ALU.add)
                v.drain()
                V_.scalar_tensor_tensor(posf[:, k, :], sm[:, 6 + k, :], float(E), sm[:, 3 + k, :], ALU.mult, ALU.add)
            v.drain()
            V_.tensor_copy(posi[:, :, :], posf[:, :, :])
            v.drain().then_inc(pos_made, 1)
            V_.tensor_scalar(sm[0:1, 5, 1:2], sm[0:1, 5, 0:1], float(B - 1), None, ALU.add)
            v.drain()
            V_.tensor_copy(rounds[:, :], sm[0:1, 5, 1:2])
            v.drain()
            V_.tensor_single_scalar(rounds[:, :], rounds[:, :], B.bit_length() - 1, ALU.logical_shift_right)
            v.drain().then_inc(round_made, 1)
            for c in range(5):
                for k in range(2):
                    t = 2 * c + k
                    g = shared_out(c, k)
                    reads("shared", g)
                    V_.scalar_tensor_tensor(HM[:, t, :], bank(TURNS.bank("shared", g), D, P), 0.25, row("bs2"), ALU.mult, ALU.add).then_inc(dve_read, 1)
            R = v.value_load(rounds[0:1, 0:1], min_val=1, max_val=RANKS // B)

            def one_round(r):
                v.wait_ge(lst_in, 16 * (r + 1))
                if not isinstance(r, int):
                    v.wait_ge(zg_in[U - 1], 16 * (GROUPS + 1) * r)
                V_.tensor_single_scalar(gat[:, :], lst[:, :], 1, ALU.logical_shift_right)
                v.drain().then_inc(gat_made, 1)

                def group(g, first):
                    for u in range(U):
                        n = E * r + U * g + u
                        v.wait_ge(tr_done, n + 1)
                        at_least(v, h_done, n - 1)
                        for k in range(KD):
                            i = V_.tensor_scalar(hgT[:, u % 2, k, :], bank(u % 2, B, 128, k * B), col("g1", k), col("b1ln", k), ALU.mult, ALU.add)
                        i.then_inc(tr_read, 1)
                group(0, True)
                with v.Fori(1, GROUPS) as g:
                    group(g, False)

            v.wait_ge(cols_in, 16)
            one_round(0)
            with v.If(R > 1):
                with v.Fori(1, R) as r:
                    one_round(r)
            for t in range(T):
                v.wait_ge(yt_in[t % 2], 16 * (t // 2 + 1))
                V_.scalar_tensor_tensor(HM[:, t, :], Yt[:, t % 2, 0, :], wtop[:, t, 0:1], HM[:, t, :], ALU.mult, ALU.add)
                v.drain()
                V_.scalar_tensor_tensor(HM[:, t, :], Yt[:, t % 2, 1, :], wtop[:, t, 1:2], HM[:, t, :], ALU.mult, ALU.add)
                v.drain().then_inc(yt_used, 1)
            stats(HM, mv, range(T))
            inverse_std(4)
            for t in range(T):
                if t >= 2:
                    v.wait_ge(filled, TURNS.filled("fT", t - 2))
                normalise(fz[:, t % 2, :], HM[:, t, :], mv, t).then_inc(fz_made, 1)
                V_.tensor_tensor(XR[:, t, :], XR[:, t, :], row("bf2"), ALU.add)
                v.drain()
                V_.tensor_tensor(XR[:, t, :], XR[:, t, :], HM[:, t, :], ALU.add)
            v.drain()
            for t in range(T):
                reads("f2", t)
                if t >= 2:
                    v.wait_ge(out_sent[t % 2], 16 * (t // 2))
                V_.tensor_tensor(outS[:, t % 2, :], bank(TURNS.bank("f2", t), D, P), XR[:, t, :], ALU.add).then_inc(dve_read, 1)
                v.drain().then_inc(out_made, 1)

        @blk.scalar
        def _(a):
            S_ = nc.scalar

            def reads(name, i):
                a.wait_ge(filled, TURNS.filled(name, i))

            def std(mvt, count):
                a.wait_ge(ln_var, count)
                S_.activation(rs[:, :].unsqueeze(2), mvt[:, :, 1:2], ACT.Sqrt, bias=eps[:, :]).then_inc(ln_std, 1)

            std(mv, 1)
            for t in range(0, T, 2):
                reads("xnT", t)
                S_.copy(xnT[:, :, t * P:t * P + P], bank(TURNS.bank("xnT", t), 4 * P).rearrange("p (k n) -> p k n", k=4)).then_inc(act_read, 1)
            a.wait_ge(cols_in, 16)
            for m in range(KD):
                for c, (o, n) in enumerate(CHUNKS):
                    i = 3 * m + c
                    reads("mix_q", i)
                    if i >= 2:
                        a.wait_ge(qT_made, i - 1)
                    b = bank(TURNS.bank("mix_q", i), n)
                    S_.activation(eq[:, i % 2, 0:n], b, ACT.Exp, bias=col("mbq", m))
                    S_.activation(rq[:, i % 2, 0:n], b, ACT.Relu, bias=col("mbq", m)).then_inc(act_read, 1)
                    a.drain().then_inc(feat_q, 1)
            a.wait_ge(qT_made, 12)
            for t in range(T):
                a.wait_ge(tk_made, t + 1)
                if t >= 2:
                    a.wait_ge(kf_made, t - 1)
                S_.activation(ek[:, t % 2, :], tk[:, t % 2, :], ACT.Exp).then_inc(ek_made, 1)
            for i in range(4):
                for c, (o, n) in enumerate(CHUNKS):
                    reads("gnn_qk", 3 * i + c)
                    if i >= 2 and c == 0:
                        a.wait_ge(split_made, i - 1)
                    S_.activation(fqk[:, i % 2, o:o + n], bank(TURNS.bank("gnn_qk", 3 * i + c), n), ACT.Identity,
                                  bias=col("gbq" if i < 2 else "gbk", i % 2)).then_inc(act_read, 1)
            a.wait_ge(filled, TURNS.filled("gnn_v", 9))
            a.wait_ge(range_made, 1)
            at_range = [a.value_load(ranges[b:b + 1, 1:2], min_val=1, max_val=EC // EG) for b in range(T)]

            def keep_counts(b):
                a.wait_ge(c_sum, b + 1)
                S_.copy(C[:, b, 0:N], ps[0:P, (b % 2) * 1536:(b % 2) * 1536 + N]).then_inc(c_kept, 1)

            for b, n_b in enumerate(at_range):
                if b == 0:
                    a.drain().then_inc(dA_used[0], 1)
                with a.Fori(0, n_b) as g:
                    a.drain()
                    a.wait_ge(dA_made[b], g + 1)
                    S_.activation(sqA[:, :, :], dA[:, :, :], ACT.Square).then_inc(dA_used[b], 1)
                    a.drain()
                    for j in range(EG):
                        a.wait_ge(oh_used[b], g * EG + j + 1)
                        S_.activation(ohA[:, j, :], sqA[:, j, :], ACT.Relu, bias=1.0, scale=-1.0).then_inc(ohA_made[b], 1)
                if b + 1 < T:
                    a.drain().then_inc(dA_used[b + 1], 1)
                if b:
                    keep_counts(b - 1)
            keep_counts(T - 1)
            def keep_den(i):
                a.wait_ge(head_sum, i + 1)
                if i:
                    a.wait_ge(head_kept, i)
                S_.activation(rden[:, :, :], sums_of(i, 0, 128), ACT.Identity, bias=tiny[:, :]).then_inc(den_kept, 1)

            for n in range(HEADS * 2 * T):
                i, s = divmod(n // 2, T)
                a.wait_ge(s_made, n + 1)
                b = scores_of(n)
                S_.activation(b, b, ACT.Exp, scale=float(DK) ** -0.5).then_inc(s_exp, 1)
                if s == 1 and n % 2 == 0 and i >= 1:
                    keep_den(i - 1)
            keep_den(HEADS - 1)
            for m in range(KD):
                for c, (o, n) in enumerate(CHUNKS):
                    i = 3 * m + c
                    reads("gnn_a", i)
                    S_.activation(h1T[:, m, o:o + n], bank(TURNS.bank("gnn_a", i), n), ACT.Relu, bias=col("ba", m)).then_inc(act_read, 1)
            std(mv, 2)
            std(mv2, 3)
            for t in range(T):
                reads("hT", t)
                for k in range(KD):
                    i = S_.activation(hT[:, k, t * P:t * P + P], bank(TURNS.bank("hT", t), P, 128, k * P), ACT.Identity,
                                      bias=col("b1ln", k), scale=col("g1", k))
                i.then_inc(act_read, 1)
            for c, (o, n) in enumerate(CHUNKS):
                reads("rT", c)
                S_.copy(rTs[:, o:o + n], bank(TURNS.bank("rT", c), n, E)).then_inc(act_read, 1)
            a.wait_ge(lmax_made, 1)
            for t in range(T):
                S_.activation(prob[:, t, :], prob[:, t, :], ACT.Exp, bias=sm[:, 0, t:t + 1], accum_out=sm[:, 1, t:t + 1]).then_inc(prob_exp, 1)
            for c, tiles in enumerate(((0, 4), (4, 4), (8, 2))):
                reads("combT", c)
                S_.copy(combT[:, tiles[0] * P:(tiles[0] + tiles[1]) * P], bank(TURNS.bank("combT", c), tiles[1] * P, E)).then_inc(act_read, 1)
            for c in range(5):
                if c >= 2:
                    a.wait_ge(filled, TURNS.filled("shared", shared_out(c - 2, 1)))
                for i in range(4):
                    g = shared_hid(c, i)
                    reads("shared", g)
                    for k in range(2):
                        j = S_.activation(hsT[:, c % 2, 2 * i + k, :], bank(TURNS.bank("shared", g), 250, 128, 250 * k), ACT.Silu, bias=col("bs1", 2 * i + k))
                    j.then_inc(act_read, 1)
            a.wait_ge(round_made, 1)
            R = a.value_load(rounds[0:1, 0:1], min_val=1, max_val=RANKS // B)

            def hidden(r, g, u):
                n = E * r + U * g + u
                a.wait_ge(h_done, n + 1)
                at_least(a, e_done, n - 1)
                for m in range(2):
                    i = S_.activation(ehT[:, u % 2, m, :], bank(2 + u % 2, B, 128, m * B), ACT.Silu,
                                      bias=cols[:, bass.ds(COLS["eb1"][0] + m + 2 * (U * g + u), 1)])
                i.then_inc(h_read, 1)

            def result(r, g, u):
                n = E * r + U * g + u
                a.wait_ge(e_done, n + 1)
                at_least(a, y_out[u], 16 * (GROUPS * r + g))
                S_.copy(eo[:, u, :], bank(4 + u % 2, D)).then_inc(e_read, 1)

            def one_round(r):
                def group(g, first):
                    for u in range(U):
                        hidden(r, g, u)
                        if u:
                            result(r, g, u - 1)
                        elif not first:
                            result(r, g - 1, U - 1)
                group(0, True)
                with a.Fori(1, GROUPS) as g:
                    group(g, False)
                result(r, GROUPS - 1, U - 1)

            one_round(0)
            with a.If(R > 1):
                with a.Fori(1, R) as r:
                    one_round(r)
            std(mv, 4)
            for t in range(T):
                reads("fT", t)
                for k in range(KD):
                    i = S_.activation(fT[:, k, t * P:t * P + P], bank(TURNS.bank("fT", t), P, 128, k * P), ACT.Identity,
                                      bias=col("bfln", k), scale=col("gf", k))
                i.then_inc(act_read, 1)
            for c, (o, n) in enumerate(CHUNKS):
                for m in range(2):
                    i = 2 * c + m
                    reads("f1", i)
                    S_.activation(f1T[:, m, o:o + n], bank(TURNS.bank("f1", i), n), ACT.Silu, bias=col("bf1", m)).then_inc(act_read, 1)

        @blk.tensor
        def _(pe):
            MM = nc.tensor.matmul

            def turn(name, i):
                g = TURNS.first[name] + i
                if g >= RING:
                    who, count = TURNS.read(g - RING)
                    pe.wait_ge(act_read if who == "act" else dve_read, count)
                return TURNS.bank(name, i)

            def read_by_now(name, i):
                who, count = TURNS.group_read(name, i)
                pe.wait_ge(act_read if who == "act" else dve_read, count)

            pe.wait_ge(consts, 1)
            for t in range(T):
                pe.wait_ge(xn_made, t + 1)
                b = turn("xnT", t)
                for k in range(KD):
                    i = nc.tensor.transpose(bank(b, P, 128, k * P), xn[:, t, k:D:KD], ident[0:P, 0:P])
                i.then_inc(filled, 1)
            read_by_now("xnT", 8)
            read_by_now("xnT", 9)
            pe.wait_ge(mw_in, 48)
            for m in range(KD):
                for c, (o, n) in enumerate(CHUNKS):
                    b = turn("mix_q", 3 * m + c)
                    for k in range(KD):
                        i = MM(bank(b, n), mW[:, 0, k, m * 128:m * 128 + 128], xnT[:, k, o:o + n], start=k == 0, stop=k == KD - 1)
                    i.then_inc(filled, 1)

            def sum_kv(t):
                pe.wait_ge(kf_made, t + 1)
                read_by_now("mix_kv", 2 * t + 1)
                for p in range(KD):
                    i = MM(bank(6 + p // 2, 129, 128, (p % 2) * 129), kf[:, t % 2, p * 128:p * 128 + 128], vt[:, t % 2, p, :],
                           start=t == 0 and p % 2 == 0, stop=t == T - 1 and p % 2 == 1, skip_group_check=True)
                i.then_inc(kv_used, 1)

            for t in range(T):
                for w in range(2):
                    b = turn("mix_kv", 2 * t + w)
                    for k in range(KD):
                        i = MM(bank(b, D, P), xnT[:, k, t * P:t * P + P], mW[:, 1 + w, k, :], start=k == 0, stop=k == KD - 1)
                    i.then_inc(filled, 1)
                if t:
                    sum_kv(t - 1)
            sum_kv(T - 1)
            pe.drain().then_inc(kv_summed, 1)
            pe.wait_ge(kvb_made, 1)
            pe.wait_ge(qT_made, 12)
            for i in range(12):
                p, (o, n) = i // 3, CHUNKS[i % 3]
                for j, w in enumerate((ksb, kvb)):
                    b = turn("mix_o", 2 * i + j)
                    MM(bank(b, n), w[:, p, :], qT[:, p, o:o + n], start=True, stop=True).then_inc(filled, 1)
            read_by_now("mix_o", 23)
            pe.wait_ge(mwo_in, 16)
            for t in range(T):
                b = turn("mix_wo", t)
                for k in range(KD):
                    i = MM(bank(b, D, P), moT[:, k, t * P:t * P + P], mWo[:, k, :], start=k == 0, stop=k == KD - 1)
                i.then_inc(filled, 1)
            pe.wait_ge(gw_in, 48)
            for i in range(4):
                for c, (o, n) in enumerate(CHUNKS):
                    b = turn("gnn_qk", 3 * i + c)
                    for k in range(KD):
                        j = MM(bank(b, n), gW[:, i // 2, k, (i % 2) * 128:(i % 2) * 128 + 128], xnT[:, k, o:o + n], start=k == 0, stop=k == KD - 1)
                    j.then_inc(filled, 1)
            for t in range(T):
                b = turn("gnn_v", t)
                for k in range(KD):
                    i = MM(bank(b, HEADS * DK, P), xnT[:, k, t * P:t * P + P], gW[:, 2, k, :], start=k == 0, stop=k == KD - 1)
                i.then_inc(filled, 1)
            for i in range(RING):
                read_by_now("gnn_v", 9 - i)
            pe.wait_ge(range_made, 1)
            at_range = [pe.value_load(ranges[b:b + 1, 1:2], min_val=1, max_val=EC // EG) for b in range(T)]
            for b, n_b in enumerate(at_range):
                if b >= 2:
                    pe.wait_ge(c_kept, b - 1)
                for o, n in BANKED:
                    i = MM(ps[0:P, (b % 2) * 1536 + o:(b % 2) * 1536 + o + n], zeros[0:1, 0:P], zeros[0:1, 0:n],
                           start=True, stop=False, skip_group_check=True)
                i.then_inc(oh_used[b], EG)
                with pe.Fori(0, n_b) as g:
                    for j in range(EG):
                        pe.wait_ge(oh_made[b], g * EG + j + 1)
                        pe.wait_ge(ohA_made[b], g * EG + j + 1)
                        for o, n in BANKED:
                            i = MM(ps[0:P, (b % 2) * 1536 + o:(b % 2) * 1536 + o + n], ohA[:, j, :], ohB[:, j, o:o + n],
                                   start=False, stop=False, skip_group_check=True)
                        i.then_inc(oh_used[b], 1)
                pe.drain().then_inc(c_sum, 1)
            def scores(n):
                i, s = divmod(n // 2, T)
                h = 2 * (i // 2) + n % 2
                if s == 0 and i % 2 == 0:
                    pe.wait_ge(st_in[h % 4], 128 * (h // 4 + 1))
                if n >= 2:
                    pe.wait_ge(att_made, n - 1)
                for a in range(2):
                    o = (i % 2) * HALF + a * PIECE
                    j = MM(scores_of(n)[:, a, :], Kst[:, h % 4, s * P:s * P + P], Qst[:, h % 4, o:o + PIECE], start=True, stop=True)
                j.then_inc(s_made, 1)
                if s == T - 1 and i % 2 and n % 2:
                    pe.drain().then_inc(st_used, 1)

            def sums(m):
                i, s = divmod(m, T)
                pe.wait_ge(att_made, 2 * m + 2)
                if s == 0 and i >= 2:
                    pe.wait_ge(head_kept, i - 1)
                for a in range(2):
                    for j in range(2):
                        h = 2 * (i // 2) + j
                        k = MM(sums_of(i, 64 * j, 64)[:, a, :], V[:, s, h // 2, j:j + 2, :], att[:, (2 * m + j) % 4, a, :],
                               start=s == 0, stop=s == T - 1, skip_group_check=True)
                k.then_inc(att_used, 1)
                if s == T - 1:
                    pe.drain().then_inc(head_sum, 1)

            pe.wait_ge(c_kept, T)
            pe.wait_ge(pads_made, 1)
            scores(0)
            scores(1)
            for m in range(HEADS * T):
                if m + 1 < HEADS * T:
                    scores(2 * m + 2)
                    scores(2 * m + 3)
                sums(m)
            pe.wait_ge(head_kept, HEADS)
            pe.wait_ge(waf_in, 32)
            for m in range(KD):
                for c, (o, n) in enumerate(CHUNKS):
                    b = turn("gnn_a", 3 * m + c)
                    for k in range(2):
                        i = MM(bank(b, n), Wa_s[:, k, m:D:KD], aggT[:, k, o:o + n], start=k == 0, stop=k == 1)
                    i.then_inc(filled, 1)
            read_by_now("gnn_a", 11)
            for t in range(T):
                b = turn("gnn_f", t)
                for k in range(KD):
                    i = MM(bank(b, D, P), h1T[:, k, t * P:t * P + P], Wf_s[:, k, :], start=k == 0, stop=k == KD - 1)
                i.then_inc(filled, 1)
            for t in range(T):
                pe.wait_ge(z_made, t + 1)
                b = turn("hT", t)
                for k in range(KD):
                    i = nc.tensor.transpose(bank(b, P, 128, k * P), yz[:, t, k:D:KD], ident[0:P, 0:P])
                i.then_inc(filled, 1)
            read_by_now("hT", 9)
            pe.wait_ge(small_in, 48)
            for c, (o, n) in enumerate(CHUNKS):
                b = turn("rT", c)
                for k in range(KD):
                    i = MM(bank(b, n, E), Wr_s[:, k, :], hT[:, k, o:o + n], start=k == 0, stop=k == KD - 1)
                i.then_inc(filled, 1)
            read_by_now("rT", 2)
            for c in range(2):
                b = turn("logit", c)
                for t in range(5):
                    i = MM(bank(b, E, P, t * E), rTs[:, (5 * c + t) * P:(5 * c + t + 1) * P], cbT_s[:, :], start=True, stop=True)
                i.then_inc(filled, 1)
            pe.wait_ge(m_made, 1)
            for c in range(3):
                b = turn("rank", c)
                for t in (range(5 * c, 5 * c + 5) if c < 2 else (T,)):
                    o = (t - 5 * c) * E
                    for q in range(min(t + 1, T)):
                        i = MM(bank(b, E, P, o), (ltri if q == t else ones)[:, :], Mb[:, q, :], start=q == 0, stop=q == min(t, T - 1))
                i.then_inc(filled, 1)
            pe.wait_ge(comb_made, 1)
            for c, (t0, n) in enumerate(((0, 4), (4, 4), (8, 2))):
                b = turn("combT", c)
                for t in range(n):
                    i = nc.tensor.transpose(bank(b, P, E, t * P), prob[:, t0 + t, :], ident[0:P, 0:P])
                i.then_inc(filled, 1)
            pe.wait_ge(ws1_in, 16)
            pe.wait_ge(ws2_in, 16)

            def shared_rows(c):
                read_by_now("shared", shared_hid(c, 3))
                if c == 0:
                    read_by_now("combT", 2)
                for k2 in range(2):
                    t = 2 * c + k2
                    b = turn("shared", shared_out(c, k2))
                    MM(bank(b, D, P), combT[:, t * P:t * P + P], b2_s[:, :], start=True, stop=False)
                    for k in range(DSH // 128):
                        i = MM(bank(b, D, P), hsT[:, c % 2, k, k2 * P:k2 * P + P], Ws2_s[:, k, :], start=False, stop=k == DSH // 128 - 1)
                    i.then_inc(filled, 1)

            for c in range(5):
                for g in range(4):
                    b = turn("shared", shared_hid(c, g))
                    for k2 in range(2):
                        for k in range(KD):
                            i = MM(bank(b, 250, 128, 250 * k2), Ws1_s[:, k, (2 * g + k2) * 128:(2 * g + k2 + 1) * 128],
                                   hT[:, k, c * 250:c * 250 + 250], start=k == 0, stop=k == KD - 1)
                    i.then_inc(filled, 1)
                if c:
                    shared_rows(c - 1)
            shared_rows(4)
            for i in range(RING):
                read_by_now("shared", len(TURNS.who[TURNS.first["shared"]:TURNS.first["fT"]]) - 1 - i)
            R = pe.value_load(rounds[0:1, 0:1], min_val=1, max_val=RANKS // B)

            def transposes(r, g, u):
                n = E * r + U * g + u
                pe.wait_ge(zg_in[u], 16 * ((GROUPS + 1) * r + g + 1))
                at_least(pe, tr_read, n - 1)
                for k in range(KD):
                    i = nc.tensor.transpose(bank(u % 2, B, 128, k * B), Zg[:, u, k:D:KD], ident[:, :])
                i.then_inc(tr_done, 1)

            def hidden(r, g, u):
                n = E * r + U * g + u
                pe.wait_ge(tr_read, n + 1)
                pe.wait_ge(w_in[u], 32 * (GROUPS * r + g + 1))
                at_least(pe, h_read, n - 1)
                for m in range(2):
                    for k in range(KD):
                        i = MM(bank(2 + u % 2, B, 128, m * B), W1[u][:, k, m:DFF:2], hgT[:, u % 2, k, :], start=k == 0, stop=k == KD - 1)
                i.then_inc(h_done, 1)

            def result(r, g, u):
                n = E * r + U * g + u
                pe.wait_ge(h_read, n + 1)
                at_least(pe, e_read, n - 1)
                for m in range(2):
                    i = MM(bank(4 + u % 2, D), ehT[:, u % 2, m, :], W2[u][:, m, :], start=m == 0, stop=m == 1)
                i.then_inc(e_done, 1)

            def one_round(r):
                def group(g, first):
                    for u in range(U):
                        transposes(r, g, u)
                        if u:
                            hidden(r, g, u - 1)
                            if u > 1:
                                result(r, g, u - 2)
                            elif not first:
                                result(r, g - 1, U - 1)
                        elif not first:
                            hidden(r, g - 1, U - 1)
                            result(r, g - 1, U - 2)
                group(0, True)
                with pe.Fori(1, GROUPS) as g:
                    group(g, False)
                hidden(r, GROUPS - 1, U - 1)
                result(r, GROUPS - 1, U - 2)
                result(r, GROUPS - 1, U - 1)

            one_round(0)
            with pe.If(R > 1):
                with pe.Fori(1, R) as r:
                    one_round(r)
            pe.wait_ge(tr_read, R * E)
            pe.wait_ge(h_read, R * E)
            pe.wait_ge(e_read, R * E)
            for t in range(T):
                pe.wait_ge(fz_made, t + 1)
                b = turn("fT", t)
                for k in range(KD):
                    i = nc.tensor.transpose(bank(b, P, 128, k * P), fz[:, t % 2, k:D:KD], ident[0:P, 0:P])
                i.then_inc(filled, 1)
            pe.wait_ge(wf1_in, 16)
            pe.wait_ge(wf2_in, 16)
            for c, (o, n) in enumerate(CHUNKS):
                read_by_now("fT", min(T - 1, (o + n) // P - 1))
                for m in range(2):
                    b = turn("f1", 2 * c + m)
                    for k in range(KD):
                        i = MM(bank(b, n), Wf1_s[:, k, m:DFF:2], fT[:, k, o:o + n], start=k == 0, stop=k == KD - 1)
                    i.then_inc(filled, 1)
            for t in range(T):
                read_by_now("f1", 2 * min(2, t // 4) + 1)
                b = turn("f2", t)
                for k in range(2):
                    i = MM(bank(b, D, P), f1T[:, k, t * P:t * P + P], Wf2_s[:, k, :], start=k == 0, stop=k == 1)
                i.then_inc(filled, 1)


def shared_hid(c, i):
    return i if c == 0 else 4 + 6 * (c - 1) + i


def shared_out(c, k):
    return 4 + 6 * c + 4 + k if c < 4 else 4 + 6 * 4 + k


def kernel(**inputs):
    import concourse.bacc as bacc
    from concourse.bass_utils import run_bass_kernel_spmd

    g = {k: np.asarray(a) for k, a in inputs.items()}

    def pk(a, k):
        return a.reshape(128, k)

    def kp(a):
        return a.reshape(-1, 128).T

    cols = np.concatenate([
        kp(g["L0_mix_bq"]), kp(g["L0_gnn_bq"]), kp(g["L0_gnn_bk"]), pk(g["L0_gnn_ba"], 4), kp(g["L0_ffn_bs1"]),
        pk(g["L0_ffn_bf1"], 2), pk(g["L0_ffn_ln1_g"], 4), pk(g["L0_ffn_ln1_b"], 4), pk(g["L0_ffn_ffln_g"], 4),
        pk(g["L0_ffn_ffln_b"], 4), g["L0_ffn_b1"].reshape(E, 128, 2).transpose(1, 0, 2).reshape(128, 2 * E)], axis=1)
    gbv = np.zeros(D, np.float32)
    gbv[:HEADS * DK] = g["L0_gnn_bv"]
    rows = np.stack([g["L0_mix_bk"], g["L0_mix_bv"], g["L0_mix_bo"], g["L0_gnn_bf"], g["L0_ffn_bs2"], g["L0_ffn_bf2"], gbv])
    arrays = {
        "x": g["x"], "cols": cols, "rows": rows,
        "src": g["src"].reshape(EC, P).T, "dst": g["dst"].reshape(EC, P).T,
        "mWqT": g["L0_mix_Wq"].T, "mWkT": g["L0_mix_Wk"].T, "mWvT": g["L0_mix_Wv"].T, "mWoT": g["L0_mix_Wo"].T,
        "gWq": g["L0_gnn_Wq"], "gWk": g["L0_gnn_Wk"], "gWv": g["L0_gnn_Wv"], "Wa": g["L0_gnn_Wa"], "Wf": g["L0_gnn_Wf"],
        "Wr": g["L0_ffn_Wr"], "cbT": g["L0_ffn_codebook"].T, "W1": g["L0_ffn_W1"], "W2": g["L0_ffn_W2"],
        "b2": g["L0_ffn_b2"], "Ws1": g["L0_ffn_Ws1"], "Ws2": g["L0_ffn_Ws2"], "Wf1": g["L0_ffn_Wf1"], "Wf2": g["L0_ffn_Wf2"],
    }
    arrays = {f"in_{k}": np.ascontiguousarray(a) for k, a in arrays.items()}
    nc = bacc.Bacc("TRN2", target_bir_lowering=False, num_devices=1)
    A = {k[3:]: nc.dram_tensor(k, a.shape, mybir.dt.from_np(a.dtype), kind="ExternalInput").ap() for k, a in arrays.items()}
    out = nc.dram_tensor("out_dram", (N, D), F32, kind="ExternalOutput").ap()
    block_kernel(nc, A, out)
    r = run_bass_kernel_spmd(nc, [arrays], core_ids=[0])
    return r.results[0]["out_dram"]
```

```python
from contextlib import ExitStack

import numpy as np
import concourse.bass as bass
from concourse import mybir

F32 = mybir.dt.float32
F32R = mybir.dt.float32r
BF16 = mybir.dt.bfloat16
F16 = mybir.dt.float16
I32 = mybir.dt.int32
U32 = mybir.dt.uint32
ALU = mybir.AluOpType
ACT = mybir.ActivationFunctionType
AX = mybir.AxisListType

N, D, P = 1250, 512, 125
T = N // P
KD = D // 128
EDGES = 40000
EC = EDGES // P
EG = 4
HEADS, DK = 8, 32
E, TOPK, DFF, DSH = 64, 2, 256, 1024
B = 128
RANKS = -(-N // B) * B
U = 4
GROUPS = E // U
NOBODY = 1 << 20
RING = 6
CHUNKS = [(0, 500), (500, 500), (1000, 250)]
BANKED = [(0, 512), (512, 512), (1024, 226)]
NQ = 1280
HALF, PIECE = NQ // 2, NQ // 4
TINY = 1.2e-38

COLS = {}
for _name, _n in (("mbq", 4), ("gbq", 2), ("gbk", 2), ("ba", 4), ("bs1", 8), ("bf1", 2), ("g1", 4),
                  ("b1ln", 4), ("gf", 4), ("bfln", 4), ("eb1", 2 * E)):
    COLS[_name] = (sum(n for _, n in COLS.values()), _n)
NCOLS = sum(n for _, n in COLS.values())
ROWS = {"mbk": 0, "mbv": 1, "mbo": 2, "gbf": 3, "bs2": 4, "bf2": 5, "gbv": 6}


class Turns:

    def __init__(self, plan):
        self.place, self.who = {}, []
        for name, consumers in plan:
            for who in consumers:
                self.place.setdefault(name, []).append(len(self.who))
                self.who.append(who)

    def bank(self, name, i):
        return self.place[name][i] % RING

    def filled(self, name, i):
        return self.place[name][i] + 1

    def read(self, g):
        return self.who[g], self.who[:g + 1].count(self.who[g])

    def group_read(self, name, i):
        return self.read(self.place[name][i])


TURNS = Turns([
    ("xnT", ["act", "dve"] * 5),
    ("mix_q", ["act"] * 12),
    ("mix_kv", ["dve"] * 20),
    ("mix_o", ["dve"] * 20),
    ("moT", ["act"] * 10),
    ("mix_wo", ["dve"] * 10),
    ("gnn_qk", ["act"] * 12),
    ("gnn_v", ["dve"] * 10),
    ("gnn_a", ["act"] * 12),
    ("gnn_f", ["dve"] * 10),
    ("hT", ["act", "dve"] * 5),
    ("rT", ["act"] * 3),
    ("logit", ["dve"] * 2),
    ("hidden", ["act"] * 8),
    ("rank", ["dve"] * 3),
    ("combT", ["act"] * 3),
    ("shared", ["dve"] * 2), ("hidden", ["act"] * 4),
    ("shared", ["dve"] * 2), ("hidden", ["act"] * 4),
    ("shared", ["dve"] * 2), ("hidden", ["act"] * 4),
    ("shared", ["dve"] * 4),
    ("fT", ["act", "dve"] * 2), ("f1", ["act"] * 2),
    ("fT", ["act", "dve"] * 2), ("f2", ["dve"] * 4), ("f1", ["act"] * 2),
    ("fT", ["act", "dve"]), ("f2", ["dve"] * 4), ("f1", ["act"] * 2),
    ("f2", ["dve"] * 2),
])


def at_least(eng, sem, value):
    if not isinstance(value, int) or value > 0:
        eng.wait_ge(sem, value)


def block_kernel(nc, A, out):
    ctx = ExitStack()
    with ctx:
        KB = 1024
        base = nc.sbuf_base + (-nc.sbuf_base) % 64

        def at(name, shape, dt, offset):
            return nc.alloc_sbuf_tensor_at(name, shape, dt, offset=base + int(offset))

        def sem(name):
            return ctx.enter_context(nc.semaphore(name))

        fixed = [0]

        def keep(name, shape, dt):
            size = int(np.prod(shape[1:])) * mybir.dt.size(dt)
            off = fixed[0]
            fixed[0] += size + (-size) % 64
            return at(name, shape, dt, off)

        ident = keep("ident", [128, 128], F32)
        cols = keep("cols", [128, NCOLS], F32)
        rows = keep("rows", [128, len(ROWS), D], F32)
        XR = keep("XR", [P, T, D], F32)
        st = keep("st", [P, T, 6], F32)
        mv = keep("mv", [P, T, 2], F32)
        mv2 = keep("mv2", [P, T, 2], F32)
        rs = keep("rs", [P, T], F32)
        eps = keep("eps", [P, 1], F32)
        Wr_s = keep("Wr_s", [128, KD, E], F32)
        cbT_s = keep("cbT_s", [E, E], F32)
        b2_s = keep("b2_s", [E, D], F32)
        spare = keep("spare", [1, 1], F32)
        tiny = keep("tiny", [128, 1], F32)
        counted = keep("counted", [1, 2], F32)
        wtop = keep("wtop", [P, T, TOPK], F32)
        idxg = keep("idxg", [128, U, 1], U32)
        idxs = keep("idxs", [128, U, 1], U32)
        lst = keep("lst", [128, E + U], U32)
        gat = keep("gat", [128, E + U], U32)
        carry = keep("carry", [1, 5, 1], F32)
        rounds = keep("rounds", [1, 1], I32)
        ranges = keep("ranges", [T, 2], I32)
        zeros = keep("zeros", [1, 640], BF16)
        fixed[0] += (-fixed[0]) % 64
        W1 = [keep(f"W1_{u}", [128, KD, DFF], F32) for u in range(U)]
        W2 = [keep(f"W2_{u}", [128, 2, D], F32) for u in range(U)]
        G = fixed[0]

        def ph(name, shape, dt, kb):
            return at(name, shape, dt, G + kb * KB)

        xs = ph("xs", [P, T, D], F32, 0)
        xn = ph("xn", [P, T, D], F32, 20)
        xnT = ph("xnT", [128, KD, N], F32, 40)
        mW = ph("mW", [128, 3, KD, D], F32, 60)
        mWo = ph("mWo", [128, KD, D], F32, 84)
        gW = ph("gW", [128, 3, KD, HEADS * DK], F32, 92)
        qT = ph("qT", [128, KD, N], F32, 104)
        eq = ph("eq", [128, 2, 500], F32, 124)
        rq = ph("rq", [128, 2, 500], F32, 128)
        tk = ph("tk", [P, 2, D], F32, 124)
        ek = ph("ek", [P, 2, D], F32, 128)
        kf = ph("kf", [P, 2, D], F32, 34)
        vt = ph("vt", [P, 2, KD, 129], F32, 20)
        kvb = ph("kvb", [128, KD, 130], F32, 60)
        zt = ph("zt", [P, 2, HEADS], F32, 63)
        mo = ph("mo", [P, T, D], F32, 0)
        moT = ph("moT", [128, KD, N], F32, 20)
        fqk = ph("fqk", [128, 2, N], F32, 60)
        qk_hi = ph("qk_hi", [128, 2, N], F32R, 20)
        qk_lo = ph("qk_lo", [128, 2, N], F32R, 30)
        V = ph("V", [P, T, HEADS // 2, 3, DK], F32, 119.25)

        C = ph("C", [P, T, NQ], F32, 40)
        Wa_s = ph("Wa_s", [128, 2, D], F32, 20)
        Wf_s = ph("Wf_s", [128, KD, D], F32, 0)
        ohB = ph("ohB", [P, EG, N], BF16, 104)
        ohA = ph("ohA", [P, EG, P], BF16, 103)
        iota = ph("iota", [P, N], F16, 114.25)
        e_i = ph("e_i", [P, 2, EC], I32, 104)
        e_f = ph("e_f", [P, 2, EC], F32, 116.75)
        neg = ph("neg", [P, EC], F32, 86.5)
        cmx = ph("cmx", [P, 2, EC], F32, 84)
        ov = ph("ov", [T, 3, EC], F32, 104)
        gi = ph("gi", [T, 2, EC], F32, 108)
        lim = ph("lim", [T, 8], F32, 111)
        dA = ph("dA", [P, EG, P], F16, 92)
        sqA = ph("sqA", [P, EG, P], F32, 93)
        att = ph("att", [P, 4, 2, PIECE], F32, 104)
        rden = ph("rden", [128, 2, PIECE], F32, 114)
        Kst = ph("Kst", [128, 4, N], F32R, 0)
        Qst = ph("Qst", [128, 4, NQ], F32R, 20)
        aggT = ph("aggT", [128, 2, NQ], F32, 92)
        h1T = ph("h1T", [128, KD, N], F32, 40)
        tf = ph("tf", [P, 2, D], F32, 30)

        yz = ph("yz", [P, T, D], F32, 102)
        HM = ph("HM", [P, T, D], F32, 20)
        hT = ph("hT", [128, KD, N], F32, 60)
        Ws1_s = ph("Ws1_s", [128, KD, DSH], F32, 80)
        Ws2_s = ph("Ws2_s", [128, DSH // 128, D], F32, 0)
        hsT = ph("hsT", [128, 2, DSH // 128, 250], F32, 96)
        Wf1_s = ph("Wf1_s", [128, KD, DFF], F32, 16)
        Wf2_s = ph("Wf2_s", [128, 2, D], F32, 112)
        rTs = ph("rTs", [E, N], F32, 96)
        prob = ph("prob", [P, T, E], F32, 40)
        M1 = ph("M1", [P, T, E], F32, 42.5)
        M2 = ph("M2", [P, T, E], F32, 45)
        Mb = ph("Mb", [P, T, E], BF16, 47.5)
        tmpr = ph("tmpr", [P, T, E], F32, 49)
        rankS = ph("rankS", [P, T, E], F32, 51.5)
        combT = ph("combT", [E, N], F32, 54)
        iotaE = ph("iotaE", [P, E], F32, 130)
        iotaE_i = ph("iotaE_i", [P, E], I32, 130.5)
        sm = ph("sm", [P, 16, T], F32, 124)
        top8 = ph("top8", [P, T, 8], F32, 124.75)
        idx8 = ph("idx8", [P, T, 8], U32, 125.25)
        posf = ph("posf", [P, TOPK, T], F32, 125.75)
        posi = ph("posi", [P, TOPK, T], U32, 126)
        toki = ph("toki", [P, TOPK, T], U32, 126.25)
        ltri = ph("ltri", [P, P], BF16, 126.5)
        ones = ph("ones", [P, P], BF16, 126.75)
        nobody = ph("nobody", [128, RANKS * E // 128], U32, 127)
        Zg = ph("Zg", [128, U, D], F32, 116)
        hgT = ph("hgT", [128, 2, KD, B], F32, 124)
        ehT = ph("ehT", [128, 2, 2, B], F32, 128)
        eo = ph("eo", [128, U, D], F32, 40)
        Yt = ph("Yt", [P, 2, TOPK, D], F32, 80)
        fz = ph("fz", [P, 2, D], F32, 88)
        fT = ph("fT", [128, KD, N], F32, 60)
        f1T = ph("f1T", [128, 2, N], F32, 96)
        outS = ph("outS", [P, 2, D], F32, 92)

        ps = ctx.enter_context(nc.psum_tensor("ps", [128, 8 * 512], F32))

        def bank(b, n, p=128, off=0):
            return ps[0:p, b * 512 + off:b * 512 + off + n]

        def scores_of(n):
            return ps[0:P, (n % 2) * 1024:(n % 2) * 1024 + 1024].rearrange("p (a n) -> p a n", a=2)[:, :, 0:PIECE]

        def sums_of(i, p0, n):
            o = 2048 + (i % 2) * 1024
            return ps[p0:p0 + n, o:o + 1024].rearrange("p (a n) -> p a n", a=2)[:, :, 0:PIECE]

        qk_d = nc.dram_tensor("qk_d", [2, 2, 2 * 128, N], F32, kind="Internal").ap()
        z_d = nc.dram_tensor("z_d", [N, D], F32, kind="Internal").ap()
        y_d = nc.dram_tensor("y_d", [N * TOPK, D], F32, kind="Internal").ap()
        list_d = nc.dram_tensor("list_d", [RANKS * E, 1], U32, kind="Internal").ap()

        x_in = [sem(f"x_in{i}") for i in range(2)]
        edges_in, cols_in, rows_in = sem("edges_in"), sem("cols_in"), sem("rows_in")
        mw_in, mwo_in, gw_in = sem("mw_in"), sem("mwo_in"), sem("gw_in")
        waf_in, small_in = sem("waf_in"), sem("small_in")
        ws1_in, ws2_in, wf1_in, wf2_in = sem("ws1_in"), sem("ws2_in"), sem("wf1_in"), sem("wf2_in")
        st_in = [sem(f"st_in{i}") for i in range(4)]
        w_in = [sem(f"w_in{u}") for u in range(U)]
        consts = sem("consts")
        filled = sem("filled")
        act_read, dve_read = sem("act_read"), sem("dve_read")
        ln_var, ln_std = sem("ln_var"), sem("ln_std")
        y_var, y_std, z_var, z_std, f_var, f_std = (sem("y_var"), sem("y_std"), sem("z_var"), sem("z_std"),
                                                    sem("f_var"), sem("f_std"))
        xy_kept = sem("xy_kept")
        xn_made, xr_made = sem("xn_made"), sem("xr_made")
        feat_q = sem("feat_q")
        qT_made = sem("qT_made")
        tk_made, ek_made, kf_made = sem("tk_made"), sem("ek_made"), sem("kf_made")
        kv_summed, kvb_made = sem("kv_summed"), sem("kvb_made")
        kv_used = sem("kv_used")
        split_made = sem("split_made")
        qk_out = [sem(f"qk_out{i}") for i in range(4)]
        cmax_made, range_made = sem("cmax_made"), sem("range_made")
        edges_f = sem("edges_f")
        oh_made = [sem(f"oh_made{b}") for b in range(T)]
        oh_used = [sem(f"oh_used{b}") for b in range(T)]
        dA_made = [sem(f"dA_made{b}") for b in range(T)]
        dA_used = [sem(f"dA_used{b}") for b in range(T)]
        ohA_made = [sem(f"ohA_made{b}") for b in range(T)]
        c_sum, c_kept, pads_made = sem("c_sum"), sem("c_kept"), sem("pads_made")
        s_made, s_exp, att_made, att_used = sem("s_made"), sem("s_exp"), sem("att_made"), sem("att_used")
        head_sum, head_kept, den_kept, rden_used = sem("head_sum"), sem("head_kept"), sem("den_kept"), sem("rden_used")
        idxg_made, idxs_made = sem("idxg_made"), sem("idxs_made")
        st_used = sem("st_used")
        y_made, z_made, z_out = sem("y_made"), sem("z_made"), sem("z_out")
        lmax_made, prob_exp, m_made = sem("lmax_made"), sem("prob_exp"), sem("m_made")
        comb_made, pos_made, list_clear, list_made = (sem("comb_made"), sem("pos_made"),
                                                      sem("list_clear"), sem("list_made"))
        round_made, lst_in, gat_made = sem("round_made"), sem("lst_in"), sem("gat_made")
        zg_in = [sem(f"zg_in{u}") for u in range(U)]
        tr_done, tr_read, h_done, h_read = sem("tr_done"), sem("tr_read"), sem("h_done"), sem("h_read")
        e_done, e_read = sem("e_done"), sem("e_read")
        y_out = [sem(f"y_out{u}") for u in range(U)]
        yt_in = [sem(f"yt_in{i}") for i in range(2)]
        yt_used, fz_made = sem("yt_used"), sem("fz_made")
        out_made = sem("out_made")
        out_sent = [sem(f"out_sent{i}") for i in range(2)]
        blk = ctx.enter_context(nc.Block())

        def col(name, i, n=1, p=128):
            o = COLS[name][0] + i
            return cols[0:p, o:o + n]

        def row(name, n=D):
            return rows[0:P, ROWS[name], 0:n]

        def in_range(group):
            return nc.s_assert_within(group, 0, EC // EG - 1, skip_runtime_bounds_check_because=
                                      "first group + count is at most the number of groups, as made on VectorE")

        @blk.sync
        def _(sp):
            x_v = A["x"].rearrange("(t p) d -> p t d", p=P)
            for i in range(2):
                sp.dma_start(xs[:, 5 * i:5 * i + 5, :], x_v[:, 5 * i:5 * i + 5, :]).then_inc(x_in[i], 16)
            sp.dma_start(cols[:, :], A["cols"]).then_inc(cols_in, 16)
            for j, w in enumerate(("mWqT", "mWkT", "mWvT")):
                sp.dma_start(mW[:, j], A[w].rearrange("(p k) n -> p k n", k=KD)).then_inc(mw_in, 16)
            for name, j in ROWS.items():
                sp.dma_start(rows[:, j, :], A["rows"][j:j + 1, :].partition_broadcast(128)).then_inc(rows_in, 16)
            sp.dma_start(mWo[:, :, :], A["mWoT"].rearrange("(k p) n -> p k n", p=128)).then_inc(mwo_in, 16)
            for j, w in enumerate(("gWq", "gWk", "gWv")):
                sp.dma_start(gW[:, j], A[w].rearrange("(p k) n -> p k n", k=KD)).then_inc(gw_in, 16)
            sp.dma_start(Wr_s[:, :, :], A["Wr"].rearrange("(p k) n -> p k n", k=KD)).then_inc(small_in, 16)
            sp.dma_start(cbT_s[:, :], A["cbT"]).then_inc(small_in, 16)
            sp.dma_start(b2_s[:, :], A["b2"]).then_inc(small_in, 16)

            def weights(e, u, static=False):
                w1 = A["W1"] if static else A["W1"]
                sp.dma_start(W1[u][:, :, :], w1[bass.ds(e, 1)].rearrange("e (p k) f -> p (e k) f", k=KD)).then_inc(w_in[u], 16)
                sp.dma_start(W2[u][:, :, :], A["W2"][bass.ds(e, 1)].rearrange("e (p m) n -> p (e m) n", m=2)).then_inc(w_in[u], 16)

            for u in range(U):
                weights(u, u)
            sp.wait_ge(filled, TURNS.filled("mix_o", 19))
            for j, w in enumerate(("src", "dst")):
                sp.dma_start(e_i[:, j, :], A[w]).then_inc(edges_in, 16)
            for i in range(4):
                sp.wait_ge(qk_out[i], 32)
            for h in range(HEADS):
                if h >= 4:
                    sp.wait_ge(st_used, h // 2 - 1)
                for j in range(4):
                    d = h * DK
                    sp.dma_start(Kst[32 * j:32 * j + 32, h % 4, :].bitcast(F32), qk_d[1, j // 2, d:d + DK, :]).then_inc(st_in[h % 4], 16)
                    sp.dma_start(Qst[32 * j:32 * j + 32, h % 4, 0:N].bitcast(F32), qk_d[0, j % 2, d:d + DK, :]).then_inc(st_in[h % 4], 16)
            sp.wait_ge(st_used, 3)
            sp.dma_start(Wa_s[:, :, :], A["Wa"].rearrange("(k p) n -> p k n", p=128)).then_inc(waf_in, 16)
            sp.dma_start(Wf_s[:, :, :], A["Wf"].rearrange("(p k) n -> p k n", k=KD)).then_inc(waf_in, 16)
            sp.wait_ge(filled, TURNS.filled("gnn_f", 9))
            sp.dma_start(Ws2_s[:, :, :], A["Ws2"].rearrange("(k p) n -> p k n", p=128)).then_inc(ws2_in, 16)
            sp.dma_start(Wf1_s[:, :, :], A["Wf1"].rearrange("(p k) n -> p k n", k=KD)).then_inc(wf1_in, 16)
            sp.dma_start(Ws1_s[:, :, :], A["Ws1"].rearrange("(p k) n -> p k n", k=KD)).then_inc(ws1_in, 16)
            with sp.Fori(1, GROUPS) as g:
                for u in range(U):
                    sp.wait_ge(e_done, U * g + u - U + 1)
                    weights(U * g + u, u)
            sp.wait_ge(round_made, 1)
            R = sp.value_load(rounds[0:1, 0:1], min_val=1, max_val=RANKS // B)
            with sp.If(R > 1):
                with sp.Fori(1, R) as r:
                    with sp.Fori(0, GROUPS) as g:
                        for u in range(U):
                            sp.wait_ge(e_done, E * r + U * g + u - U + 1)
                            weights(U * g + u, u)
            sp.dma_start(Wf2_s[:, :, :], A["Wf2"].rearrange("(p k) n -> p k n", k=2)).then_inc(wf2_in, 16)
            for u in range(U):
                sp.wait_ge(y_out[u], R * (16 * GROUPS))
            y_v = y_d.rearrange("(t p k) d -> t p k d", p=P, k=TOPK)
            for t in range(T):
                if t >= 2:
                    sp.wait_ge(yt_used, t - 1)
                sp.dma_start(Yt[:, t % 2], y_v[t]).then_inc(yt_in[t % 2], 16)
            o_v = out.rearrange("(t p) d -> t p d", p=P)
            for t in range(T):
                sp.wait_ge(out_made, t + 1)
                sp.dma_start(o_v[t], outS[:, t % 2, :]).then_inc(out_sent[t % 2], 16)
            for i in range(2):
                sp.wait_ge(out_sent[i], 16 * (T // 2))

        @blk.gpsimd
        def _(gp):
            nc.gpsimd.memset(ident[:, :], 0.0)
            nc.gpsimd.memset(eps[:, :], 1e-5)
            nc.gpsimd.memset(tiny[:, :], TINY)
            nc.gpsimd.memset(zeros[:, :], 0.0)
            gp.drain()
            nc.gpsimd.affine_select(out=ident[:, :], in_=ident[:, :], compare_op=ALU.not_equal, fill=1.0,
                                    base=0, pattern=[[-1, 128]], channel_multiplier=1)
            gp.drain().then_inc(consts, 1)
            gp.wait_ge(rows_in, 16 * len(ROWS))
            for t in range(T):
                gp.wait_ge(xn_made, t + 1)
                nc.gpsimd.tensor_tensor(XR[:, t, :], xs[:, t, :], xn[:, t, :], ALU.add)
            gp.drain()
            for t in range(T):
                nc.gpsimd.tensor_tensor(XR[:, t, :], XR[:, t, :], row("mbo"), ALU.add)
            gp.drain().then_inc(xr_made, 1)
            gp.wait_ge(act_read, TURNS.group_read("xnT", 8)[1])
            gp.wait_ge(dve_read, TURNS.group_read("xnT", 9)[1])
            nc.gpsimd.memset(vt[:, :, :, 128:129], 1.0)
            gp.drain().then_inc(consts, 1)
            gp.wait_ge(filled, TURNS.filled("mix_o", 19))
            nc.gpsimd.iota(gi[:, 0, :], pattern=[[1, EC // EG], [0, EG]], base=1, channel_multiplier=0,
                           allow_small_or_imprecise_dtypes=True)
            nc.gpsimd.iota(gi[:, 1, :], pattern=[[-1, EC // EG], [0, EG]], base=EC // EG, channel_multiplier=0,
                           allow_small_or_imprecise_dtypes=True)
            nc.gpsimd.iota(lim[:, 0:1], pattern=[[0, 1]], base=0, channel_multiplier=P,
                           allow_small_or_imprecise_dtypes=True)
            nc.gpsimd.iota(lim[:, 1:2], pattern=[[0, 1]], base=-P, channel_multiplier=-P,
                           allow_small_or_imprecise_dtypes=True)
            nc.gpsimd.iota(iota[:, :], pattern=[[1, N]], base=0, channel_multiplier=0,
                           allow_small_or_imprecise_dtypes=True)
            gp.wait_ge(edges_f, 1)
            nc.gpsimd.partition_all_reduce(cmx[:, 0, :], e_f[:, 1, :], P, bass.bass_isa.ReduceOp.max)
            nc.gpsimd.partition_all_reduce(cmx[:, 1, :], neg[:, :], P, bass.bass_isa.ReduceOp.max)
            gp.drain().then_inc(cmax_made, 1)
            gp.drain().then_inc(consts, 1)
            for i in range(4):
                gp.wait_ge(split_made, i + 1)
                w, m = i // 2, i % 2
                gp.dma_start(qk_d[w, 0, 128 * m:128 * m + 128, :], qk_hi[:, i % 2, :].bitcast(F32)).then_inc(qk_out[i], 16)
                gp.dma_start(qk_d[w, 1, 128 * m:128 * m + 128, :], qk_lo[:, i % 2, :].bitcast(F32)).then_inc(qk_out[i], 16)
            gp.wait_ge(range_made, 1)
            at_range = [(gp.value_load(ranges[b:b + 1, 0:1], min_val=0, max_val=EC // EG - 1),
                         gp.value_load(ranges[b:b + 1, 1:2], min_val=1, max_val=EC // EG)) for b in range(T)]
            for b, (lo_b, n_b) in enumerate(at_range):
                with gp.Fori(0, n_b) as g:
                    grp = in_range(lo_b + g)
                    gp.wait_ge(dA_used[b], g + 1)
                    nc.gpsimd.tensor_tensor(dA[:, :, :], iota[:, b * P:b * P + P].unsqueeze(1).to_broadcast([P, EG, P]),
                                            e_f[:, 1, bass.ds(grp * EG, EG)].unsqueeze(2).to_broadcast([P, EG, P]),
                                            ALU.subtract).then_inc(dA_made[b], 1)
            for i in range(4):
                gp.wait_ge(qk_out[i], 32)
            nc.gpsimd.memset(C[:, :, N:NQ], 0.0)
            nc.gpsimd.memset(Qst[:, :, N:NQ].bitcast(F32), 0.0)
            gp.drain().then_inc(pads_made, 1)
            z_v = z_d.rearrange("(t p) d -> t p d", p=P)
            for t in range(T):
                gp.wait_ge(y_made, t + 1)
                nc.gpsimd.tensor_tensor(XR[:, t, :], XR[:, t, :], yz[:, t, :], ALU.add).then_inc(xy_kept, 1)
            for t in range(T):
                gp.wait_ge(z_made, t + 1)
                gp.dma_start(z_v[t], yz[:, t, :]).then_inc(z_out, 16)
            nc.gpsimd.iota(iotaE_i[:, :], pattern=[[1, E]], base=0, channel_multiplier=0)
            gp.wait_ge(z_out, 16 * T)
            gp.wait_ge(act_read, TURNS.group_read("hT", 8)[1])
            gp.wait_ge(dve_read, TURNS.group_read("hT", 9)[1])
            nc.gpsimd.iota(toki[:, :, :], pattern=[[1, TOPK], [TOPK * P, T]], base=0, channel_multiplier=TOPK)
            nc.gpsimd.memset(nobody[:, :], NOBODY)
            nc.gpsimd.memset(lst[:, :], NOBODY)
            nc.gpsimd.memset(ones[:, :], 1.0)
            gp.drain()
            nc.gpsimd.tensor_copy(iotaE[:, :], iotaE_i[:, :])
            nc.gpsimd.affine_select(out=ltri[:, :], in_=ones[:, :], compare_op=ALU.is_gt, fill=0.0,
                                    base=0, pattern=[[1, P]], channel_multiplier=-1)
            gp.drain().then_inc(consts, 1)
            gp.dma_start(list_d.rearrange("(p n) o -> p (n o)", p=128), nobody[:, :]).then_inc(list_clear, 16)
            gp.wait_ge(xy_kept, T)
            for t in range(T):
                nc.gpsimd.tensor_tensor(XR[:, t, :], XR[:, t, :], row("bf2"), ALU.add).then_inc(xy_kept, 1)
            gp.wait_ge(list_clear, 16)
            gp.wait_ge(pos_made, 1)
            for k in range(TOPK):
                for t in range(T):
                    gp.indirect_dma_start(
                        out=list_d, out_offset=bass.IndirectOffsetOnAxis(ap=posi[:, k, t:t + 1], axis=0),
                        in_=toki[:, k, t:t + 1], in_offset=None).then_inc(list_made, 16)
            gp.wait_ge(list_made, 16 * TOPK * T)
            gp.wait_ge(dve_read, TURNS.group_read("rank", 2)[1])
            nc.gpsimd.memset(Zg[:, :, :], 0.0)
            gp.drain()
            gp.wait_ge(round_made, 1)
            R = gp.value_load(rounds[0:1, 0:1], min_val=1, max_val=RANKS // B)

            def wait_alone(s, value, j=0):
                gp.wait_ge(s, value)
                nc.gpsimd.tensor_tensor(carry[:, j, :], eps[0:1, :], eps[0:1, :], ALU.add)

            def rows_of(u):
                gp.indirect_dma_start(out=Zg[:, u, :], out_offset=None, in_=z_d,
                                      in_offset=bass.IndirectOffsetOnAxis(ap=idxg[:, u, :], axis=0),
                                      bounds_check=N - 1, oob_is_err=False).then_inc(zg_in[u], 16)

            def one_round(r):
                if not isinstance(r, int):
                    gp.drain()
                    for u in range(U):
                        wait_alone(zg_in[u], 16 * (GROUPS + 1) * r)
                    gp.drain()
                gp.dma_start(lst[:, 0:E], list_d.rearrange("(r p e) o -> r p (e o)", p=B, e=E)[bass.ds(r, 1)]
                             .rearrange("r p e -> (r p) e")).then_inc(lst_in, 16)
                wait_alone(gat_made, r + 1)
                for u in range(U):
                    nc.gpsimd.tensor_copy(idxg[:, u, :], gat[:, u:u + 1])
                gp.drain()
                for u in range(U):
                    rows_of(u)

                def gather_next(g, u):
                    n = E * r + U * g + u
                    wait_alone(tr_done, n + 1)
                    nc.gpsimd.tensor_copy(idxg[:, u, :], gat[:, bass.ds(U * g + u + U, 1)]).then_inc(idxg_made, 1)
                    wait_alone(idxg_made, n + 1, 1)
                    rows_of(u)

                def scatter(g, u):
                    n = E * r + U * g + u
                    wait_alone(e_read, n + 1, 2)
                    sent = (GROUPS * r + g) * 16
                    if not isinstance(sent, int) or sent > 0:
                        wait_alone(y_out[u], sent, 3)
                    nc.gpsimd.tensor_copy(idxs[:, u, :], lst[:, bass.ds(U * g + u, 1)]).then_inc(idxs_made, 1)
                    wait_alone(idxs_made, n + 1, 4)
                    gp.indirect_dma_start(out=y_d, out_offset=bass.IndirectOffsetOnAxis(ap=idxs[:, u, :], axis=0),
                                          in_=eo[:, u, :], in_offset=None,
                                          bounds_check=N * TOPK - 1, oob_is_err=False).then_inc(y_out[u], 16)

                def group(g, first):
                    for u in range(U):
                        gather_next(g, u)
                        if u >= 2:
                            scatter(g, u - 2)
                        elif not first:
                            scatter(g - 1, U + u - 2)
                group(0, True)
                group(1, False)
                with gp.Fori(2, GROUPS) as g:
                    group(g, False)
                scatter(GROUPS - 1, U - 2)
                scatter(GROUPS - 1, U - 1)

            one_round(0)
            with gp.If(R > 1):
                with gp.Fori(1, R) as r:
                    one_round(r)
            for u in range(U):
                wait_alone(zg_in[u], R * (16 * (GROUPS + 1)))
                gp.drain()

        @blk.vector
        def _(v):
            V_ = nc.vector

            def reads(name, i):
                v.wait_ge(filled, TURNS.filled(name, i))

            def stats(src, mvt, tiles):
                for t in tiles:
                    V_.bn_stats(st[:, t, :], src[:, t, :])
                v.drain()
                for t in tiles:
                    V_.bn_aggr(mvt[:, t, :], st[:, t, :])
                v.drain().then_inc(ln_var, 1)

            def inverse_std(count):
                v.wait_ge(ln_std, count)
                V_.reciprocal(rs[:, :], rs[:, :])
                v.drain()

            def normalise(dst, src, mvt, t):
                return V_.tensor_scalar(dst, src, mvt[:, t, 0:1], rs[:, t:t + 1], ALU.subtract, ALU.mult)

            v.wait_ge(x_in[0], 16)
            v.wait_ge(x_in[1], 16)
            v.wait_ge(consts, 1)
            stats(xs, mv, range(T))
            inverse_std(1)
            for t in range(T):
                normalise(xn[:, t, :], xs[:, t, :], mv, t).then_inc(xn_made, 1)
            for t in range(1, T, 2):
                reads("xnT", t)
                V_.tensor_copy(xnT[:, :, t * P:t * P + P],
                               bank(TURNS.bank("xnT", t), 4 * P).rearrange("p (k n) -> p k n", k=4)).then_inc(dve_read, 1)
            for m in range(KD):
                for c, (o, n) in enumerate(CHUNKS):
                    i = 3 * m + c
                    v.wait_ge(feat_q, i + 1)
                    V_.scalar_tensor_tensor(qT[:, m, o:o + n], eq[:, i % 2, 0:n], 1.0, rq[:, i % 2, 0:n],
                                            ALU.min, ALU.add).then_inc(qT_made, 1)
            v.wait_ge(rows_in, 16 * len(ROWS))
            v.wait_ge(consts, 2)
            v.drain()
            for t in range(T):
                reads("mix_kv", 2 * t)
                V_.tensor_tensor(tk[:, t % 2, :], bank(TURNS.bank("mix_kv", 2 * t), D, P), row("mbk"), ALU.add).then_inc(dve_read, 1)
                v.drain().then_inc(tk_made, 1)
                if t >= 2:
                    v.wait_ge(kv_used, t - 1)
                V_.tensor_scalar(kf[:, t % 2, :], tk[:, t % 2, :], 0.0, None, ALU.max)
                reads("mix_kv", 2 * t + 1)
                V_.tensor_tensor(vt[:, t % 2, :, 0:128], bank(TURNS.bank("mix_kv", 2 * t + 1), D, P).rearrange("p (k n) -> p k n", k=KD),
                                 row("mbv").rearrange("p (k n) -> p k n", k=KD), ALU.add).then_inc(dve_read, 1)
                v.wait_ge(ek_made, t + 1)
                v.drain()
                V_.scalar_tensor_tensor(kf[:, t % 2, :], ek[:, t % 2, :], 1.0, kf[:, t % 2, :], ALU.min, ALU.add)
                v.drain().then_inc(kf_made, 1)
            v.wait_ge(kv_summed, 1)
            V_.memset(kvb[:, :, :], 0.0)
            v.drain()
            for p in range(KD):
                src = ps[:, (6 + p // 2) * 512 + (p % 2) * 129:(6 + p // 2) * 512 + (p % 2) * 129 + 129]
                for j in range(2):
                    a = 64 * j
                    V_.tensor_copy(kvb[a:a + 64, p, a:a + 64], src[a:a + 64, a:a + 64])
                    V_.tensor_copy(kvb[a:a + 64, p, 128 + j:129 + j], src[a:a + 64, 128:129])
            v.drain().then_inc(kvb_made, 1)
            v.wait_ge(xr_made, 1)
            for t in range(T):
                pairs = []
                for i in range(2):
                    reads("mix_o", 2 * t + i)
                    pairs.append(bank(TURNS.bank("mix_o", 2 * t + i), 260, P).rearrange("p (k n) -> p k n", k=2))
                    V_.tensor_scalar(zt[:, t % 2, 4 * i:4 * i + 4].rearrange("p (k h) -> p k h", k=2), pairs[i][:, :, 128:130],
                                     1e-6, None, ALU.add)
                v.drain()
                V_.reciprocal(zt[:, t % 2, :], zt[:, t % 2, :])
                v.drain()
                for i in range(2):
                    V_.tensor_tensor(mo[:, t, 256 * i:256 * i + 256].rearrange("p (k h d) -> p k h d", k=2, h=2),
                                     pairs[i][:, :, 0:128].rearrange("p k (h d) -> p k h d", h=2),
                                     zt[:, t % 2, 4 * i:4 * i + 4].rearrange("p (k h) -> p k h", k=2).unsqueeze(3).to_broadcast([P, 2, 2, 64]),
                                     ALU.mult).then_inc(dve_read, 1)
            for t in range(T):
                reads("mix_wo", t)
                V_.tensor_tensor(XR[:, t, :], bank(TURNS.bank("mix_wo", t), D, P), XR[:, t, :], ALU.add).then_inc(dve_read, 1)
            v.wait_ge(edges_in, 32)
            V_.tensor_copy(e_f[:, :, :], e_i[:, :, :])
            v.drain()
            V_.tensor_scalar(neg[:, :], e_f[:, 1, :], -1.0, None, ALU.mult)
            v.drain().then_inc(edges_f, 1)
            for i in range(4):
                v.wait_ge(act_read, TURNS.group_read("gnn_qk", 3 * i + 2)[1])
                if i >= 2:
                    v.wait_ge(qk_out[i - 2], 32)
                V_.tensor_copy(qk_hi[:, i % 2, :], fqk[:, i % 2, :])
                v.drain()
                V_.tensor_tensor(qk_lo[:, i % 2, :], fqk[:, i % 2, :], qk_hi[:, i % 2, :].bitcast(F32), ALU.subtract)
                v.drain().then_inc(split_made, 1)
            V_.memset(V[:, :, :, 1, :], 1.0)
            for t in range(T):
                reads("gnn_v", t)
                V_.tensor_tensor(V[:, t, :, 0:3:2, :], bank(TURNS.bank("gnn_v", t), HEADS * DK, P).rearrange("p (h j d) -> p h j d", j=2, d=DK),
                                 row("gbv", HEADS * DK).rearrange("p (h j d) -> p h j d", j=2, d=DK), ALU.add).then_inc(dve_read, 1)
            v.wait_ge(cmax_made, 1)
            v.wait_ge(consts, 3)
            lo, hi = lim[:, 2:3], lim[:, 3:4]
            V_.tensor_scalar(ov[:, 0, :], cmx[0:T, 0, :], lim[:, 0:1], None, ALU.is_ge)
            V_.tensor_scalar(ov[:, 1, :], cmx[0:T, 1, :], lim[:, 1:2], None, ALU.is_gt)
            v.drain()
            V_.tensor_tensor(ov[:, 2, :], ov[:, 0, :], ov[:, 1, :], ALU.mult)
            v.drain()
            V_.tensor_tensor(ov[:, 0, :], ov[:, 2, :], gi[:, 0, :], ALU.mult)
            V_.tensor_tensor(ov[:, 1, :], ov[:, 2, :], gi[:, 1, :], ALU.mult)
            v.drain()
            V_.tensor_reduce(hi, ov[:, 0, :], axis=AX.X, op=ALU.max)
            V_.tensor_reduce(lo, ov[:, 1, :], axis=AX.X, op=ALU.max)
            v.drain()
            V_.tensor_scalar(hi, hi, 1.0, None, ALU.max)
            V_.tensor_scalar(lo, lo, -1.0, float(EC // EG), ALU.mult, ALU.add)
            v.drain()
            V_.tensor_scalar(lim[:, 4:5], hi, -1.0, None, ALU.add)
            v.drain()
            V_.tensor_tensor(lo, lo, lim[:, 4:5], ALU.min)
            v.drain()
            V_.tensor_tensor(hi, hi, lo, ALU.subtract)
            v.drain()
            V_.tensor_copy(ranges[:, :], lim[:, 2:4])
            v.drain().then_inc(range_made, 1)
            at_range = [(v.value_load(ranges[b:b + 1, 0:1], min_val=0, max_val=EC // EG - 1),
                         v.value_load(ranges[b:b + 1, 1:2], min_val=1, max_val=EC // EG)) for b in range(T)]
            for b, (lo_b, n_b) in enumerate(at_range):
                with v.Fori(0, n_b) as g:
                    grp = in_range(lo_b + g)
                    for j in range(EG):
                        v.wait_ge(oh_used[b], g * EG + j + 1)
                        V_.tensor_scalar(ohB[:, j, :], iota[:, :], e_f[:, 0, bass.ds(grp * EG + j, 1)], None, ALU.is_equal)\
                          .then_inc(oh_made[b], 1)
            v.wait_ge(c_kept, T)
            v.wait_ge(pads_made, 1)

            def keep_heads(i, step):
                if step == 0:
                    v.wait_ge(den_kept, i + 1)
                if step < 4:
                    a, o = step // 2, (step % 2) * (PIECE // 2)
                    V_.reciprocal(rden[:, a, o:o + PIECE // 2], rden[:, a, o:o + PIECE // 2])
                    return
                if step == 4:
                    v.drain()
                j = step - 4
                h = 2 * (i // 2) + j
                o = (i % 2) * HALF
                V_.scalar_tensor_tensor(aggT[32 * (h % 4):32 * (h % 4) + 32, h // 4, o:o + HALF].rearrange("p (a n) -> p a n", a=2),
                                        sums_of(i, 96 * j, 32), 0.0, rden[32 * j + 32:32 * j + 64, :, :], ALU.max, ALU.mult)
                if step == 5:
                    v.drain().then_inc(head_kept, 1)

            for n in range(HEADS * 2 * T):
                i, s = divmod(n // 2, T)
                v.wait_ge(s_exp, n + 1)
                if n >= 4:
                    v.wait_ge(att_used, n // 2 - 1)
                o = (i % 2) * HALF
                V_.tensor_tensor(att[:, n % 4, :, :], scores_of(n), C[:, s, o:o + HALF].rearrange("p (a n) -> p a n", a=2), ALU.mult).then_inc(att_made, 1)
                if n % 2 and i >= 1 and 1 <= s <= 6:
                    keep_heads(i - 1, s - 1)
            for step in range(6):
                keep_heads(HEADS - 1, step)
            def spread(src, mvt, t, made):
                V_.bn_stats(st[:, t, :], src)
                v.drain()
                V_.bn_aggr(mvt[:, t, :], st[:, t, :])
                v.drain().then_inc(made, 1)

            def norm_tile(dst, src, mvt, t, std):
                v.wait_ge(std, t + 1)
                V_.reciprocal(rs[:, t:t + 1], rs[:, t:t + 1])
                v.drain()
                return normalise(dst, src, mvt, t)

            for t in range(T + 2):
                if t < T:
                    reads("gnn_f", t)
                    V_.tensor_tensor(tf[:, t % 2, :], bank(TURNS.bank("gnn_f", t), D, P), row("gbf"), ALU.add).then_inc(dve_read, 1)
                    v.drain()
                    V_.scalar_tensor_tensor(XR[:, t, :], tf[:, t % 2, :], 0.0, XR[:, t, :], ALU.max, ALU.add)
                    v.drain()
                    spread(XR[:, t, :], mv, t, y_var)
                if 1 <= t <= T:
                    norm_tile(yz[:, t - 1, :], XR[:, t - 1, :], mv, t - 1, y_std).then_inc(y_made, 1)
                    v.drain()
                    spread(yz[:, t - 1, :], mv2, t - 1, z_var)
                if t >= 2:
                    v.wait_ge(xy_kept, t - 1)
                    norm_tile(yz[:, t - 2, :], yz[:, t - 2, :], mv2, t - 2, z_std).then_inc(z_made, 1)
            for t in range(1, T, 2):
                reads("hT", t)
                for k in range(KD):
                    i = V_.tensor_scalar(hT[:, k, t * P:t * P + P], bank(TURNS.bank("hT", t), P, 128, k * P),
                                         col("g1", k), col("b1ln", k), ALU.mult, ALU.add)
                i.then_inc(dve_read, 1)
            V_.tensor_scalar(row("bs2"), row("bs2"), 0.25, None, ALU.mult)
            for i in range(2):
                reads("logit", i)
                V_.tensor_scalar(prob[:, 5 * i:5 * i + 5, :], bank(TURNS.bank("logit", i), 5 * E, P).rearrange("p (t e) -> p t e", t=5),
                                 1 / 0.7, None, ALU.mult).then_inc(dve_read, 1)
            v.drain()
            V_.tensor_reduce(sm[:, 0, :], prob[:, :, :], axis=AX.X, op=ALU.max)
            v.drain()
            V_.tensor_scalar(sm[:, 0, :], sm[:, 0, :], -1.0, None, ALU.mult)
            v.drain().then_inc(lmax_made, 1)
            v.wait_ge(prob_exp, T)
            V_.reciprocal(sm[:, 1, :], sm[:, 1, :])
            v.drain()
            V_.tensor_tensor(prob[:, :, :], prob[:, :, :], sm[:, 1, :].unsqueeze(2).to_broadcast([P, T, E]), ALU.mult)
            v.drain()
            for t in range(T):
                V_.max(top8[:, t, :], prob[:, t, :])
            v.drain()
            for t in range(T):
                V_.max_index(idx8[:, t, :], top8[:, t, :], prob[:, t, :])
            V_.tensor_tensor(sm[:, 2, :].unsqueeze(2), top8[:, :, 0:1], top8[:, :, 1:2], ALU.add)
            v.drain()
            V_.reciprocal(sm[:, 2, :], sm[:, 2, :])
            V_.tensor_copy(sm[:, 3:5, :].rearrange("p k t -> p t k"), idx8[:, :, 0:TOPK])
            v.drain()
            v.wait_ge(consts, 4)
            V_.tensor_tensor(wtop[:, :, :], top8[:, :, 0:TOPK], sm[:, 2, :].unsqueeze(2).to_broadcast([P, T, TOPK]), ALU.mult)
            for k, M in ((0, M1), (1, M2)):
                V_.tensor_tensor(M[:, :, :], iotaE[:, :].unsqueeze(1).to_broadcast([P, T, E]),
                                 sm[:, 3 + k, :].unsqueeze(2).to_broadcast([P, T, E]), ALU.is_equal)
            v.drain()
            V_.tensor_tensor(Mb[:, :, :], M1[:, :, :], M2[:, :, :], ALU.add)
            v.drain().then_inc(m_made, 1)
            V_.tensor_tensor(prob[:, :, :], M1[:, :, :], wtop[:, :, 0:1].to_broadcast([P, T, E]), ALU.mult)
            V_.tensor_tensor(tmpr[:, :, :], M2[:, :, :], wtop[:, :, 1:2].to_broadcast([P, T, E]), ALU.mult)
            v.drain()
            V_.tensor_tensor(prob[:, :, :], prob[:, :, :], tmpr[:, :, :], ALU.add)
            v.drain()
            V_.tensor_scalar(prob[:, :, :], prob[:, :, :], 4.0, None, ALU.mult)
            v.drain().then_inc(comb_made, 1)
            for i in range(2):
                reads("rank", i)
                V_.tensor_copy(rankS[:, 5 * i:5 * i + 5, :], bank(TURNS.bank("rank", i), 5 * E, P).rearrange("p (t e) -> p t e", t=5)).then_inc(dve_read, 1)
            reads("rank", 2)
            V_.tensor_reduce(sm[0:1, 5, 0:1], bank(TURNS.bank("rank", 2), E, 1), axis=AX.X, op=ALU.max).then_inc(dve_read, 1)
            v.drain()
            for k, M in ((0, M1), (1, M2)):
                V_.tensor_tensor(tmpr[:, :, :], M[:, :, :], rankS[:, :, :], ALU.mult)
                v.drain()
                V_.tensor_reduce(sm[:, 6 + k, :], tmpr[:, :, :], axis=AX.X, op=ALU.add)
                v.drain()
                V_.scalar_tensor_tensor(posf[:, k, :], sm[:, 6 + k, :], float(E), sm[:, 3 + k, :], ALU.mult, ALU.add)
            v.drain()
            V_.tensor_copy(posi[:, :, :], posf[:, :, :])
            v.drain().then_inc(pos_made, 1)
            V_.tensor_scalar(sm[0:1, 5, 1:2], sm[0:1, 5, 0:1], float(B - 1), None, ALU.add)
            v.drain()
            V_.tensor_copy(rounds[:, :], sm[0:1, 5, 1:2])
            v.drain()
            V_.tensor_single_scalar(rounds[:, :], rounds[:, :], B.bit_length() - 1, ALU.logical_shift_right)
            v.drain().then_inc(round_made, 1)
            for c in range(5):
                for k in range(2):
                    t = 2 * c + k
                    reads("shared", t)
                    V_.scalar_tensor_tensor(HM[:, t, :], bank(TURNS.bank("shared", t), D, P), 0.25, row("bs2"), ALU.mult, ALU.add).then_inc(dve_read, 1)
            R = v.value_load(rounds[0:1, 0:1], min_val=1, max_val=RANKS // B)

            def one_round(r):
                v.wait_ge(lst_in, 16 * (r + 1))
                if not isinstance(r, int):
                    v.wait_ge(zg_in[U - 1], 16 * (GROUPS + 1) * r)
                V_.tensor_single_scalar(gat[:, :], lst[:, :], 1, ALU.logical_shift_right)
                v.drain().then_inc(gat_made, 1)

                def group(g, first):
                    for u in range(U):
                        n = E * r + U * g + u
                        v.wait_ge(tr_done, n + 1)
                        at_least(v, h_done, n - 1)
                        for k in range(KD):
                            i = V_.tensor_scalar(hgT[:, u % 2, k, :], bank(u % 2, B, 128, k * B), col("g1", k), col("b1ln", k), ALU.mult, ALU.add)
                        i.then_inc(tr_read, 1)
                group(0, True)
                with v.Fori(1, GROUPS) as g:
                    group(g, False)

            v.wait_ge(cols_in, 16)
            one_round(0)
            with v.If(R > 1):
                with v.Fori(1, R) as r:
                    one_round(r)
            def f_read(t):
                reads("fT", t)
                for k in range(KD):
                    i = V_.tensor_scalar(fT[:, k, t * P:t * P + P], bank(TURNS.bank("fT", t), P, 128, k * P),
                                         col("gf", k), col("bfln", k), ALU.mult, ALU.add)
                i.then_inc(dve_read, 1)

            def output(t):
                reads("f2", t)
                if t >= 2:
                    v.wait_ge(out_sent[t % 2], 16 * (t // 2))
                V_.tensor_tensor(outS[:, t % 2, :], bank(TURNS.bank("f2", t), D, P), XR[:, t, :], ALU.add).then_inc(dve_read, 1)
                v.drain().then_inc(out_made, 1)

            v.wait_ge(xy_kept, 2 * T)
            for t in range(T + 3):
                if t < T:
                    v.wait_ge(yt_in[t % 2], 16 * (t // 2 + 1))
                    V_.scalar_tensor_tensor(HM[:, t, :], Yt[:, t % 2, 0, :], wtop[:, t, 0:1], HM[:, t, :], ALU.mult, ALU.add)
                    v.drain()
                    V_.scalar_tensor_tensor(HM[:, t, :], Yt[:, t % 2, 1, :], wtop[:, t, 1:2], HM[:, t, :], ALU.mult, ALU.add)
                    v.drain().then_inc(yt_used, 1)
                    spread(HM[:, t, :], mv, t, f_var)
                if 1 <= t <= T:
                    if t >= 3:
                        v.wait_ge(filled, TURNS.filled("fT", t - 3))
                    norm_tile(fz[:, (t - 1) % 2, :], HM[:, t - 1, :], mv, t - 1, f_std).then_inc(fz_made, 1)
                    V_.tensor_tensor(XR[:, t - 1, :], XR[:, t - 1, :], HM[:, t - 1, :], ALU.add)
                if t >= 3 and t % 2:
                    f_read(t - 2)
                if t == T:
                    for i in range(4):
                        output(i)
            for i in range(4, T):
                output(i)

        @blk.scalar
        def _(a):
            S_ = nc.scalar

            def reads(name, i):
                a.wait_ge(filled, TURNS.filled(name, i))

            def std(mvt, count):
                a.wait_ge(ln_var, count)
                S_.activation(rs[:, :].unsqueeze(2), mvt[:, :, 1:2], ACT.Sqrt, bias=eps[:, :]).then_inc(ln_std, 1)

            std(mv, 1)
            for t in range(0, T, 2):
                reads("xnT", t)
                S_.copy(xnT[:, :, t * P:t * P + P], bank(TURNS.bank("xnT", t), 4 * P).rearrange("p (k n) -> p k n", k=4)).then_inc(act_read, 1)
            a.wait_ge(cols_in, 16)
            for m in range(KD):
                for c, (o, n) in enumerate(CHUNKS):
                    i = 3 * m + c
                    reads("mix_q", i)
                    if i >= 2:
                        a.wait_ge(qT_made, i - 1)
                    b = bank(TURNS.bank("mix_q", i), n)
                    S_.activation(eq[:, i % 2, 0:n], b, ACT.Exp, bias=col("mbq", m))
                    S_.activation(rq[:, i % 2, 0:n], b, ACT.Relu, bias=col("mbq", m)).then_inc(act_read, 1)
                    a.drain().then_inc(feat_q, 1)
            a.wait_ge(qT_made, 12)
            for t in range(T):
                a.wait_ge(tk_made, t + 1)
                if t >= 2:
                    a.wait_ge(kf_made, t - 1)
                S_.activation(ek[:, t % 2, :], tk[:, t % 2, :], ACT.Exp).then_inc(ek_made, 1)
            for t in range(T):
                reads("moT", t)
                S_.copy(moT[:, :, t * P:t * P + P], bank(TURNS.bank("moT", t), 4 * P).rearrange("p (k n) -> p k n", k=4)).then_inc(act_read, 1)
            for i in range(4):
                for c, (o, n) in enumerate(CHUNKS):
                    reads("gnn_qk", 3 * i + c)
                    if i >= 2 and c == 0:
                        a.wait_ge(split_made, i - 1)
                    S_.activation(fqk[:, i % 2, o:o + n], bank(TURNS.bank("gnn_qk", 3 * i + c), n), ACT.Identity,
                                  bias=col("gbq" if i < 2 else "gbk", i % 2)).then_inc(act_read, 1)
            a.wait_ge(filled, TURNS.filled("gnn_v", 9))
            a.wait_ge(range_made, 1)
            at_range = [a.value_load(ranges[b:b + 1, 1:2], min_val=1, max_val=EC // EG) for b in range(T)]

            def keep_counts(b):
                a.wait_ge(c_sum, b + 1)
                S_.copy(C[:, b, 0:N], ps[0:P, (b % 2) * 1536:(b % 2) * 1536 + N]).then_inc(c_kept, 1)

            for b, n_b in enumerate(at_range):
                if b == 0:
                    a.drain().then_inc(dA_used[0], 1)
                with a.Fori(0, n_b) as g:
                    a.drain()
                    a.wait_ge(dA_made[b], g + 1)
                    S_.activation(sqA[:, :, :], dA[:, :, :], ACT.Square).then_inc(dA_used[b], 1)
                    a.drain()
                    for j in range(EG):
                        a.wait_ge(oh_used[b], g * EG + j + 1)
                        S_.activation(ohA[:, j, :], sqA[:, j, :], ACT.Relu, bias=1.0, scale=-1.0).then_inc(ohA_made[b], 1)
                if b + 1 < T:
                    a.drain().then_inc(dA_used[b + 1], 1)
                if b:
                    keep_counts(b - 1)
            keep_counts(T - 1)
            def keep_den(i):
                a.wait_ge(head_sum, i + 1)
                if i:
                    a.wait_ge(head_kept, i)
                S_.activation(rden[:, :, :], sums_of(i, 0, 128), ACT.Identity, bias=tiny[:, :]).then_inc(den_kept, 1)

            for n in range(HEADS * 2 * T):
                i, s = divmod(n // 2, T)
                a.wait_ge(s_made, n + 1)
                b = scores_of(n)
                S_.activation(b, b, ACT.Exp, scale=float(DK) ** -0.5).then_inc(s_exp, 1)
                if s == 1 and n % 2 == 0 and i >= 1:
                    keep_den(i - 1)
            keep_den(HEADS - 1)
            for m in range(KD):
                for c, (o, n) in enumerate(CHUNKS):
                    i = 3 * m + c
                    reads("gnn_a", i)
                    S_.activation(h1T[:, m, o:o + n], bank(TURNS.bank("gnn_a", i), n), ACT.Relu, bias=col("ba", m)).then_inc(act_read, 1)
            def std_tile(mvt, t, var, done):
                a.wait_ge(var, t + 1)
                S_.activation(rs[:, t:t + 1], mvt[:, t, 1:2], ACT.Sqrt, bias=eps[:, :]).then_inc(done, 1)

            for t in range(T + 1):
                if t < T:
                    std_tile(mv, t, y_var, y_std)
                if t:
                    a.wait_ge(y_made, t)
                    std_tile(mv2, t - 1, z_var, z_std)
            for t in range(0, T, 2):
                reads("hT", t)
                for k in range(KD):
                    i = S_.activation(hT[:, k, t * P:t * P + P], bank(TURNS.bank("hT", t), P, 128, k * P), ACT.Identity,
                                      bias=col("b1ln", k), scale=col("g1", k))
                i.then_inc(act_read, 1)
            for c, (o, n) in enumerate(CHUNKS):
                reads("rT", c)
                S_.copy(rTs[:, o:o + n], bank(TURNS.bank("rT", c), n, E)).then_inc(act_read, 1)
            a.wait_ge(lmax_made, 1)
            for t in range(T):
                S_.activation(prob[:, t, :], prob[:, t, :], ACT.Exp, bias=sm[:, 0, t:t + 1], accum_out=sm[:, 1, t:t + 1]).then_inc(prob_exp, 1)
            def shared_hidden(c):
                for i in range(4):
                    reads("hidden", 4 * c + i)
                    for k in range(2):
                        j = S_.activation(hsT[:, c % 2, 2 * i + k, :], bank(TURNS.bank("hidden", 4 * c + i), 250, 128, 250 * k), ACT.Silu, bias=col("bs1", 2 * i + k))
                    j.then_inc(act_read, 1)

            a.wait_ge(z_out, 16 * T)
            shared_hidden(0)
            shared_hidden(1)
            for c, tiles in enumerate(((0, 4), (4, 4), (8, 2))):
                reads("combT", c)
                S_.copy(combT[:, tiles[0] * P:(tiles[0] + tiles[1]) * P], bank(TURNS.bank("combT", c), tiles[1] * P, E)).then_inc(act_read, 1)
            for c in range(2, 5):
                a.wait_ge(filled, TURNS.filled("shared", 2 * c - 3))
                shared_hidden(c)
            a.wait_ge(round_made, 1)
            R = a.value_load(rounds[0:1, 0:1], min_val=1, max_val=RANKS // B)

            def hidden(r, g, u):
                n = E * r + U * g + u
                a.wait_ge(h_done, n + 1)
                at_least(a, e_done, n - 1)
                for m in range(2):
                    i = S_.activation(ehT[:, u % 2, m, :], bank(2 + u % 2, B, 128, m * B), ACT.Silu,
                                      bias=cols[:, bass.ds(COLS["eb1"][0] + m + 2 * (U * g + u), 1)])
                i.then_inc(h_read, 1)

            def result(r, g, u):
                n = E * r + U * g + u
                a.wait_ge(e_done, n + 1)
                at_least(a, y_out[u], 16 * (GROUPS * r + g))
                S_.copy(eo[:, u, :], bank(4 + u % 2, D)).then_inc(e_read, 1)

            def one_round(r):
                def group(g, first):
                    for u in range(U):
                        hidden(r, g, u)
                        if u:
                            result(r, g, u - 1)
                        elif not first:
                            result(r, g - 1, U - 1)
                group(0, True)
                group(1, False)
                with a.Fori(2, GROUPS) as g:
                    group(g, False)
                result(r, GROUPS - 1, U - 1)

            one_round(0)
            with a.If(R > 1):
                with a.Fori(1, R) as r:
                    one_round(r)
            def f_read(t):
                reads("fT", t)
                for k in range(KD):
                    i = S_.activation(fT[:, k, t * P:t * P + P], bank(TURNS.bank("fT", t), P, 128, k * P), ACT.Identity,
                                      bias=col("bfln", k), scale=col("gf", k))
                i.then_inc(act_read, 1)

            def f1_read(c):
                o, n = CHUNKS[c]
                for m in range(2):
                    i = 2 * c + m
                    reads("f1", i)
                    S_.activation(f1T[:, m, o:o + n], bank(TURNS.bank("f1", i), n), ACT.Silu, bias=col("bf1", m)).then_inc(act_read, 1)

            for t in range(T):
                std_tile(mv, t, f_var, f_std)
                if t >= 2 and t % 2 == 0:
                    f_read(t - 2)
                if t == 5:
                    f1_read(0)
            f1_read(1)
            f_read(8)
            f1_read(2)

        @blk.tensor
        def _(pe):
            MM = nc.tensor.matmul

            def turn(name, i):
                g = TURNS.place[name][i]
                if g >= RING:
                    who, count = TURNS.read(g - RING)
                    pe.wait_ge(act_read if who == "act" else dve_read, count)
                return TURNS.bank(name, i)

            def read_by_now(name, i):
                who, count = TURNS.group_read(name, i)
                pe.wait_ge(act_read if who == "act" else dve_read, count)

            pe.wait_ge(consts, 1)
            for t in range(T):
                pe.wait_ge(xn_made, t + 1)
                b = turn("xnT", t)
                for k in range(KD):
                    i = nc.tensor.transpose(bank(b, P, 128, k * P), xn[:, t, k:D:KD], ident[0:P, 0:P])
                i.then_inc(filled, 1)
            read_by_now("xnT", 8)
            read_by_now("xnT", 9)
            pe.wait_ge(mw_in, 48)
            for m in range(KD):
                for c, (o, n) in enumerate(CHUNKS):
                    b = turn("mix_q", 3 * m + c)
                    for k in range(KD):
                        i = MM(bank(b, n), mW[:, 0, k, m * 128:m * 128 + 128], xnT[:, k, o:o + n], start=k == 0, stop=k == KD - 1)
                    i.then_inc(filled, 1)

            def sum_kv(t):
                pe.wait_ge(kf_made, t + 1)
                read_by_now("mix_kv", 2 * t + 1)
                for p in range(KD):
                    i = MM(bank(6 + p // 2, 129, 128, (p % 2) * 129), kf[:, t % 2, p * 128:p * 128 + 128], vt[:, t % 2, p, :],
                           start=t == 0 and p % 2 == 0, stop=t == T - 1 and p % 2 == 1, skip_group_check=True)
                i.then_inc(kv_used, 1)

            for t in range(T):
                for w in range(2):
                    b = turn("mix_kv", 2 * t + w)
                    for k in range(KD):
                        i = MM(bank(b, D, P), xnT[:, k, t * P:t * P + P], mW[:, 1 + w, k, :], start=k == 0, stop=k == KD - 1)
                    i.then_inc(filled, 1)
                if t:
                    sum_kv(t - 1)
            sum_kv(T - 1)
            pe.drain().then_inc(kv_summed, 1)
            pe.wait_ge(kvb_made, 1)
            pe.wait_ge(qT_made, 12)
            for t in range(T):
                for i in range(2):
                    b = turn("mix_o", 2 * t + i)
                    for j in range(2):
                        k = MM(bank(b, 130, P, 130 * j), qT[:, 2 * i + j, t * P:t * P + P], kvb[:, 2 * i + j, :], start=True, stop=True)
                    k.then_inc(filled, 1)
            for t in range(T):
                read_by_now("mix_o", 2 * t + 1)
                b = turn("moT", t)
                for k in range(KD):
                    i = nc.tensor.transpose(bank(b, P, 128, k * P), mo[:, t, k * 128:k * 128 + 128], ident[0:P, 0:P])
                i.then_inc(filled, 1)
            pe.wait_ge(mwo_in, 16)
            for t in range(T):
                read_by_now("moT", t)
                b = turn("mix_wo", t)
                for k in range(KD):
                    i = MM(bank(b, D, P), moT[:, k, t * P:t * P + P], mWo[:, k, :], start=k == 0, stop=k == KD - 1)
                i.then_inc(filled, 1)
            pe.wait_ge(gw_in, 48)
            for i in range(4):
                for c, (o, n) in enumerate(CHUNKS):
                    b = turn("gnn_qk", 3 * i + c)
                    for k in range(KD):
                        j = MM(bank(b, n), gW[:, i // 2, k, (i % 2) * 128:(i % 2) * 128 + 128], xnT[:, k, o:o + n], start=k == 0, stop=k == KD - 1)
                    j.then_inc(filled, 1)
            for t in range(T):
                b = turn("gnn_v", t)
                for k in range(KD):
                    i = MM(bank(b, HEADS * DK, P), xnT[:, k, t * P:t * P + P], gW[:, 2, k, :], start=k == 0, stop=k == KD - 1)
                i.then_inc(filled, 1)
            for i in range(RING):
                read_by_now("gnn_v", 9 - i)
            pe.wait_ge(range_made, 1)
            at_range = [pe.value_load(ranges[b:b + 1, 1:2], min_val=1, max_val=EC // EG) for b in range(T)]
            for b, n_b in enumerate(at_range):
                if b >= 2:
                    pe.wait_ge(c_kept, b - 1)
                for o, n in BANKED:
                    i = MM(ps[0:P, (b % 2) * 1536 + o:(b % 2) * 1536 + o + n], zeros[0:1, 0:P], zeros[0:1, 0:n],
                           start=True, stop=False, skip_group_check=True)
                i.then_inc(oh_used[b], EG)
                with pe.Fori(0, n_b) as g:
                    for j in range(EG):
                        pe.wait_ge(oh_made[b], g * EG + j + 1)
                        pe.wait_ge(ohA_made[b], g * EG + j + 1)
                        for o, n in BANKED:
                            i = MM(ps[0:P, (b % 2) * 1536 + o:(b % 2) * 1536 + o + n], ohA[:, j, :], ohB[:, j, o:o + n],
                                   start=False, stop=False, skip_group_check=True)
                        i.then_inc(oh_used[b], 1)
                pe.drain().then_inc(c_sum, 1)
            def scores(n):
                i, s = divmod(n // 2, T)
                h = 2 * (i // 2) + n % 2
                if s == 0 and i % 2 == 0:
                    pe.wait_ge(st_in[h % 4], 128 * (h // 4 + 1))
                if n >= 2:
                    pe.wait_ge(att_made, n - 1)
                for a in range(2):
                    o = (i % 2) * HALF + a * PIECE
                    j = MM(scores_of(n)[:, a, :], Kst[:, h % 4, s * P:s * P + P], Qst[:, h % 4, o:o + PIECE], start=True, stop=True)
                j.then_inc(s_made, 1)
                if s == T - 1 and i % 2 and n % 2:
                    pe.drain().then_inc(st_used, 1)

            def sums(m):
                i, s = divmod(m, T)
                pe.wait_ge(att_made, 2 * m + 2)
                if s == 0 and i >= 2:
                    pe.wait_ge(head_kept, i - 1)
                for a in range(2):
                    for j in range(2):
                        h = 2 * (i // 2) + j
                        k = MM(sums_of(i, 64 * j, 64)[:, a, :], V[:, s, h // 2, j:j + 2, :], att[:, (2 * m + j) % 4, a, :],
                               start=s == 0, stop=s == T - 1, skip_group_check=True)
                k.then_inc(att_used, 1)
                if s == T - 1:
                    pe.drain().then_inc(head_sum, 1)

            pe.wait_ge(c_kept, T)
            pe.wait_ge(pads_made, 1)
            scores(0)
            scores(1)
            for m in range(HEADS * T):
                if m + 1 < HEADS * T:
                    scores(2 * m + 2)
                    scores(2 * m + 3)
                sums(m)
            pe.wait_ge(head_kept, HEADS)
            pe.wait_ge(waf_in, 32)
            for m in range(KD):
                for c, (o, n) in enumerate(CHUNKS):
                    b = turn("gnn_a", 3 * m + c)
                    for k in range(2):
                        i = MM(bank(b, n), Wa_s[:, k, m:D:KD], aggT[:, k, o:o + n], start=k == 0, stop=k == 1)
                    i.then_inc(filled, 1)
            read_by_now("gnn_a", 11)
            for t in range(T):
                b = turn("gnn_f", t)
                for k in range(KD):
                    i = MM(bank(b, D, P), h1T[:, k, t * P:t * P + P], Wf_s[:, k, :], start=k == 0, stop=k == KD - 1)
                i.then_inc(filled, 1)
            for t in range(T):
                pe.wait_ge(z_made, t + 1)
                b = turn("hT", t)
                for k in range(KD):
                    i = nc.tensor.transpose(bank(b, P, 128, k * P), yz[:, t, k:D:KD], ident[0:P, 0:P])
                i.then_inc(filled, 1)
            read_by_now("hT", 8)
            read_by_now("hT", 9)
            pe.wait_ge(small_in, 48)
            for c, (o, n) in enumerate(CHUNKS):
                b = turn("rT", c)
                for k in range(KD):
                    i = MM(bank(b, n, E), Wr_s[:, k, :], hT[:, k, o:o + n], start=k == 0, stop=k == KD - 1)
                i.then_inc(filled, 1)
            read_by_now("rT", 2)
            for c in range(2):
                b = turn("logit", c)
                for t in range(5):
                    i = MM(bank(b, E, P, t * E), rTs[:, (5 * c + t) * P:(5 * c + t + 1) * P], cbT_s[:, :], start=True, stop=True)
                i.then_inc(filled, 1)
            pe.wait_ge(ws1_in, 16)
            pe.wait_ge(ws2_in, 16)

            def shared_hidden(c):
                for g in range(4):
                    b = turn("hidden", 4 * c + g)
                    for k2 in range(2):
                        for k in range(KD):
                            i = MM(bank(b, 250, 128, 250 * k2), Ws1_s[:, k, (2 * g + k2) * 128:(2 * g + k2 + 1) * 128],
                                   hT[:, k, c * 250:c * 250 + 250], start=k == 0, stop=k == KD - 1)
                    i.then_inc(filled, 1)

            def shared_rows(c):
                read_by_now("hidden", 4 * c + 3)
                for t in (2 * c, 2 * c + 1):
                    b = turn("shared", t)
                    MM(bank(b, D, P), combT[:, t * P:t * P + P], b2_s[:, :], start=True, stop=False)
                    for k in range(DSH // 128):
                        i = MM(bank(b, D, P), hsT[:, c % 2, k, (t % 2) * P:(t % 2) * P + P], Ws2_s[:, k, :], start=False, stop=k == DSH // 128 - 1)
                    i.then_inc(filled, 1)

            shared_hidden(0)
            shared_hidden(1)
            pe.wait_ge(m_made, 1)
            for c in range(3):
                b = turn("rank", c)
                for t in (range(5 * c, 5 * c + 5) if c < 2 else (T,)):
                    o = (t - 5 * c) * E
                    for q in range(min(t + 1, T)):
                        i = MM(bank(b, E, P, o), (ltri if q == t else ones)[:, :], Mb[:, q, :], start=q == 0, stop=q == min(t, T - 1))
                i.then_inc(filled, 1)
            pe.wait_ge(comb_made, 1)
            for c, (t0, n) in enumerate(((0, 4), (4, 4), (8, 2))):
                b = turn("combT", c)
                for t in range(n):
                    i = nc.tensor.transpose(bank(b, P, E, t * P), prob[:, t0 + t, :], ident[0:P, 0:P])
                i.then_inc(filled, 1)
            read_by_now("combT", 2)
            for c in range(3):
                shared_rows(c)
                shared_hidden(c + 2)
            shared_rows(3)
            shared_rows(4)
            for i in range(RING):
                read_by_now("shared", len(TURNS.place["shared"]) - 1 - i)
            R = pe.value_load(rounds[0:1, 0:1], min_val=1, max_val=RANKS // B)

            def transposes(r, g, u):
                n = E * r + U * g + u
                pe.wait_ge(zg_in[u], 16 * ((GROUPS + 1) * r + g + 1))
                at_least(pe, tr_read, n - 1)
                for k in range(KD):
                    i = nc.tensor.transpose(bank(u % 2, B, 128, k * B), Zg[:, u, k:D:KD], ident[:, :])
                i.then_inc(tr_done, 1)

            def hidden(r, g, u):
                n = E * r + U * g + u
                pe.wait_ge(tr_read, n + 1)
                pe.wait_ge(w_in[u], 32 * (GROUPS * r + g + 1))
                at_least(pe, h_read, n - 1)
                for m in range(2):
                    for k in range(KD):
                        i = MM(bank(2 + u % 2, B, 128, m * B), W1[u][:, k, m:DFF:2], hgT[:, u % 2, k, :], start=k == 0, stop=k == KD - 1)
                i.then_inc(h_done, 1)

            def result(r, g, u):
                n = E * r + U * g + u
                pe.wait_ge(h_read, n + 1)
                at_least(pe, e_read, n - 1)
                for m in range(2):
                    i = MM(bank(4 + u % 2, D), ehT[:, u % 2, m, :], W2[u][:, m, :], start=m == 0, stop=m == 1)
                i.then_inc(e_done, 1)

            def one_round(r):
                def group(g, first):
                    for u in range(U):
                        transposes(r, g, u)
                        if u:
                            hidden(r, g, u - 1)
                            if u > 1:
                                result(r, g, u - 2)
                            elif not first:
                                result(r, g - 1, U - 1)
                        elif not first:
                            hidden(r, g - 1, U - 1)
                            result(r, g - 1, U - 2)
                group(0, True)
                with pe.Fori(1, GROUPS) as g:
                    group(g, False)
                hidden(r, GROUPS - 1, U - 1)
                result(r, GROUPS - 1, U - 2)
                result(r, GROUPS - 1, U - 1)

            one_round(0)
            with pe.If(R > 1):
                with pe.Fori(1, R) as r:
                    one_round(r)
            pe.wait_ge(tr_read, R * E)
            pe.wait_ge(h_read, R * E)
            pe.wait_ge(e_read, R * E)
            def f_transposed(tiles):
                for t in tiles:
                    pe.wait_ge(fz_made, t + 1)
                    b = turn("fT", t)
                    for k in range(KD):
                        i = nc.tensor.transpose(bank(b, P, 128, k * P), fz[:, t % 2, k:D:KD], ident[0:P, 0:P])
                    i.then_inc(filled, 1)

            def f1(c):
                o, n = CHUNKS[c]
                last = (o + n) // P - 1
                read_by_now("fT", last)
                read_by_now("fT", last - 1)
                for m in range(2):
                    b = turn("f1", 2 * c + m)
                    for k in range(KD):
                        i = MM(bank(b, n), Wf1_s[:, k, m:DFF:2], fT[:, k, o:o + n], start=k == 0, stop=k == KD - 1)
                    i.then_inc(filled, 1)

            def f2(tiles):
                for t in tiles:
                    read_by_now("f1", 2 * min(2, t // 4) + 1)
                    b = turn("f2", t)
                    for k in range(2):
                        i = MM(bank(b, D, P), f1T[:, k, t * P:t * P + P], Wf2_s[:, k, :], start=k == 0, stop=k == 1)
                    i.then_inc(filled, 1)

            pe.wait_ge(wf1_in, 16)
            pe.wait_ge(wf2_in, 16)
            f_transposed(range(0, 4))
            f1(0)
            f_transposed(range(4, 8))
            f2(range(0, 4))
            f1(1)
            f_transposed(range(8, T))
            f2(range(4, 8))
            f1(2)
            f2(range(8, T))


def kernel(**inputs):
    import concourse.bacc as bacc
    from concourse.bass_utils import run_bass_kernel_spmd

    g = {k: np.asarray(a) for k, a in inputs.items()}

    def pk(a, k):
        return a.reshape(128, k)

    def kp(a):
        return a.reshape(-1, 128).T

    cols = np.concatenate([
        kp(g["L0_mix_bq"]), kp(g["L0_gnn_bq"]), kp(g["L0_gnn_bk"]), pk(g["L0_gnn_ba"], 4), kp(g["L0_ffn_bs1"]),
        pk(g["L0_ffn_bf1"], 2), pk(g["L0_ffn_ln1_g"], 4), pk(g["L0_ffn_ln1_b"], 4), pk(g["L0_ffn_ffln_g"], 4),
        pk(g["L0_ffn_ffln_b"], 4), g["L0_ffn_b1"].reshape(E, 128, 2).transpose(1, 0, 2).reshape(128, 2 * E)], axis=1)
    gbv = np.zeros(D, np.float32)
    gbv[:HEADS * DK] = g["L0_gnn_bv"]
    rows = np.stack([g["L0_mix_bk"], g["L0_mix_bv"], g["L0_mix_bo"], g["L0_gnn_bf"], g["L0_ffn_bs2"], g["L0_ffn_bf2"], gbv])
    arrays = {
        "x": g["x"], "cols": cols, "rows": rows,
        "src": g["src"].reshape(EC, P).T, "dst": g["dst"].reshape(EC, P).T,
        "mWqT": g["L0_mix_Wq"].T, "mWkT": g["L0_mix_Wk"].T, "mWvT": g["L0_mix_Wv"].T, "mWoT": g["L0_mix_Wo"].T,
        "gWq": g["L0_gnn_Wq"], "gWk": g["L0_gnn_Wk"], "gWv": g["L0_gnn_Wv"], "Wa": g["L0_gnn_Wa"], "Wf": g["L0_gnn_Wf"],
        "Wr": g["L0_ffn_Wr"], "cbT": g["L0_ffn_codebook"].T, "W1": g["L0_ffn_W1"], "W2": g["L0_ffn_W2"],
        "b2": g["L0_ffn_b2"], "Ws1": g["L0_ffn_Ws1"], "Ws2": g["L0_ffn_Ws2"], "Wf1": g["L0_ffn_Wf1"], "Wf2": g["L0_ffn_Wf2"],
    }
    arrays = {f"in_{k}": np.ascontiguousarray(a) for k, a in arrays.items()}
    nc = bacc.Bacc("TRN2", target_bir_lowering=False, num_devices=1)
    A = {k[3:]: nc.dram_tensor(k, a.shape, mybir.dt.from_np(a.dtype), kind="ExternalInput").ap() for k, a in arrays.items()}
    out = nc.dram_tensor("out_dram", (N, D), F32, kind="ExternalOutput").ap()
    block_kernel(nc, A, out)
    r = run_bass_kernel_spmd(nc, [arrays], core_ids=[0])
    return r.results[0]["out_dram"]
```
